# Optimizing a Trainium2 kernel written in Bass

```python
import numpy as np
import jax
import jax.numpy as jnp

def _softmax(x, axis=-1):
    return jax.nn.softmax(x, axis=axis)

def _gelu(x):
    return jax.nn.gelu(x, approximate=True)

def _silu(x):
    return jax.nn.silu(x)

def _sigmoid(x):
    return jax.nn.sigmoid(x)

def _layernorm(x, axis=-1, eps=1e-05):
    m = jnp.mean(x, axis=axis, keepdims=True)
    v = jnp.var(x, axis=axis, keepdims=True)
    return (x - m) / jnp.sqrt(v + eps)

def _scatter_add(tgt, idx, src, axis=0):
    return tgt.at[idx].add(src)

def _segment_sum(src, seg, n):
    return jax.ops.segment_sum(src, seg, n)
kernel_name = 'mk_vit_tower_cls_d1_tok_img768_r4_ede17e'

def setup_inputs(seed: int=0):
    np.random.seed(seed)
    _w = jnp.asarray

    def _rec_inputs():
        import jax
        import jax.numpy as jnp
        _rk = jax.random.key(seed)
        x = -9.30917e-05 + 1.0002 * jax.random.normal(jax.random.fold_in(_rk, 1), (128, 3, 84, 84), jnp.float32)
        cls_tok = 0.02 * jax.random.normal(jax.random.fold_in(_rk, 5), (1, 1, 192), jnp.float32)
        return (x, cls_tok)
    x, cls_tok = _rec_inputs()

    def _L0_tok_setup():
        import jax, jax.numpy as jnp
        import numpy as np
        DN = ('NCHW', 'OIHW', 'NCHW')
        G = 7

        def conv(x, w, stride, pad, groups=1):
            return jax.lax.conv_general_dilated(x, w, (stride, stride), [(pad, pad), (pad, pad)], feature_group_count=groups, dimension_numbers=DN)

        def gelu(x):
            return jax.nn.gelu(x, approximate=False)

        def bn(x, s, b):
            return x * s[None, :, None, None] + b[None, :, None, None]

        def region_layer_dw(x, wdw, sdw, bdw, wpw, spw, bpw):
            B, C, H, W = x.shape
            h, w = (H // G, W // G)
            xr = x.reshape(B, C, G, h, G, w).transpose(0, 2, 4, 1, 3, 5).reshape(B, G * G * C, h, w)
            y = gelu(bn(conv(xr, wdw, 1, 1, groups=G * G * C), sdw, bdw))
            y = bn(conv(y, wpw, 1, 0, groups=G * G), spw, bpw)
            xr = y + xr
            return xr.reshape(B, G, G, C, h, w).transpose(0, 3, 1, 4, 2, 5).reshape(B, C, H, W)
        key = jax.random.key(seed)
        ks = jax.random.split(key, 8)
        B, C0, H, W = (32, 3, 224, 224)
        E = 192
        C1 = E // 16
        C2 = E // 4
        R = G * G
        rn = lambda k, shp, sc: jax.random.normal(k, shp, jnp.float32) * sc
        return {'x': rn(ks[0], (B, C0, H, W), 1.0), 'w0': rn(ks[1], (C1, C0, 3, 3), 0.2), 's0': jnp.ones((C1,), jnp.float32), 'b0': jnp.zeros((C1,), jnp.float32), 'wdw': rn(ks[2], (R * C1, 1, 3, 3), 0.2), 'sdw': jnp.ones((R * C1,), jnp.float32), 'bdw': jnp.zeros((R * C1,), jnp.float32), 'wpw': rn(ks[3], (R * C1, C1, 1, 1), 0.1), 'spw': jnp.ones((R * C1,), jnp.float32), 'bpw': jnp.zeros((R * C1,), jnp.float32), 'w1': rn(ks[4], (C2, C1, 4, 4), 0.05), 's1': jnp.ones((C2,), jnp.float32), 'b1': jnp.zeros((C2,), jnp.float32), 'w2': rn(ks[5], (C2, C2, 2, 2), 0.05), 's2': jnp.ones((C2,), jnp.float32), 'b2': jnp.zeros((C2,), jnp.float32), 'w3': rn(ks[6], (E, C2, 2, 2), 0.05), 's3': jnp.ones((E,), jnp.float32), 'b3': jnp.zeros((E,), jnp.float32)}
    _L0_tok_all = _L0_tok_setup()
    _L0_tok_in = {k: v for k, v in _L0_tok_all.items() if k in ('w0', 's0', 'b0', 'wdw', 'sdw', 'bdw', 'wpw', 'spw', 'bpw', 'w1', 's1', 'b1', 'w2', 's2', 'b2', 'w3', 's3', 'b3')}
    del _L0_tok_all

    def _L0_attn_setup():
        import jax, jax.numpy as jnp
        import numpy as np
        N_HEAD = 12

        def _rotate_half(x):
            x_even = x[..., ::2]
            x_odd = x[..., 1::2]
            return jnp.stack((-x_odd, x_even), axis=-1).reshape(x.shape)

        def _rope_tables(T, D, dtype):
            inv_freq = 1.0 / 10000.0 ** (jnp.arange(0, D, 2, dtype=jnp.float32) / D)
            freqs = jnp.arange(T, dtype=jnp.float32)[:, None] * inv_freq[None, :]
            cos = jnp.repeat(jnp.cos(freqs), 2, axis=-1).astype(dtype)
            sin = jnp.repeat(jnp.sin(freqs), 2, axis=-1).astype(dtype)
            return (cos, sin)
        key = jax.random.key(seed)
        ks = jax.random.split(key, 5)
        B, T, C = (8, 256, 192)
        return {'x': jax.random.normal(ks[0], (B, T, C), dtype=jnp.float32), 'W_attn': jax.random.normal(ks[1], (C, 3 * C), dtype=jnp.float32) * C ** (-0.5), 'b_attn': jax.random.normal(ks[2], (3 * C,), dtype=jnp.float32) * 0.02, 'W_proj': jax.random.normal(ks[3], (C, C), dtype=jnp.float32) * C ** (-0.5), 'b_proj': jax.random.normal(ks[4], (C,), dtype=jnp.float32) * 0.02}
    _L0_attn_all = _L0_attn_setup()
    _L0_attn_in = {k: v for k, v in _L0_attn_all.items() if k in ('W_attn', 'b_attn', 'W_proj', 'b_proj')}
    del _L0_attn_all

    def _L0_ffn_setup():
        import jax, jax.numpy as jnp
        import numpy as np
        B, N, D, H, E, HID, TOPK = (8, 197, 192, 12, 8, 768, 2)

        def _layernorm(x, w, b, eps=1e-05):
            mu = jnp.mean(x, axis=-1, keepdims=True)
            var = jnp.mean((x - mu) ** 2, axis=-1, keepdims=True)
            return (x - mu) * jax.lax.rsqrt(var + eps) * w + b
        key = jax.random.key(seed)
        ks = jax.random.split(key, 8)
        s = 0.02
        return {'x': jax.random.normal(ks[0], (B, N, D), jnp.float32), 'norm1_w': jnp.ones((D,), jnp.float32), 'norm1_b': jnp.zeros((D,), jnp.float32), 'qkv_w': jax.random.normal(ks[1], (3 * D, D), jnp.float32) * s, 'qkv_b': jnp.zeros((3 * D,), jnp.float32), 'proj_w': jax.random.normal(ks[2], (D, D), jnp.float32) * s, 'proj_b': jnp.zeros((D,), jnp.float32), 'norm2_w': jnp.ones((D,), jnp.float32), 'norm2_b': jnp.zeros((D,), jnp.float32), 'w_gate': jax.random.normal(ks[3], (D, E), jnp.float32) * s, 'W1': jax.random.normal(ks[4], (E, D, HID), jnp.float32) * s, 'b1': jnp.zeros((E, HID), jnp.float32), 'W2': jax.random.normal(ks[5], (E, HID, D), jnp.float32) * s, 'b2': jnp.zeros((E, D), jnp.float32)}
    _L0_ffn_all = _L0_ffn_setup()
    _L0_ffn_in = {k: v for k, v in _L0_ffn_all.items() if k in ('norm1_w', 'norm1_b', 'qkv_w', 'qkv_b', 'proj_w', 'proj_b', 'norm2_w', 'norm2_b', 'w_gate', 'W1', 'b1', 'W2', 'b2')}
    del _L0_ffn_all
    return {'x': x, 'cls_tok': cls_tok, 'L0_tok_w0': _L0_tok_in['w0'], 'L0_tok_s0': _L0_tok_in['s0'], 'L0_tok_b0': _L0_tok_in['b0'], 'L0_tok_wdw': _L0_tok_in['wdw'], 'L0_tok_sdw': _L0_tok_in['sdw'], 'L0_tok_bdw': _L0_tok_in['bdw'], 'L0_tok_wpw': _L0_tok_in['wpw'], 'L0_tok_spw': _L0_tok_in['spw'], 'L0_tok_bpw': _L0_tok_in['bpw'], 'L0_tok_w1': _L0_tok_in['w1'], 'L0_tok_s1': _L0_tok_in['s1'], 'L0_tok_b1': _L0_tok_in['b1'], 'L0_tok_w2': _L0_tok_in['w2'], 'L0_tok_s2': _L0_tok_in['s2'], 'L0_tok_b2': _L0_tok_in['b2'], 'L0_tok_w3': _L0_tok_in['w3'], 'L0_tok_s3': _L0_tok_in['s3'], 'L0_tok_b3': _L0_tok_in['b3'], 'L0_attn_W_attn': _L0_attn_in['W_attn'], 'L0_attn_b_attn': _L0_attn_in['b_attn'], 'L0_attn_W_proj': _L0_attn_in['W_proj'], 'L0_attn_b_proj': _L0_attn_in['b_proj'], 'L0_ffn_norm1_w': _L0_ffn_in['norm1_w'], 'L0_ffn_norm1_b': _L0_ffn_in['norm1_b'], 'L0_ffn_qkv_w': _L0_ffn_in['qkv_w'], 'L0_ffn_qkv_b': _L0_ffn_in['qkv_b'], 'L0_ffn_proj_w': _L0_ffn_in['proj_w'], 'L0_ffn_proj_b': _L0_ffn_in['proj_b'], 'L0_ffn_norm2_w': _L0_ffn_in['norm2_w'], 'L0_ffn_norm2_b': _L0_ffn_in['norm2_b'], 'L0_ffn_w_gate': _L0_ffn_in['w_gate'], 'L0_ffn_W1': _L0_ffn_in['W1'], 'L0_ffn_b1': _L0_ffn_in['b1'], 'L0_ffn_W2': _L0_ffn_in['W2'], 'L0_ffn_b2': _L0_ffn_in['b2']}

def reference(x, cls_tok, L0_tok_w0, L0_tok_s0, L0_tok_b0, L0_tok_wdw, L0_tok_sdw, L0_tok_bdw, L0_tok_wpw, L0_tok_spw, L0_tok_bpw, L0_tok_w1, L0_tok_s1, L0_tok_b1, L0_tok_w2, L0_tok_s2, L0_tok_b2, L0_tok_w3, L0_tok_s3, L0_tok_b3, L0_attn_W_attn, L0_attn_b_attn, L0_attn_W_proj, L0_attn_b_proj, L0_ffn_norm1_w, L0_ffn_norm1_b, L0_ffn_qkv_w, L0_ffn_qkv_b, L0_ffn_proj_w, L0_ffn_proj_b, L0_ffn_norm2_w, L0_ffn_norm2_b, L0_ffn_w_gate, L0_ffn_W1, L0_ffn_b1, L0_ffn_W2, L0_ffn_b2):
    import jax
    import jax.numpy as jnp

    def _L0_tok_ref(x, w0, s0, b0, wdw, sdw, bdw, wpw, spw, bpw, w1, s1, b1, w2, s2, b2, w3, s3, b3):
        import jax, jax.numpy as jnp
        import numpy as np
        DN = ('NCHW', 'OIHW', 'NCHW')
        G = 7

        def conv(x, w, stride, pad, groups=1):
            return jax.lax.conv_general_dilated(x, w, (stride, stride), [(pad, pad), (pad, pad)], feature_group_count=groups, dimension_numbers=DN)

        def gelu(x):
            return jax.nn.gelu(x, approximate=False)

        def bn(x, s, b):
            return x * s[None, :, None, None] + b[None, :, None, None]

        def region_layer_dw(x, wdw, sdw, bdw, wpw, spw, bpw):
            B, C, H, W = x.shape
            h, w = (H // G, W // G)
            xr = x.reshape(B, C, G, h, G, w).transpose(0, 2, 4, 1, 3, 5).reshape(B, G * G * C, h, w)
            y = gelu(bn(conv(xr, wdw, 1, 1, groups=G * G * C), sdw, bdw))
            y = bn(conv(y, wpw, 1, 0, groups=G * G), spw, bpw)
            xr = y + xr
            return xr.reshape(B, G, G, C, h, w).transpose(0, 3, 1, 4, 2, 5).reshape(B, C, H, W)
        x = gelu(bn(conv(x, w0, 1, 1), s0, b0))
        x = region_layer_dw(x, wdw, sdw, bdw, wpw, spw, bpw)
        x = gelu(x)
        x = gelu(bn(conv(x, w1, 4, 0), s1, b1))
        x = gelu(bn(conv(x, w2, 2, 0), s2, b2))
        x = bn(conv(x, w3, 2, 0), s3, b3)
        B, E, Hp, Wp = x.shape
        return x.reshape(B, E, Hp * Wp).transpose(0, 2, 1)

    def _L0_attn_ref(x, W_attn, b_attn, W_proj, b_proj):
        import jax, jax.numpy as jnp
        import numpy as np
        N_HEAD = 12

        def _rotate_half(x):
            x_even = x[..., ::2]
            x_odd = x[..., 1::2]
            return jnp.stack((-x_odd, x_even), axis=-1).reshape(x.shape)

        def _rope_tables(T, D, dtype):
            inv_freq = 1.0 / 10000.0 ** (jnp.arange(0, D, 2, dtype=jnp.float32) / D)
            freqs = jnp.arange(T, dtype=jnp.float32)[:, None] * inv_freq[None, :]
            cos = jnp.repeat(jnp.cos(freqs), 2, axis=-1).astype(dtype)
            sin = jnp.repeat(jnp.sin(freqs), 2, axis=-1).astype(dtype)
            return (cos, sin)
        B, T, C = x.shape
        H = N_HEAD
        D = C // H
        qkv = x @ W_attn + b_attn
        q, k, v = jnp.split(qkv, 3, axis=-1)
        q = q.reshape(B, T, H, D).transpose(0, 2, 1, 3)
        k = k.reshape(B, T, H, D).transpose(0, 2, 1, 3)
        v = v.reshape(B, T, H, D).transpose(0, 2, 1, 3)
        cos, sin = _rope_tables(T, D, x.dtype)
        q = q * cos + _rotate_half(q) * sin
        k = k * cos + _rotate_half(k) * sin
        att = jnp.einsum('bhqd,bhkd->bhqk', q, k) * D ** (-0.5)
        causal = jnp.tril(jnp.ones((T, T), dtype=bool))
        att = jnp.where(causal, att, -jnp.inf)
        att = jax.nn.softmax(att, axis=-1)
        y = jnp.einsum('bhqk,bhkd->bhqd', att, v)
        y = y.transpose(0, 2, 1, 3).reshape(B, T, C)
        return y @ W_proj + b_proj

    def _L0_ffn_ref(x, norm1_w, norm1_b, qkv_w, qkv_b, proj_w, proj_b, norm2_w, norm2_b, w_gate, W1, b1, W2, b2):
        import jax, jax.numpy as jnp
        import numpy as np
        B, N, D, H, E, HID, TOPK = (8, 197, 192, 12, 8, 768, 2)

        def _layernorm(x, w, b, eps=1e-05):
            mu = jnp.mean(x, axis=-1, keepdims=True)
            var = jnp.mean((x - mu) ** 2, axis=-1, keepdims=True)
            return (x - mu) * jax.lax.rsqrt(var + eps) * w + b
        Bx, Nx, C = x.shape
        hd = C // H
        scale = hd ** (-0.5)
        xn = _layernorm(x, norm1_w, norm1_b)
        qkv = (xn @ qkv_w.T + qkv_b).reshape(Bx, Nx, 3, H, hd).transpose(2, 0, 3, 1, 4)
        q, k, v = (qkv[0], qkv[1], qkv[2])
        attn = jax.nn.softmax(jnp.einsum('bhqd,bhkd->bhqk', q, k) * scale, axis=-1)
        o = jnp.einsum('bhqk,bhkd->bqhd', attn, v).reshape(Bx, Nx, C)
        x = x + (o @ proj_w.T + proj_b)
        xn2 = _layernorm(x, norm2_w, norm2_b).reshape(-1, C)
        T = xn2.shape[0]
        logits = xn2 @ w_gate
        top_vals, top_idx = jax.lax.top_k(logits, TOPK)
        gates = jax.nn.softmax(top_vals, axis=-1)
        gates_full = jnp.zeros((T, E), xn2.dtype).at[jnp.arange(T)[:, None], top_idx].add(gates)

        def body(acc, p):
            w1, bb1, w2, bb2, g = p
            h = jax.nn.gelu(xn2 @ w1 + bb1, approximate=False)
            return (acc + g[:, None] * (h @ w2 + bb2), None)
        moe_out, _ = jax.lax.scan(body, jnp.zeros_like(xn2), (W1, b1, W2, b2, gates_full.T))
        return x + moe_out.reshape(Bx, Nx, C)
    h = _L0_tok_ref(x, L0_tok_w0, L0_tok_s0, L0_tok_b0, L0_tok_wdw, L0_tok_sdw, L0_tok_bdw, L0_tok_wpw, L0_tok_spw, L0_tok_bpw, L0_tok_w1, L0_tok_s1, L0_tok_b1, L0_tok_w2, L0_tok_s2, L0_tok_b2, L0_tok_w3, L0_tok_s3, L0_tok_b3)
    h = jnp.concatenate([jnp.broadcast_to(cls_tok, (h.shape[0], 1, h.shape[2])), h], axis=1)
    h = h + _L0_attn_ref(_layernorm(h, axis=-1), L0_attn_W_attn, L0_attn_b_attn, L0_attn_W_proj, L0_attn_b_proj)
    h = h + _L0_ffn_ref(_layernorm(h, axis=-1), L0_ffn_norm1_w, L0_ffn_norm1_b, L0_ffn_qkv_w, L0_ffn_qkv_b, L0_ffn_proj_w, L0_ffn_proj_b, L0_ffn_norm2_w, L0_ffn_norm2_b, L0_ffn_w_gate, L0_ffn_W1, L0_ffn_b1, L0_ffn_W2, L0_ffn_b2)
    return h

_drawn_inputs = setup_inputs


def setup_inputs(seed=0):
    import zlib

    import numpy as np

    out = dict(_drawn_inputs(seed))
    spreads = {'L0_tok_s0': (1.0, 0.2),
     'L0_tok_b0': (0.0, 0.1),
     'L0_tok_sdw': (1.0, 0.6),
     'L0_tok_bdw': (0.0, 0.775),
     'L0_tok_spw': (1.0, 0.6),
     'L0_tok_bpw': (0.0, 0.1),
     'L0_tok_s1': (1.0, 0.2),
     'L0_tok_b1': (0.0, 0.1),
     'L0_tok_s2': (1.0, 0.2),
     'L0_tok_b2': (0.0, 0.1),
     'L0_tok_s3': (1.0, 0.2),
     'L0_tok_b3': (0.0, 0.1),
     'L0_ffn_norm1_w': (1.0, 0.6),
     'L0_ffn_norm1_b': (0.0, 0.8),
     'L0_ffn_qkv_b': (0.0, 0.398),
     'L0_ffn_proj_b': (0.0, 0.1),
     'L0_ffn_norm2_w': (1.0, 0.2),
     'L0_ffn_norm2_b': (0.0, 0.342),
     'L0_ffn_b1': (0.0, 0.673),
     'L0_ffn_b2': (0.0, 0.1)}
    factors = {}
    for name, (base, spread) in spreads.items():
        noise = np.random.default_rng([zlib.crc32(name.encode()), seed]).standard_normal(out[name].shape)
        drawn = base * np.exp(spread * noise) if base else spread * noise
        out[name] = jnp.asarray(drawn.astype(out[name].dtype))
    for name, factor in factors.items():
        out[name] = (out[name] * factor).astype(out[name].dtype)
    return out
```

```python
from contextlib import ExitStack

import concourse.bass as bass
from concourse import mybir

F32 = mybir.dt.float32
U32 = mybir.dt.uint32
ACT = mybir.ActivationFunctionType
ALU = mybir.AluOpType
AX_X = mybir.AxisListType.X

NIMG, CIN, HW = 128, 3, 84
G7, RH = 7, 12
NREG = G7 * G7
C1, C2, E = 12, 48, 192
RG = 10
NGRP = 5
BI = 16
NBLK = NIMG // BI
SBI = 2 * BI
NSB = NIMG // SBI
SPS = 2 * NGRP
LANES = RG * C1
WIN = RH + 2
LINE = BI * WIN
GRPR = [RG] * (NGRP - 1) + [NREG - RG * (NGRP - 1)]
CH = 2 * BI * RH
NTOK = 26
HEADS, HD = 12, 16
NEXP, HID = 8, 768
HC = HID // 128
EPS = 1e-5
CONSTS = ["k_ident", "k_regmask", "k_headmask", "k_vmask", "k_causal", "k_cos", "k_sin", "k_iota"]


def bc(ap, dim, n):
    a = ap.unsqueeze(dim)
    shape = list(a.shape)
    shape[dim] = n
    return a.broadcast_to(shape)


def conv_chunks():
    seq = []
    for k in range(SPS):
        if k % NGRP == 1 and k > 1:
            seq += [("conv2", 0, 0), ("conv2", 0, 1)]
        if k:
            seq += [("conv1", k - 1, c) for c in range(0, GRPR[(k - 1) % NGRP], 3)]
    seq += [("conv1", SPS - 1, c) for c in range(0, GRPR[(SPS - 1) % NGRP], 3)]
    seq += [("conv2", 1, 0), ("conv2", 1, 1)]
    return seq


def vit_tower(nc, A, out):
    seq = conv_chunks()
    NCH = len(seq)
    assert NCH % 2 == 0
    place = {c: q for q, c in enumerate(seq)}
    pcount = [0]
    for k in range(SPS):
        pcount.append(pcount[-1] + 16 * 2 * GRPR[k % NGRP])

    with ExitStack() as ctx:
        def sb(name, shape, dt=F32, to=ctx):
            return to.enter_context(nc.sbuf_tensor(name, shape, dt))

        def sem(name):
            return ctx.enter_context(nc.semaphore(name))

        ident = sb("ident", [128, 128])
        regmask = sb("regmask", [LANES, 2 * RG])
        headmask = sb("headmask", [96, 6])
        vmask = sb("vmask", [104, E])
        causal = sb("causal", [128, NTOK])
        cos = sb("cos", [96, NTOK])
        sin = sb("sin", [96, NTOK])
        iota8 = sb("iota8", [128, NEXP])
        w0rep = sb("w0rep", [90, 3, C1])
        w0 = sb("w0", [90, 3, LANES])
        sb0 = sb("sb0", [LANES, 2])
        wdw = sb("wdw", [LANES, NGRP, 9])
        sbdw = sb("sbdw", [LANES, 2, NGRP])
        pwrep = sb("pwrep", [LANES, NGRP, C1])
        spwrep = sb("spwrep", [LANES, NGRP, C1])
        bpw = sb("bpw", [LANES, NGRP])
        wpw = sb("wpw", [LANES, NGRP, LANES])
        w1 = sb("w1", [96, 2, 64])
        sb1 = sb("sb1", [64, 2])
        w2 = sb("w2", [128, 2, 64])
        sb2 = sb("sb2", [128, 2])
        w3 = sb("w3", [128, 2, E])
        s3row = sb("s3row", [128, E])
        b3row = sb("b3row", [128, E])
        wa = [sb(f"wa{a}", [97, 2, 3 * E]) for a in range(2)]
        wrot = sb("wrot", [97, 2, 2 * E])
        wp0 = [sb(f"wp0_{a}", [128, E]) for a in range(2)]
        wp1 = [sb(f"wp1_{a}", [65, E]) for a in range(2)]
        lnwb = sb("lnwb", [96, 4, 2])
        wg = sb("wg", [96, 2, NEXP])
        b2 = sb("b2", [NEXP, E])
        b1t = sb("b1t", [128, NEXP * HC])

        conv = ExitStack()
        h2 = sb("h2", [128, 50, NIMG], to=conv)
        xin = [sb(f"xin{u}", [90, RH, BI, WIN], to=conv) for u in range(2)]
        g0 = [sb(f"g0_{u}", [LANES, WIN, BI, WIN], to=conv) for u in range(2)]
        acc = [sb(f"acc{u}", [LANES, RH, BI * RH], to=conv) for u in range(2)]
        g3 = sb("g3", [LANES, 16, 9 * BI], to=conv)
        patches = sb("patches", [96, 2, RG, 9 * BI], to=conv)
        h1 = sb("h1", [128, 21 * 21 * BI], to=conv)
        conv.close()

        ot0 = sb("ot0", [128, NTOK, NIMG])
        ot1 = sb("ot1", [65, NTOK, NIMG])
        H = sb("H", [128, NTOK, E])
        X = sb("X", [128, NTOK, E])
        N = sb("N", [128, NTOK, E])
        NT = sb("NT", [97, 2, NTOK, NIMG])
        stats = sb("stats", [128, NTOK, 6])
        mv = sb("mv", [128, NTOK, 2])
        rstd = sb("rstd", [128, NTOK])
        att = ExitStack()
        xg = [sb(f"xg{u}", [97, 2, BI, 4 * NTOK], to=att) for u in range(2)]
        qkT = [sb(f"qkT{u}", [96, 4, BI, NTOK], to=att) for u in range(2)]
        rope = [sb(f"rope{u}", [96, 2, BI, NTOK], to=att) for u in range(2)]
        kbd = [sb(f"kbd{u}", [96, 2, 4, 6 * NTOK], to=att) for u in range(2)]
        P = [sb(f"P{u}", [128, HEADS, NTOK], to=att) for u in range(2)]
        PT = [sb(f"PT{u}", [104, 3, 128], to=att) for u in range(2)]
        vbd = [sb(f"vbd{u}", [104, 4, E], to=att) for u in range(2)]
        smax = sb("smax", [128, HEADS], to=att)
        ssum = sb("ssum", [128, HEADS], to=att)
        srec = sb("srec", [128, HEADS], to=att)
        att.close()
        ew1 = [sb(f"ew1_{u}", [96, 2, HID]) for u in range(2)]
        ew2 = [sb(f"ew2_{u}", [128, HC, E]) for u in range(2)]
        b1e = [sb(f"b1e{u}", [128, HC]) for u in range(2)]
        hT = [sb(f"hT{u}", [128, HC, 512]) for u in range(2)]
        logits = sb("logits", [128, NTOK, NEXP])
        top = sb("top", [128, NTOK, 8])
        topi = sb("topi", [128, NTOK, 8], U32)
        topf = sb("topf", [128, NTOK, 2])
        gg = sb("gg", [128, 4, NTOK])
        oneh = sb("oneh", [128, NTOK, NEXP])
        gates = sb("gates", [128, NTOK, NEXP])
        gT = sb("gT", [NEXP, NTOK, 128])

        ps = ctx.enter_context(nc.psum_tensor("ps", [128, 8, 512], F32))

        w_loaded = sem("w_loaded")
        cleared = sem("cleared")
        w_built = sem("w_built")
        xin_loaded = [sem(f"xin_loaded{u}") for u in range(2)]
        conv0_done = sem("conv0_done")
        gelu0_done = sem("gelu0_done")
        dw_done = sem("dw_done")
        dwtap = sem("dwtap")
        gelud_done = sem("gelud_done")
        pw_done = sem("pw_done")
        gelu3_done = sem("gelu3_done")
        p_loaded = sem("p_loaded")
        c12_done = sem("c12_done")
        c12_out = sem("c12_out")
        conv1_steps = sem("conv1_steps")
        h1_done = sem("h1_done")
        h1_shifted = sem("h1_shifted")
        conv2_blocks = sem("conv2_blocks")

        block = ctx.enter_context(nc.Block())

        loads = []

        def load(dst, src):
            loads.append((dst, src))

        for dst, name in ((ident, "k_ident"), (regmask, "k_regmask"), (headmask, "k_headmask"), (vmask, "k_vmask"),
                          (causal, "k_causal"), (cos, "k_cos"), (sin, "k_sin"), (iota8, "k_iota"),
                          (w0rep, "w0"), (sb0, "sb0"), (wdw, "wdw"), (sbdw, "sbdw"), (pwrep, "wpw"), (spwrep, "spw"),
                          (bpw, "bpw"), (w1, "w1"), (sb1, "sb1"), (w2, "w2"), (sb2, "sb2"), (w3, "w3"),
                          (wa[0], "wa0"), (wa[1], "wa1"), (lnwb, "lnwb"), (wg, "wg"), (b2, "L0_ffn_b2"), (b1t, "b1")):
            load(dst[:], A[name])
        for a in range(2):
            load(wp0[a][:], A[f"wp{a}"][0:128])
            load(wp1[a][:], A[f"wp{a}"][128:193])
        load(s3row[:], A["L0_tok_s3"].unsqueeze(0).broadcast_to([128, E]))
        load(b3row[:], A["L0_tok_b3"].unsqueeze(0).broadcast_to([128, E]))
        ALL_LOADED = 16 * len(loads)

        conv3_mm = sem("conv3_mm")
        h_ready = sem("h_ready")
        cls_loaded = sem("cls_loaded")
        chain = sem("chain")
        var_ready = sem("var_ready")
        std_ready = sem("std_ready")
        ln_done = sem("ln_done")
        tr_mm = sem("tr_mm")
        tr_out = sem("tr_out")
        ones_set = sem("ones_set")
        xg_ready = sem("xg_ready")
        qk_mm = sem("qk_mm")
        qk_out = sem("qk_out")
        rope_mul = sem("rope_mul")
        qk_ready = sem("qk_ready")
        kbd_ready = sem("kbd_ready")
        s_mm = sem("s_mm")
        s_out = sem("s_out")
        s_shift = sem("s_shift")
        sm = sem("softmax_stat")
        s_exp = sem("s_exp")
        p_ready = sem("p_ready")
        pt_mm = sem("pt_mm")
        pt_out = sem("pt_out")
        v_mm = sem("v_mm")
        v_out = sem("v_out")
        o_mm = sem("o_mm")
        o_out = sem("o_out")
        proj_mm = sem("proj_mm")
        proj_out = sem("proj_out")
        ps_cleared = sem("ps_cleared")
        lg_mm = sem("lg_mm")
        e_ready = sem("e_ready")
        e_exp = sem("e_exp")
        gates_ready = sem("gates_ready")
        gt_mm = sem("gt_mm")
        gt_out = sem("gt_out")
        b2_mm = sem("b2_mm")
        b2_out = sem("b2_out")
        ew_loaded = [sem(f"ew_loaded{u}") for u in range(2)]
        b1_here = sem("b1_here")
        up_mm = sem("up_mm")
        up_out = sem("up_out")
        down_mm = sem("down_mm")
        down_out = sem("down_out")
        exp_done = sem("exp_done")
        stored = sem("stored")

        pairs = [(s, min(2, NTOK - s)) for s in range(0, NTOK, 2)]
        quads = [(h, s, min(4, NTOK - s)) for h in range(2) for s in range(0, NTOK, 4)]
        NQ = len(quads)
        ebl = [(s, min(4, NTOK - s)) for s in range(0, NTOK, 4)]
        NITS = NIMG // BI

        @block.sync
        def _(sp):
            sp.sem_inc(p_loaded, 1)
            for dst, src in loads:
                sp.dma_start(dst, src).then_inc(w_loaded, 16)

            def load_xin(i, k):
                g, b, u = k % NGRP, (k // NGRP) % 2, k % 2
                for dy in range(3):
                    sp.dma_start(xin[u][30 * dy:30 * dy + 3 * GRPR[g]].rearrange("p y i x -> p (y i x)"),
                                 A["windows"][bass.ds(2 * i + b, 1), 3 * RG * g:3 * (RG * g + GRPR[g]),
                                              dy * LINE:(dy + RH) * LINE].rearrange("b r w -> (b r) w")
                                 ).then_inc(xin_loaded[u], 16)

            def shift_h1(i, b):
                sp.wait_ge(h1_done, 2 * i + b + 1)
                sp.dma_start(h1[64:128, 0:(21 * 21 - 1) * BI], h1[0:64, BI:21 * 21 * BI]
                             ).then_inc(h1_shifted, 16)

            def superblock(i, last):
                for k in range(SPS):
                    if k == NGRP:
                        shift_h1(i, 0)
                    if not (last and k >= SPS - 2):
                        sp.wait_ge(conv0_done, 3 * (SPS * i + k + 1))
                        if k < SPS - 2:
                            load_xin(i, k + 2)
                        else:
                            load_xin(i + 1, k + 2 - SPS)
                    sp.wait_ge(gelu3_done, 3 * (SPS * i + k + 1) + 6)
                    sp.wait_ge(conv1_steps, SPS * i + k + 1)
                    for r in range(GRPR[k % NGRP]):
                        for h in range(2):
                            sp.dma_start(patches[:, h, r, :], g3[r * C1 + 6 * h:r * C1 + 6 * h + 6, :, :]
                                         ).then_inc(p_loaded, 16)
                shift_h1(i, 1)

            sp.wait_ge(cleared, 1)
            load_xin(0, 0)
            load_xin(0, 1)
            with sp.Fori(0, NSB - 1) as i:
                superblock(i, False)
            superblock(NSB - 1, True)

            sp.wait_ge(conv3_mm, 1)
            sp.dma_start(H[:, 0, :], A["cls_tok"].rearrange("a b d -> (a b) d").broadcast_to([128, E])
                         ).then_inc(cls_loaded, 16)

            sp.wait_ge(proj_out, 2 * len(pairs))
            with sp.Fori(0, NEXP // 2) as i:
                for u in range(2):
                    sp.wait_ge(exp_done, 2 * i + u + 1)
                    sp.dma_start(ew1[u][:].rearrange("p h n -> p (h n)"), A["W1"][bass.ds(2 * i + u, 1)].rearrange("e p n -> (e p) n")
                                 ).then_inc(ew_loaded[u], 16)
                    sp.dma_start(ew2[u][:].rearrange("p h n -> p (h n)"), A["W2"][bass.ds(2 * i + u, 1)].rearrange("e p n -> (e p) n")
                                 ).then_inc(ew_loaded[u], 16)
            sp.wait_ge(down_out, NEXP * len(pairs) + 2)
            sp.dma_start(out, H[:]).then_inc(stored, 16)
            sp.wait_ge(stored, 16)

        @block.gpsimd
        def _(pool):
            for t in (xin[0], xin[1], g0[0], g0[1]):
                last = pool.memset(t[:], 0.0)
            last.then_inc(cleared, 1)

            pool.wait_ge(ln_done, 1)
            pool.memset(NT[96:97, :, :, :], 1.0)
            pool.memset(ot1[64:65, :, :], 1.0).then_inc(ones_set, 1)
            for a in range(2):
                pool.wait_ge(tr_out, NQ * (a + 1))
                pool.wait_ge(ones_set, 1)

                def copy_images(u, at):
                    for h in range(2):
                        for c in range(4):
                            last = pool.tensor_copy(xg[u][:, h, :, c * NTOK:(c + 1) * NTOK],
                                                    NT[:, h, :, bass.ds(at, BI)].rearrange("p s i -> p i s"))
                    last.then_inc(xg_ready, 1)

                def gather(t, u):
                    pool.wait_ge(o_mm, 4 * (t + NITS * a - 1))
                    copy_images(u, t * BI)

                def keys(t, u):
                    pool.wait_ge(qk_ready, 4 * (t + NITS * a + 1))
                    for sub in range(4):
                        n = 4 * (t + NITS * a) + sub
                        v = sub % 2
                        pool.wait_ge(s_mm, n + 1)
                        for h in range(2):
                            for j in range(4):
                                last = pool.tensor_tensor(
                                    kbd[v][:, h, j, :].rearrange("p (g k) -> p g k", g=6),
                                    bc(qkT[u][:, 2 + h, 4 * sub + j, :], 1, 6),
                                    bc(headmask[:], 2, NTOK), ALU.mult)
                        last.then_inc(kbd_ready, 1)

                for u in range(2):
                    if a == 1:
                        pool.wait_ge(o_mm, 4 * NITS)
                    copy_images(u, u * BI)
                with pool.Fori(0, NITS // 2 - 1) as i:
                    for u in range(2):
                        keys(2 * i + u, u)
                        gather(2 * i + u + 2, u)
                for u in range(2):
                    keys(NITS - 2 + u, u)

        @block.tensor
        def _(pe):
            pe.wait_ge(w_built, 1)
            pe.sem_inc(conv1_steps, 1)
            pe.sem_inc(conv2_blocks, 1)
            pe.sem_inc(down_mm, 1)

            def conv0(i, k, first):
                n = SPS * i + k
                u = k % 2
                pe.wait_ge(xin_loaded[u], 48 * (NGRP * i + k // 2 + 1))
                xv = xin[u]
                for j in range(3):
                    if first == 1:
                        pe.wait_ge(gelu0_done, j + 1)
                    elif first is None:
                        pe.wait_ge(gelu3_done, 3 * n + j + 1)
                    for c in range(2):
                        y = 4 * j + 2 * c
                        for dx in range(3):
                            last = pe.matmul(ps[0:LANES, 2 * j + c, 0:CH], w0[:, dx, :],
                                             xv[:, y:y + 2, :, dx:dx + RH], start=(dx == 0), stop=(dx == 2))
                    last.then_inc(conv0_done, 1)

            def pointwise(i, k, last_step):
                n = SPS * i + k
                u, g = k % 2, k % NGRP
                pe.wait_ge(gelud_done, n + 1)
                for j in range(3):
                    if last_step:
                        pe.wait_ge(gelu3_done, 3 * (n - 1) + j + 1 + 6)
                    else:
                        pe.wait_ge(gelu0_done, 3 * (n + 1) + j + 1)
                    for c in range(2):
                        y = 4 * j + 2 * c
                        pe.matmul(ps[0:LANES, 2 * j + c, 0:CH], wpw[:, g, :], acc[u][:, y:y + 2, :],
                                  start=True, stop=False)
                        last = pe.matmul(ps[0:LANES, 2 * j + c, 0:CH], ident[0:LANES, 0:LANES],
                                         g0[u][:, y + 1:y + 3, :, 1:RH + 1], start=False, stop=True)
                    last.then_inc(pw_done, 1)

            def conv1(i, k):
                g = k % NGRP
                pe.wait_ge(p_loaded, pcount[SPS] * i + pcount[k + 1] + 1)
                for c in range(0, GRPR[g], 3):
                    q = place[("conv1", k, c)]
                    n = min(3, GRPR[g] - c)
                    pe.wait_ge(c12_out, NCH * i + q + 1)
                    for h in range(2):
                        last = pe.matmul(ps[0:64, 6 + q % 2, 0:n * 9 * BI], w1[:, h, :],
                                         patches[:, h, c:c + n, :], start=(h == 0), stop=(h == 1))
                    last.then_inc(c12_done, 1)
                pe.wait_ge(c12_done, NCH * i + q + 1)
                pe.sem_inc(conv1_steps, 1)

            def conv2(i, b):
                pe.wait_ge(h1_shifted, 16 * (2 * i + b + 1))
                hv = h1[:].rearrange("p (y x i) -> p y x i", y=21, x=21)
                for part in range(2):
                    q = place[("conv2", b, part)]
                    pe.wait_ge(c12_out, NCH * i + q + 1)
                    for odd in range(2):
                        for dy in range(2):
                            y0 = 10 * part + dy
                            last = pe.matmul(ps[64 * odd:64 * odd + 64, 6 + q % 2, 0:25 * BI], w2[:, dy, :],
                                             hv[:, y0:y0 + 9:2, 2 * odd:2 * odd + 17:4, :],
                                             start=(dy == 0), stop=(dy == 1))
                    last.then_inc(c12_done, 1)
                pe.wait_ge(c12_done, NCH * i + q + 1)
                pe.sem_inc(conv2_blocks, 1)

            def superblock(i, last):
                for k in range(SPS):
                    if k == NGRP + 1:
                        conv2(i, 0)
                    if k:
                        conv1(i, k - 1)
                    pointwise(i, k, last and k == SPS - 1)
                    if k < SPS - 2:
                        conv0(i, k + 2, None)
                    elif not last:
                        conv0(i + 1, k + 2 - SPS, None)
                conv1(i, SPS - 1)
                conv2(i, 1)

            conv0(0, 0, 0)
            conv0(0, 1, 1)
            with pe.Fori(0, NSB - 1) as i:
                superblock(i, False)
            superblock(NSB - 1, True)

            pe.wait_ge(c12_out, NSB * NCH + 2)
            for n, (s, m) in enumerate(pairs):
                if n >= 4:
                    pe.wait_ge(h_ready, n - 3)
                for t in range(max(s, 1), s + m):
                    y, x = divmod(t - 1, 5)
                    for dy in range(2):
                        last = pe.matmul(ps[:, n % 4, (t - s) * E:(t - s + 1) * E], h2[:, (2 * y + dy) * 5 + x, :],
                                         w3[:, dy, :], start=(dy == 0), stop=(dy == 1))
                last.then_inc(conv3_mm, 1)

            def turn_tokens(a):
                pe.wait_ge(ln_done, [1, 3, 4][a])
                for n, (h, s, m) in enumerate(quads):
                    if a or n >= 4:
                        pe.wait_ge(tr_out, NQ * a + n - 3)
                    for t in range(m):
                        last = pe.transpose(ps[0:96, 4 + n % 4, t * 128:(t + 1) * 128],
                                            N[:, s + t, 96 * h:96 * h + 96], ident[:])
                    last.then_inc(tr_mm, 1)

            def attention(a):
                KR = (96, 97)

                def qk(t, u):
                    T = t + NITS * a
                    pe.wait_ge(xg_ready, T + 1)
                    for m in range(4):
                        for rot in range(2 if a == 0 else 1):
                            if a == 0:
                                pe.wait_ge(qk_out, 8 * t + 2 * m + rot + 1)
                                bank = rot
                                w = wrot if rot else wa[0]
                            else:
                                pe.wait_ge(qk_out, 8 * NITS + 4 * t + m + 1)
                                bank = m % 2
                                w = wa[1]
                            for h in range(2):
                                last = pe.matmul(ps[0:96, bank, 0:NTOK * BI], w[0:KR[h], h, 96 * m:96 * m + 96],
                                                 xg[u][0:KR[h], h, :, 0:NTOK], start=(h == 0), stop=(h == 1))
                            last.then_inc(qk_mm, 1)

                def scores(t, u, sub):
                    n = 4 * (t + NITS * a) + sub
                    pe.wait_ge(kbd_ready, n + 1)
                    pe.wait_ge(s_out, n + 1)
                    v = sub % 2
                    for j in range(4):
                        for h in range(2):
                            last = pe.matmul(ps[32 * j:32 * j + NTOK, 2 + v, h * 156:(h + 1) * 156],
                                             qkT[u][:, h, 4 * sub + j, :], kbd[v][:, h, j, :],
                                             start=True, stop=True)
                    last.then_inc(s_mm, 1)

                def values(t, u, sub):
                    n = 4 * (t + NITS * a) + sub
                    for b in range(2):
                        pe.wait_ge(v_out, 2 * n + b + 1)
                        for j in range(2):
                            for h in range(2):
                                last = pe.matmul(ps[0:104, 5 + b, j * E:(j + 1) * E],
                                                 xg[u][0:KR[h], h, 4 * sub + 2 * b + j, :],
                                                 wa[a][0:KR[h], h, 2 * E:3 * E], start=(h == 0), stop=(h == 1))
                        last.then_inc(v_mm, 1)

                def outputs(t, u, sub):
                    n = 4 * (t + NITS * a) + sub
                    v = sub % 2
                    pe.wait_ge(p_ready, n + 1)
                    pe.wait_ge(pt_out, n + 1)
                    for c in range(3):
                        last = pe.transpose(ps[0:104, 4, c * 128:(c + 1) * 128],
                                            P[v][:, 4 * c:4 * c + 4, :], ident[:])
                    last.then_inc(pt_mm, 1)
                    pe.wait_ge(v_out, 2 * n + 4)
                    pe.wait_ge(pt_out, n + 2)
                    pe.wait_ge(o_out, n + 1)
                    for c in range(3):
                        for j in range(4):
                            last = pe.matmul(ps[64 * (c % 2):64 * (c % 2) + 64, 7,
                                                (c // 2) * 104 + j * NTOK:(c // 2) * 104 + (j + 1) * NTOK],
                                             vbd[v][:, j, 64 * c:64 * c + 64], PT[v][:, c, 32 * j:32 * j + NTOK],
                                             start=True, stop=True)
                    last.then_inc(o_mm, 1)

                def turn(t, u):
                    qk(t, u)
                    pe.wait_ge(qk_ready, 4 * (t + NITS * a + 1))
                    scores(t, u, 0)
                    for sub in range(4):
                        if sub < 3:
                            scores(t, u, sub + 1)
                        values(t, u, sub)
                        outputs(t, u, sub)

                with pe.Fori(0, NITS // 2) as i:
                    for u in range(2):
                        turn(2 * i + u, u)

                pe.wait_ge(o_out, 4 * NITS * (a + 1) + 1)
                pe.wait_ge(ones_set, 1)
                for n, (s, m) in enumerate(pairs):
                    if a or n >= 2:
                        pe.wait_ge(proj_out, len(pairs) * a + n - 1)
                    for t in range(m):
                        o = ps[:, n % 2, t * E:(t + 1) * E]
                        pe.matmul(o, ot0[:, s + t, :], wp0[a][:], start=True, stop=False)
                        last = pe.matmul(o, ot1[:, s + t, :], wp1[a][:], start=False, stop=True)
                    last.then_inc(proj_mm, 1)

            pe.wait_ge(ps_cleared, 1)
            turn_tokens(0)
            attention(0)
            turn_tokens(1)
            attention(1)
            turn_tokens(2)

            pe.wait_ge(tr_out, 3 * NQ)
            for s in range(NTOK):
                for h in range(2):
                    last = pe.matmul(ps[:, 0, s * NEXP:(s + 1) * NEXP], NT[0:96, h, s, :], wg[:, h, :],
                                     start=(h == 0), stop=(h == 1))
            last.then_inc(lg_mm, 1)
            pe.wait_ge(gates_ready, 1)
            for n, (s, m) in enumerate(ebl):
                if n >= 2:
                    pe.wait_ge(gt_out, n - 1)
                for t in range(m):
                    last = pe.transpose(ps[0:NEXP, 1 + n % 2, t * 128:(t + 1) * 128], gates[:, s + t, :], ident[:])
                last.then_inc(gt_mm, 1)
            pe.wait_ge(gt_out, len(ebl))
            for n, (s, m) in enumerate(pairs):
                if n >= 2:
                    pe.wait_ge(b2_out, n - 1)
                for t in range(m):
                    last = pe.matmul(ps[:, 3 + n % 2, t * E:(t + 1) * E], gT[:, s + t, :], b2[:], start=True, stop=True)
                last.then_inc(b2_mm, 1)

            with pe.Fori(0, NEXP // 2) as i:
                for u in range(2):
                    pe.wait_ge(ew_loaded[u], 32 * (i + 1))
                    for n, (s, m) in enumerate(ebl):
                        w = (n + u) % 2
                        for c in range(HC):
                            q = (u * len(ebl) + n) * HC + c
                            pe.wait_ge(up_out, 2 * len(ebl) * HC * i + q + 1)
                            for h in range(2):
                                last = pe.matmul(ps[:, q % 3, 0:m * 128], ew1[u][:, h, c * 128:(c + 1) * 128],
                                                 NT[0:96, h, s:s + m, :], start=(h == 0), stop=(h == 1))
                            last.then_inc(up_mm, 1)
                        pe.wait_ge(up_out, 2 * len(ebl) * HC * i + q + 4)
                        for p in range(0, m, 2):
                            d = u * len(pairs) + (s + p) // 2
                            pe.wait_ge(down_out, 2 * len(pairs) * i + d + 1)
                            for t in range(2):
                                for c in range(HC):
                                    last = pe.matmul(ps[:, 3 + d % 2, t * E:(t + 1) * E],
                                                     hT[w][:, c, (p + t) * 128:(p + t + 1) * 128], ew2[u][:, c, :],
                                                     start=(c == 0), stop=(c == HC - 1))
                            last.then_inc(down_mm, 1)
                    pe.wait_ge(down_mm, len(pairs) * (2 * i + u + 1) + 1)
                    pe.sem_inc(exp_done, 1)

        @block.scalar
        def _(act):
            act.wait_ge(w_loaded, ALL_LOADED)
            act.wait_ge(cleared, 1)
            act.sem_inc(gelu3_done, 6)
            act.sem_inc(c12_out, 2)
            act.sem_inc(pt_out, 1)
            act.sem_inc(o_out, 1)
            act.sem_inc(up_out, 3)

            def gelu0(i, k, first):
                n = SPS * i + k
                u = k % 2
                if not first:
                    act.wait_ge(pw_done, 3 * (n - 1) + 6)
                for j in range(3):
                    act.wait_ge(conv0_done, 3 * n + j + 1)
                    act.activation(g0[u][:, 4 * j + 1:4 * j + 5, :, 1:RH + 1].rearrange("p y i x -> p (y i) x"),
                                   ps[0:LANES, 2 * j:2 * j + 2, 0:CH], ACT.Gelu,
                                   bias=sb0[:, 1:2], scale=sb0[:, 0:1]).then_inc(gelu0_done, 1)

            def gelu_dw(i, k):
                n = SPS * i + k
                act.wait_ge(dw_done, n + 1)
                act.activation(acc[k % 2][:], acc[k % 2][:], ACT.Gelu,
                               bias=sbdw[:, 1, k % NGRP:k % NGRP + 1]).then_inc(gelud_done, 1)

            def gelu3(i, k):
                n = SPS * i + k
                act.wait_ge(p_loaded, pcount[SPS] * i + pcount[k] + 1)
                for j in range(3):
                    act.wait_ge(pw_done, 3 * n + j + 1 + 6)
                    src = ps[0:LANES, 2 * j:2 * j + 2, 0:CH].rearrange("p c (l x) -> p c l x", x=RH)
                    dst = g3[:].rearrange("p (y x) (a b i) -> p a b y i x", y=4, a=3, b=3)
                    for b in range(3):
                        last = act.activation(dst[:, j, b], src[:, :, :, 4 * b:4 * b + 4], ACT.Gelu,
                                              bias=bpw[:, k % NGRP:k % NGRP + 1])
                    last.then_inc(gelu3_done, 1)

            hv = h1[0:64, :].rearrange("p (y x i) -> p y x i", y=21, x=21)

            def gelu1(i, k):
                g, b = k % NGRP, k // NGRP
                if g == 0:
                    act.wait_ge(conv2_blocks, 2 * i + b + 1)
                for c in range(0, GRPR[g], 3):
                    q = place[("conv1", k, c)]
                    act.wait_ge(c12_done, NCH * i + q + 1)
                    for m in range(min(3, GRPR[g] - c)):
                        gy, gx = divmod(RG * g + c + m, G7)
                        last = act.activation(hv[:, 3 * gy:3 * gy + 3, 3 * gx:3 * gx + 3, :].rearrange("p y x i -> p y (x i)"),
                                              ps[0:64, 6 + q % 2, m * 9 * BI:(m + 1) * 9 * BI].rearrange("p (y w) -> p y w", y=3),
                                              ACT.Gelu, bias=sb1[:, 1:2], scale=sb1[:, 0:1])
                    last.then_inc(c12_out, 1)
                if g == NGRP - 1:
                    act.wait_ge(c12_out, NCH * i + q + 1 + 2)
                    act.sem_inc(h1_done, 1)

            def gelu2(i, b):
                for part in range(2):
                    q = place[("conv2", b, part)]
                    act.wait_ge(c12_done, NCH * i + q + 1)
                    act.wait_ge(cleared, 1)
                    act.activation(h2[:, 25 * part:25 * part + 25, bass.ds(i * SBI + b * BI, BI)],
                                   ps[:, 6 + q % 2, 0:25 * BI].rearrange("p (y i) -> p y i", i=BI), ACT.Gelu,
                                   bias=sb2[:, 1:2], scale=sb2[:, 0:1]).then_inc(c12_out, 1)

            def superblock(i, last):
                for k in range(SPS):
                    if k == NGRP + 1:
                        gelu2(i, 0)
                    if k:
                        gelu1(i, k - 1)
                    gelu_dw(i, k)
                    gelu3(i, k)
                    if k < SPS - 2:
                        gelu0(i, k + 2, False)
                    elif not last:
                        gelu0(i + 1, k + 2 - SPS, False)
                gelu1(i, SPS - 1)
                gelu2(i, 1)

            gelu0(0, 0, True)
            gelu0(0, 1, True)
            with act.Fori(0, NSB - 1) as i:
                superblock(i, False)
            superblock(NSB - 1, True)

            def std(n):
                act.wait_ge(var_ready, n + 1)
                act.activation(rstd[:], mv[:, :, 1], ACT.Sqrt, bias=epsv).then_inc(std_ready, 1)

            epsv = stats[:, 0, 0:1]

            def turn_tokens(a):
                for n, (h, s, m) in enumerate(quads):
                    act.wait_ge(tr_mm, NQ * a + n + 1)
                    src = ps[0:96, 4 + n % 4, 0:m * 128]
                    dst = NT[0:96, h, s:s + m, :]
                    if a == 0:
                        act.activation(dst, src, ACT.Identity).then_inc(tr_out, 1)
                    else:
                        act.activation(dst, src, ACT.Identity, scale=lnwb[:, 2 * a - 2, h:h + 1],
                                       bias=lnwb[:, 2 * a - 1, h:h + 1]).then_inc(tr_out, 1)

            def attention(a):
                def turn(t, u):
                    T = t + NITS * a
                    if a == 1:
                        act.wait_ge(s_mm, 4 * T - 4 + 2)
                        for m in range(4):
                            act.wait_ge(qk_mm, 8 * NITS + 4 * t + m + 1)
                            act.activation(qkT[u][:, m], ps[0:96, m % 2, 0:NTOK * BI], ACT.Identity
                                           ).then_inc(qk_out, 1)
                            act.wait_ge(qk_out, 8 * NITS + 4 * t + m + 1 + 2)
                            act.sem_inc(qk_ready, 1)

                    def exps(sub):
                        n = 4 * T + sub
                        act.wait_ge(s_shift, n + 1)
                        act.activation(P[sub % 2][:], P[sub % 2][:], ACT.Exp, scale=HD ** -0.5).then_inc(s_exp, 1)

                    exps(0)
                    for sub in range(4):
                        n = 4 * T + sub
                        if sub < 3:
                            exps(sub + 1)
                        act.wait_ge(pt_mm, n + 1)
                        act.activation(PT[sub % 2][:], ps[0:104, 4, 0:384], ACT.Identity).then_inc(pt_out, 1)
                        act.wait_ge(o_mm, n + 1)
                        at = t * BI + 4 * sub
                        act.wait_ge(cleared, 1)
                        act.activation(ot0[:, :, bass.ds(at, 4)], ps[:, 7, 0:104].rearrange("p (j q) -> p q j", j=4),
                                       ACT.Identity)
                        act.activation(ot1[0:64, :, bass.ds(at, 4)],
                                       ps[0:64, 7, 104:208].rearrange("p (j q) -> p q j", j=4),
                                       ACT.Identity).then_inc(o_out, 1)

                with act.Fori(0, NITS // 2) as i:
                    for u in range(2):
                        turn(2 * i + u, u)

            std(0)
            turn_tokens(0)
            attention(0)
            std(1)
            std(2)
            turn_tokens(1)
            attention(1)
            std(3)
            turn_tokens(2)
            act.wait_ge(e_ready, 1)
            act.activation(gg[:, 1, :], gg[:, 0, :], ACT.Exp).then_inc(e_exp, 1)
            for n, (s, m) in enumerate(ebl):
                act.wait_ge(gt_mm, n + 1)
                act.activation(gT[:, s:s + m, :], ps[0:NEXP, 1 + n % 2, 0:m * 128], ACT.Identity).then_inc(gt_out, 1)
            with act.Fori(0, NEXP // 2) as i:
                for u in range(2):
                    act.copy(b1e[u][:], b1t[:, bass.ds((2 * i + u) * HC, HC)]).then_inc(b1_here, 1)
                    act.wait_ge(b1_here, 2 * i + u + 1)
                    for n, (s, m) in enumerate(ebl):
                        w = (n + u) % 2
                        before = max(s - 4, 0) // 2 if n else 0
                        act.wait_ge(down_mm, len(pairs) * (2 * i + u) + before + 1)
                        for c in range(HC):
                            q = (u * len(ebl) + n) * HC + c
                            act.wait_ge(up_mm, 2 * len(ebl) * HC * i + q + 1)
                            act.activation(hT[w][:, c, 0:m * 128], ps[:, q % 3, 0:m * 128], ACT.Gelu,
                                           bias=b1e[u][:, c:c + 1]).then_inc(up_out, 1)

        @block.vector
        def _(dve):
            links = [0]

            def link(ins):
                links[0] += 1
                ins.then_inc(chain, 1)
                dve.wait_ge(chain, links[0])

            dve.wait_ge(w_loaded, ALL_LOADED)
            for dx in range(3):
                dve.tensor_tensor(w0[:, dx, :].rearrange("p (r c) -> p r c", r=RG),
                                  bc(w0rep[:, dx, :], 1, RG), bc(regmask[0:90, 0:RG], 2, C1), ALU.mult)
            link(dve.tensor_tensor(pwrep[:], pwrep[:], spwrep[:], ALU.mult))
            for g in range(NGRP):
                dve.tensor_tensor(wpw[:, g, :].rearrange("p (r c) -> p r c", r=RG),
                                  bc(pwrep[:, g, :], 1, RG), bc(regmask[:, RG:2 * RG], 2, C1), ALU.mult)
            dve.tensor_tensor(wdw[:], wdw[:], bc(sbdw[:, 0, :], 2, 9), ALU.mult)
            for dy in range(2):
                dve.tensor_tensor(w3[:, dy, :], w3[:, dy, :], s3row[:], ALU.mult)
            for h in range(2):
                src = wa[0][:, h, 0:2 * E].rearrange("p (n e) -> p n e", e=2)
                dst = wrot[:, h, :].rearrange("p (n e) -> p n e", e=2)
                dve.tensor_scalar(dst[:, :, 0], src[:, :, 1], -1.0, None, ALU.mult)
                last = dve.tensor_copy(dst[:, :, 1], src[:, :, 0])
            last.then_inc(w_built, 1)
            dve.wait_ge(w_built, 1)
            dve.sem_inc(pw_done, 6)
            dve.sem_inc(qk_out, 2)
            dve.sem_inc(s_out, 2)
            dve.sem_inc(s_mm, 2)
            dve.sem_inc(v_out, 2)
            dve.sem_inc(exp_done, 2)

            def depthwise(i, k):
                n = SPS * i + k
                u, g = k % 2, k % NGRP
                dve.wait_ge(gelu0_done, 3 * (n + 1))
                dve.wait_ge(pw_done, 3 * (n - 1) + 6)
                o = acc[u][:].rearrange("p y (i x) -> p (y i) x", x=RH)
                for t in range(9):
                    dy, dx = divmod(t, 3)
                    src = g0[u][:, dy:dy + RH, :, dx:dx + RH].rearrange("p y i x -> p (y i) x")
                    if t == 0:
                        ins = dve.tensor_scalar(o, src, wdw[:, g, 0:1], None, ALU.mult)
                    else:
                        dve.wait_ge(dwtap, 8 * n + t)
                        ins = dve.scalar_tensor_tensor(o, src, wdw[:, g, t:t + 1], o, ALU.mult, ALU.add)
                    ins.then_inc(dw_done if t == 8 else dwtap, 1)

            with dve.Fori(0, NSB) as i:
                for k in range(SPS):
                    depthwise(i, k)

            for n, (s, m) in enumerate(pairs):
                dve.wait_ge(conv3_mm, n + 1)
                a = max(s, 1)
                dve.tensor_tensor(H[:, a:s + m, :], ps[:, n % 4, (a - s) * E:m * E].rearrange("p (t e) -> p t e", e=E),
                                  bc(b3row[:], 1, s + m - a), ALU.add).then_inc(h_ready, 1)
            dve.wait_ge(h_ready, len(pairs))
            dve.wait_ge(cls_loaded, 16)
            link(dve.memset(ps[:, 2:4, :], 0.0))
            dve.sem_inc(ps_cleared, 1)

            def layernorm(n, src, dst):
                for s in range(NTOK):
                    last = dve.bn_stats(stats[:, s, :], src[:, s, :])
                link(last)
                for s in range(NTOK):
                    last = dve.bn_aggr(mv[:, s, :], stats[:, s, :])
                link(last)
                link(dve.memset(stats[:, 0, 0:1], EPS))
                dve.sem_inc(var_ready, 1)
                dve.wait_ge(std_ready, n + 1)
                link(dve.reciprocal(rstd[:], rstd[:]))
                for s in range(NTOK):
                    last = dve.tensor_scalar(dst[:, s, :], src[:, s, :], mv[:, s, 0:1], rstd[:, s:s + 1],
                                             ALU.subtract, ALU.mult)
                link(last)
                dve.sem_inc(ln_done, 1)

            def attention(a):
                def turn(t, u):
                    T = t + NITS * a
                    if a == 0:
                        for m in range(4):
                            for rot in range(2):
                                dve.wait_ge(qk_mm, 8 * t + 2 * m + rot + 1)
                                dve.tensor_tensor(rope[m % 2][:, rot], ps[0:96, rot, 0:NTOK * BI].rearrange("p (i s) -> p i s", i=BI),
                                                  bc((sin if rot else cos)[:], 1, BI), ALU.mult).then_inc(qk_out, 1)
                            dve.wait_ge(qk_out, 8 * t + 2 * m + 2 + 2)
                            dve.tensor_tensor(qkT[u][:, m], rope[m % 2][:, 0], rope[m % 2][:, 1], ALU.add
                                              ).then_inc(qk_ready, 1)

                    def softmax(sub):
                        n = 4 * T + sub
                        v = sub % 2
                        Pv = P[v]
                        S = ps[:, 2 + v, 0:HEADS * NTOK].rearrange("p (h k) -> p h k", k=NTOK)
                        base = 3 * n
                        dve.wait_ge(s_mm, n + 1 + 2)
                        if a == 0:
                            dve.tensor_tensor(Pv[:], S, bc(causal[:], 1, HEADS), ALU.add).then_inc(s_out, 1)
                        else:
                            dve.tensor_copy(Pv[:], S).then_inc(s_out, 1)
                        dve.wait_ge(s_out, n + 1 + 2)
                        dve.tensor_reduce(smax[:], Pv[:], AX_X, ALU.max).then_inc(sm, 1)
                        dve.wait_ge(sm, base + 1)
                        dve.tensor_tensor(Pv[:], Pv[:], bc(smax[:], 2, NTOK), ALU.subtract).then_inc(s_shift, 1)

                    def normalise(sub):
                        n = 4 * T + sub
                        Pv = P[sub % 2]
                        dve.wait_ge(s_exp, n + 1)
                        dve.tensor_reduce(ssum[:], Pv[:], AX_X, ALU.add).then_inc(sm, 1)
                        dve.wait_ge(sm, 3 * n + 2)
                        dve.reciprocal(srec[:], ssum[:]).then_inc(sm, 1)
                        dve.wait_ge(sm, 3 * n + 3)
                        dve.tensor_tensor(Pv[:], Pv[:], bc(srec[:], 2, NTOK), ALU.mult).then_inc(p_ready, 1)

                    def values(sub):
                        n = 4 * T + sub
                        for b in range(2):
                            dve.wait_ge(v_mm, 2 * n + b + 1)
                            dve.tensor_tensor(vbd[sub % 2][:, 2 * b:2 * b + 2, :],
                                              ps[0:104, 5 + b, 0:2 * E].rearrange("p (j e) -> p j e", j=2),
                                              bc(vmask[:], 1, 2), ALU.mult).then_inc(v_out, 1)

                    for sub in range(4):
                        softmax(sub)
                        values(sub)
                        normalise(sub)

                with dve.Fori(0, NITS // 2) as i:
                    for u in range(2):
                        turn(2 * i + u, u)
                for n, (s, m) in enumerate(pairs):
                    dve.wait_ge(proj_mm, len(pairs) * a + n + 1)
                    R = (H, X)[a]
                    dve.tensor_tensor(R[:, s:s + m, :], R[:, s:s + m, :],
                                      ps[:, n % 2, 0:m * E].rearrange("p (t e) -> p t e", e=E), ALU.add
                                      ).then_inc(proj_out, 1)
                dve.wait_ge(proj_out, len(pairs) * (a + 1))

            layernorm(0, H, N)
            attention(0)
            layernorm(1, H, X)
            layernorm(2, X, N)
            attention(1)
            layernorm(3, X, N)

            dve.wait_ge(lg_mm, 1)
            link(dve.tensor_copy(logits[:], ps[:, 0, 0:NTOK * NEXP].rearrange("p (s e) -> p s e", e=NEXP)))
            for s in range(NTOK):
                last = dve.max(top[:, s, :], logits[:, s, :])
            link(last)
            for s in range(NTOK):
                last = dve.max_index(topi[:, s, :], top[:, s, :], logits[:, s, :])
            link(last)
            link(dve.tensor_copy(topf[:], topi[:, :, 0:2]))
            link(dve.tensor_tensor(gg[:, 0, :], top[:, :, 1], top[:, :, 0], ALU.subtract))
            dve.sem_inc(e_ready, 1)
            dve.wait_ge(e_exp, 1)
            link(dve.tensor_scalar(gg[:, 0, :], gg[:, 1, :], 1.0, None, ALU.add))
            link(dve.reciprocal(gg[:, 2, :], gg[:, 0, :]))
            link(dve.tensor_tensor(gg[:, 3, :], gg[:, 1, :], gg[:, 2, :], ALU.mult))
            link(dve.tensor_tensor(gates[:], bc(iota8[:], 1, NTOK), bc(topf[:, :, 0], 2, NEXP), ALU.is_equal))
            link(dve.tensor_tensor(gates[:], gates[:], bc(gg[:, 2, :], 2, NEXP), ALU.mult))
            link(dve.tensor_tensor(oneh[:], bc(iota8[:], 1, NTOK), bc(topf[:, :, 1], 2, NEXP), ALU.is_equal))
            link(dve.tensor_tensor(oneh[:], oneh[:], bc(gg[:, 3, :], 2, NEXP), ALU.mult))
            link(dve.tensor_tensor(gates[:], gates[:], oneh[:], ALU.add))
            dve.sem_inc(gates_ready, 1)
            link(dve.tensor_tensor(H[:], H[:], X[:], ALU.add))
            for n, (s, m) in enumerate(pairs):
                dve.wait_ge(b2_mm, n + 1)
                dve.tensor_tensor(H[:, s:s + m, :], H[:, s:s + m, :],
                                  ps[:, 3 + n % 2, 0:m * E].rearrange("p (t e) -> p t e", e=E), ALU.add
                                  ).then_inc(b2_out, 1)
            dve.wait_ge(b2_out, len(pairs))
            dve.sem_inc(down_out, 2)
            with dve.Fori(0, NEXP // 2) as i:
                for u in range(2):
                    for n, (s, m) in enumerate(pairs):
                        d = u * len(pairs) + n
                        dve.wait_ge(down_mm, 2 * len(pairs) * i + d + 2)
                        for t in range(m):
                            last = dve.scalar_tensor_tensor(H[:, s + t, :], ps[:, 3 + d % 2, t * E:(t + 1) * E],
                                                            gates[:, s + t, bass.ds(2 * i + u, 1)], H[:, s + t, :],
                                                            ALU.mult, ALU.add)
                        last.then_inc(down_out, 1)


def shape_constants(np):
    f = np.float32
    k = {"k_ident": np.eye(128, dtype=f)}
    reg = np.zeros((LANES, 2 * RG), f)
    for p in range(90):
        reg[p, (p % 30) // 3] = 1
    for p in range(LANES):
        reg[p, RG + p // C1] = 1
    k["k_regmask"] = reg
    k["k_headmask"] = (np.arange(96)[:, None] // HD == np.arange(6)[None, :]).astype(f)
    k["k_vmask"] = (np.arange(104)[:, None] // NTOK == (np.arange(E)[None, :] % 64) // HD).astype(f)
    q = np.minimum(np.arange(128) % 32, NTOK - 1)
    k["k_causal"] = np.where(np.arange(NTOK)[None, :] <= q[:, None], 0, -1e30).astype(f)
    inv = (f(1) / np.power(f(10000), np.arange(0, HD, 2, dtype=f) / f(HD))).astype(f)
    fr = (np.arange(NTOK, dtype=f)[:, None] * inv[None, :]).astype(f)
    for name, fn in (("k_cos", np.cos), ("k_sin", np.sin)):
        k[name] = np.ascontiguousarray(np.tile(np.repeat(fn(fr), 2, axis=-1).T, (6, 1)).astype(f))
    k["k_iota"] = np.tile(np.arange(NEXP, dtype=f), (128, 1))
    return k


def by_group(np, a, *tail):
    a = a.reshape((NREG * C1,) + tail)
    a = np.concatenate([a, np.zeros((NGRP * LANES - NREG * C1,) + tail, a.dtype)])
    return np.swapaxes(a.reshape((NGRP, LANES) + tail), 0, 1)


def lay_out(np, v):
    f = np.float32
    d = {}
    p = np.zeros((NIMG, CIN, HW + 2, HW + 2), f)
    p[:, :, 1:HW + 1, 1:HW + 1] = v["x"]
    w = np.empty((NBLK, NREG, CIN, WIN, BI, WIN), f)
    for r in range(NREG):
        y, x = RH * (r // G7), RH * (r % G7)
        w[:, r] = p[:, :, y:y + WIN, x:x + WIN].reshape(NBLK, BI, CIN, WIN, WIN).transpose(0, 2, 3, 1, 4)
    d["windows"] = w.reshape(NBLK, NREG * CIN, WIN * LINE)
    t = v["L0_tok_w0"].transpose(2, 1, 3, 0)
    d["w0"] = np.repeat(t[:, None], RG, axis=1).reshape(90, 3, C1)
    d["sb0"] = np.tile(np.stack([v["L0_tok_s0"], v["L0_tok_b0"]], 1), (RG, 1))
    d["wdw"] = by_group(np, v["L0_tok_wdw"], 9)
    d["sbdw"] = np.stack([by_group(np, v["L0_tok_sdw"]), by_group(np, v["L0_tok_bdw"])], 1)
    d["bpw"] = by_group(np, v["L0_tok_bpw"])
    t = v["L0_tok_wpw"].reshape(NREG, C1, C1).transpose(0, 2, 1)
    d["wpw"] = by_group(np, t, C1)
    d["spw"] = by_group(np, np.repeat(v["L0_tok_spw"].reshape(NREG, 1, C1), C1, axis=1), C1)
    t = np.zeros((C1 * 16, 64), f)
    t[:, :C2] = v["L0_tok_w1"].transpose(1, 2, 3, 0).reshape(C1 * 16, C2)
    d["w1"] = t.reshape(2, 96, 64).transpose(1, 0, 2)
    t = np.zeros((64, 2), f)
    t[:C2, 0], t[:C2, 1] = v["L0_tok_s1"], v["L0_tok_b1"]
    d["sb1"] = t
    t = np.zeros((2, 64, 2), f)
    t[:, :C2, 0], t[:, :C2, 1] = v["L0_tok_s2"], v["L0_tok_b2"]
    d["sb2"] = t.reshape(128, 2)
    for name, m, mp in (("w2", C2, 64), ("w3", E, E)):
        t = np.zeros((2, 64, 2, mp), f)
        t[:, :C2, :, :m] = v["L0_tok_" + name].transpose(3, 1, 2, 0)
        d[name] = t.reshape(128, 2, mp)
    for a, (w, b) in enumerate(((v["L0_attn_W_attn"], v["L0_attn_b_attn"]),
                                (v["L0_ffn_qkv_w"].T, v["L0_ffn_qkv_b"]))):
        t = np.zeros((97, 2, 3 * E), f)
        t[:96] = w.reshape(2, 96, 3 * E).transpose(1, 0, 2)
        t[96, 1] = b
        d[f"wa{a}"] = t
    d["wp0"] = np.concatenate([v["L0_attn_W_proj"], v["L0_attn_b_proj"][None]])
    d["wp1"] = np.concatenate([v["L0_ffn_proj_w"].T, v["L0_ffn_proj_b"][None]])
    d["lnwb"] = np.stack([v["L0_ffn_" + n].reshape(2, 96).T for n in ("norm1_w", "norm1_b", "norm2_w", "norm2_b")], 1)
    d["wg"] = v["L0_ffn_w_gate"].reshape(2, 96, NEXP).transpose(1, 0, 2)
    d["b1"] = v["L0_ffn_b1"].reshape(NEXP * HC, 128).T
    d["W1"] = v["L0_ffn_W1"].reshape(NEXP, 2, 96, HID).transpose(0, 2, 1, 3).reshape(NEXP * 96, 2 * HID)
    d["W1"] = d["W1"].reshape(NEXP, 96, 2 * HID)
    d["W2"] = v["L0_ffn_W2"].reshape(NEXP, HC, 128, E).transpose(0, 2, 1, 3).reshape(NEXP, 128, HC * E)
    for n in ("cls_tok", "L0_tok_s3", "L0_tok_b3", "L0_ffn_b2"):
        d[n] = v[n]
    return d


def kernel(**inputs):
    import numpy as _np
    import concourse.bacc as _bacc
    from concourse import mybir as _mybir
    from concourse.bass_utils import run_bass_kernel_spmd as _run

    nc = _bacc.Bacc("TRN2", target_bir_lowering=False, num_devices=1)
    arrays, A = {}, {}
    every = lay_out(_np, {name: _np.asarray(a) for name, a in inputs.items()})
    every.update(shape_constants(_np))
    for name, a in every.items():
        arrays[f"in_{name}_dram"] = _np.ascontiguousarray(a)
        A[name] = nc.dram_tensor(f"in_{name}_dram", a.shape, _mybir.dt.from_np(a.dtype), kind="ExternalInput").ap()
    out = nc.dram_tensor("out_0_dram", (NIMG, NTOK, E), _mybir.dt.float32, kind="ExternalOutput").ap()
    vit_tower(nc, A, out)
    r = _run(nc, [arrays], core_ids=[0])
    return r.results[0]["out_0_dram"]
```

```python
from contextlib import ExitStack

import concourse.bass as bass
from concourse import mybir

F32 = mybir.dt.float32
F32R = mybir.dt.float32r
U32 = mybir.dt.uint32
ACT = mybir.ActivationFunctionType
ALU = mybir.AluOpType
AX_X = mybir.AxisListType.X

NIMG, CIN, HW = 128, 3, 84
G7, RH = 7, 12
NREG = G7 * G7
C1, C2, E = 12, 48, 192
RG = 10
NGRP = 5
BI = 16
NBLK = NIMG // BI
SBI = 2 * BI
NSB = NIMG // SBI
SPS = 2 * NGRP
LANES = RG * C1
WIN = RH + 2
LINE = BI * WIN
GRPR = [RG] * (NGRP - 1) + [NREG - RG * (NGRP - 1)]
CH = 2 * BI * RH
NTOK = 26
HEADS, HD = 12, 16
NEXP, HID = 8, 768
HC = HID // 128
EPS = 1e-5
CONSTS = ["k_ident", "k_regmask", "k_headmask", "k_vmask", "k_causal", "k_cos", "k_sin", "k_iota"]


def bc(ap, dim, n):
    a = ap.unsqueeze(dim)
    shape = list(a.shape)
    shape[dim] = n
    return a.broadcast_to(shape)


CPS = [-(-r // 3) for r in GRPR]
CPB = sum(CPS) + 2


def conv1_chunk(i, k, c):
    return 2 * CPB * i + CPB * (k // NGRP) + sum(CPS[:k % NGRP]) + c


def conv2_chunk(i, b, part):
    return 2 * CPB * i + CPB * b + CPB - 2 + part


def vit_tower(nc, A, out):
    def all_patches(i, k, u):
        full, part = (sum(32 * GRPR[t % NGRP] for t in range(m) if t % 2 == u) for m in (SPS, k))
        return full * i + part + 1

    with ExitStack() as ctx:
        def sb(name, shape, dt=F32, to=ctx):
            return to.enter_context(nc.sbuf_tensor(name, shape, dt))

        def sem(name):
            return ctx.enter_context(nc.semaphore(name))

        ident = sb("ident", [128, 128])
        regmask = sb("regmask", [LANES, 2 * RG])
        headmask = sb("headmask", [96, 6])
        vmask = sb("vmask", [104, E])
        causal = sb("causal", [128, NTOK])
        cos = sb("cos", [96, NTOK])
        sin = sb("sin", [96, NTOK])
        iota8 = sb("iota8", [128, NEXP])
        sb0 = sb("sb0", [LANES, 2])
        sb1 = sb("sb1", [128, 2])
        sb2 = sb("sb2", [128, 2])
        w3 = sb("w3", [128, 2, E])
        s3row = sb("s3row", [128, E])
        b3row = sb("b3row", [128, E])
        wa = [sb(f"wa{a}", [97, 2, 3 * E]) for a in range(2)]
        wrot = sb("wrot", [97, 2, 2 * E])
        wp0 = [sb(f"wp0_{a}", [128, E]) for a in range(2)]
        wp1 = [sb(f"wp1_{a}", [65, E]) for a in range(2)]
        lnwb = sb("lnwb", [96, 4, 2])
        wg = sb("wg", [96, 2, NEXP])
        b2 = sb("b2", [NEXP, E])
        b1t = sb("b1t", [128, NEXP * HC])

        conv = ExitStack()
        h2 = sb("h2", [128, 50, NIMG], to=conv)
        w0rep = sb("w0rep", [90, 3, C1], to=conv)
        w0h = sb("w0h", [90, 3, LANES], F32R, to=conv)
        w0l = sb("w0l", [90, 3, LANES], F32R, to=conv)
        wpwh = sb("wpwh", [LANES, NGRP, LANES], F32R, to=conv)
        wpwl = sb("wpwl", [LANES, NGRP, LANES], F32R, to=conv)
        wdw = sb("wdw", [LANES, NGRP, 9], to=conv)
        sbdw = sb("sbdw", [LANES, 2, NGRP], to=conv)
        pwrep = sb("pwrep", [LANES, NGRP, C1], to=conv)
        spwrep = sb("spwrep", [LANES, NGRP, C1], to=conv)
        bpw = sb("bpw", [LANES, NGRP], to=conv)
        w1 = sb("w1", [96, 2, 64], to=conv)
        w2 = sb("w2", [128, 2, 64], to=conv)
        xin = sb("xin", [90, RH, BI, WIN], to=conv)
        xh = sb("xh", [90, RH, BI, WIN], F32R, to=conv)
        xl = sb("xl", [90, RH, BI, WIN], F32R, to=conv)
        dh = sb("dh", [LANES, RH, BI * RH], F32R, to=conv)
        dl = sb("dl", [LANES, RH, BI * RH], F32R, to=conv)
        g0 = [sb(f"g0_{u}", [LANES, WIN, BI, WIN], to=conv) for u in range(2)]
        acc = [sb(f"acc{u}", [LANES, RH, BI * RH], to=conv) for u in range(2)]
        g3 = sb("g3", [LANES, 16, 9 * BI], to=conv)
        patches = [sb(f"patches{u}", [96, 2, RG, 9 * BI], to=conv) for u in range(2)]
        whole = ExitStack()
        w0 = sb("w0", [90, 3, LANES], to=whole)
        wpw = sb("wpw", [LANES, NGRP, LANES], to=whole)
        whole.close()
        h1 = sb("h1", [128, 21 * 21 * BI], to=conv)
        conv.close()

        ot0 = sb("ot0", [128, NTOK, NIMG])
        ot1 = sb("ot1", [65, NTOK, NIMG])
        H = sb("H", [128, NTOK, E])
        X = sb("X", [128, NTOK, E])
        N = sb("N", [128, NTOK, E])
        NT = sb("NT", [97, 2, NTOK, NIMG])
        stats = sb("stats", [128, NTOK, 6])
        mv = sb("mv", [128, NTOK, 2])
        rstd = sb("rstd", [128, NTOK])
        att = ExitStack()
        xg = [sb(f"xg{u}", [97, 2, 4, 4 * NTOK], to=att) for u in range(2)]
        qkT = [sb(f"qkT{u}", [96, 4, BI, NTOK], to=att) for u in range(2)]
        rope = [sb(f"rope{u}", [96, 2, BI, NTOK], to=att) for u in range(2)]
        kbd = [sb(f"kbd{u}", [96, 2, 4, 6 * NTOK], to=att) for u in range(2)]
        P = [sb(f"P{u}", [128, HEADS, NTOK], to=att) for u in range(2)]
        PT = [sb(f"PT{u}", [104, 3, 128], to=att) for u in range(2)]
        vbd = [sb(f"vbd{u}", [104, 4, E], to=att) for u in range(2)]
        smax = sb("smax", [128, HEADS], to=att)
        ssum = sb("ssum", [128, HEADS], to=att)
        srec = sb("srec", [128, HEADS], to=att)
        att.close()
        ew1 = [sb(f"ew1_{u}", [96, 2, HID]) for u in range(2)]
        ew2 = [sb(f"ew2_{u}", [128, HC, E]) for u in range(2)]
        b1e = [sb(f"b1e{u}", [128, HC]) for u in range(2)]
        hT = [sb(f"hT{u}", [128, HC, 512]) for u in range(2)]
        logits = sb("logits", [128, NTOK, NEXP])
        top = sb("top", [128, NTOK, 8])
        topi = sb("topi", [128, NTOK, 8], U32)
        topf = sb("topf", [128, NTOK, 2])
        gg = sb("gg", [128, 4, NTOK])
        oneh = sb("oneh", [128, NTOK, NEXP])
        gates = sb("gates", [128, NTOK, NEXP])
        gT = sb("gT", [NEXP, NTOK, 128])

        ps = ctx.enter_context(nc.psum_tensor("ps", [128, 8, 512], F32))

        w_loaded = sem("w_loaded")
        cleared = sem("cleared")
        w_built = sem("w_built")
        xin_loaded = sem("xin_loaded")
        conv0_done = sem("conv0_done")
        gelu0_done = sem("gelu0_done")
        xh_done = sem("xh_done")
        xl_done = sem("xl_done")
        dh_done = sem("dh_done")
        dl_done = sem("dl_done")
        dw_done = sem("dw_done")
        dwtap = sem("dwtap")
        gelud_done = sem("gelud_done")
        pw_done = sem("pw_done")
        gelu3_done = sem("gelu3_done")
        p_loaded = [sem(f"p_loaded{u}") for u in range(2)]
        c12_done = sem("c12_done")
        c12_out = sem("c12_out")
        conv1_steps = sem("conv1_steps")
        h1_done = sem("h1_done")
        h1_shifted = sem("h1_shifted")
        conv2_blocks = sem("conv2_blocks")

        block = ctx.enter_context(nc.Block())

        loads = []

        def load(dst, src):
            loads.append((dst, src))

        for dst, name in ((ident, "k_ident"), (regmask, "k_regmask"), (headmask, "k_headmask"), (vmask, "k_vmask"),
                          (causal, "k_causal"), (cos, "k_cos"), (sin, "k_sin"), (iota8, "k_iota"),
                          (w0rep, "w0"), (sb0, "sb0"), (wdw, "wdw"), (sbdw, "sbdw"), (pwrep, "wpw"), (spwrep, "spw"),
                          (bpw, "bpw"), (w1, "w1"), (sb1, "sb1"), (w2, "w2"), (sb2, "sb2"), (w3, "w3"),
                          (wa[0], "wa0"), (wa[1], "wa1"), (lnwb, "lnwb"), (wg, "wg"), (b2, "L0_ffn_b2"), (b1t, "b1")):
            load(dst[:], A[name])
        for a in range(2):
            load(wp0[a][:], A[f"wp{a}"][0:128])
            load(wp1[a][:], A[f"wp{a}"][128:193])
        load(s3row[:], A["L0_tok_s3"].unsqueeze(0).broadcast_to([128, E]))
        load(b3row[:], A["L0_tok_b3"].unsqueeze(0).broadcast_to([128, E]))
        ALL_LOADED = 16 * len(loads)

        conv3_mm = sem("conv3_mm")
        h_ready = sem("h_ready")
        cls_loaded = sem("cls_loaded")
        chain = sem("chain")
        var_ready = sem("var_ready")
        std_ready = sem("std_ready")
        ln_done = sem("ln_done")
        tr_mm = sem("tr_mm")
        tr_out = sem("tr_out")
        ones_set = sem("ones_set")
        xg_ready = sem("xg_ready")
        qk_mm = sem("qk_mm")
        qk_out = sem("qk_out")
        rope_mul = sem("rope_mul")
        qk_ready = sem("qk_ready")
        kbd_ready = sem("kbd_ready")
        s_mm = sem("s_mm")
        s_out = sem("s_out")
        s_shift = sem("s_shift")
        sm = sem("softmax_stat")
        s_exp = sem("s_exp")
        p_ready = sem("p_ready")
        pt_mm = sem("pt_mm")
        pt_out = sem("pt_out")
        v_mm = sem("v_mm")
        v_out = sem("v_out")
        o_mm = sem("o_mm")
        o_out = sem("o_out")
        proj_mm = sem("proj_mm")
        proj_out = sem("proj_out")
        ps_cleared = sem("ps_cleared")
        lg_mm = sem("lg_mm")
        e_ready = sem("e_ready")
        e_exp = sem("e_exp")
        gates_ready = sem("gates_ready")
        gt_mm = sem("gt_mm")
        gt_out = sem("gt_out")
        b2_mm = sem("b2_mm")
        b2_out = sem("b2_out")
        ew_loaded = [sem(f"ew_loaded{u}") for u in range(2)]
        b1_here = sem("b1_here")
        up_mm = sem("up_mm")
        up_out = sem("up_out")
        down_mm = sem("down_mm")
        down_out = sem("down_out")
        exp_done = sem("exp_done")
        stored = sem("stored")

        pairs = [(s, min(2, NTOK - s)) for s in range(0, NTOK, 2)]
        quads = [(h, s, min(4, NTOK - s)) for h in range(2) for s in range(0, NTOK, 4)]
        NQ = len(quads)
        ebl = [(s, min(4, NTOK - s)) for s in range(0, NTOK, 4)]
        NITS = NIMG // BI

        @block.sync
        def _(sp):
            for u in range(2):
                sp.sem_inc(p_loaded[u], 1)
            for dst, src in loads:
                sp.dma_start(dst, src).then_inc(w_loaded, 16)

            def load_xin(i, k):
                g, b = k % NGRP, k // NGRP
                for dy in range(3):
                    sp.dma_start(xin[30 * dy:30 * dy + 3 * GRPR[g]].rearrange("p y i x -> p (y i x)"),
                                 A["windows"][bass.ds(2 * i + b, 1), 3 * RG * g:3 * (RG * g + GRPR[g]),
                                              dy * LINE:(dy + RH) * LINE].rearrange("b r w -> (b r) w")
                                 ).then_inc(xin_loaded, 16)

            def shift_h1(i, b):
                sp.wait_ge(h1_done, 2 * i + b + 1)
                sp.dma_start(h1[64:128, 0:(21 * 21 - 1) * BI], h1[0:64, BI:21 * 21 * BI]
                             ).then_inc(h1_shifted, 16)

            def step(i, k):
                if k % NGRP == 1 and k > NGRP:
                    shift_h1(i, k // NGRP - 1)
                if not (isinstance(i, int) and SPS * i + k + 3 >= SPS * NSB):
                    sp.wait_ge(xl_done, 3 * (SPS * i + k + 3))
                    load_xin(i, k + 3)
                sp.wait_ge(gelu3_done, 3 * (SPS * i + k + 1) + 6)
                sp.wait_ge(conv1_steps, SPS * i + k + 1)
                for r in range(GRPR[k % NGRP]):
                    for h in range(2):
                        sp.dma_start(patches[k % 2][:, h, r, :], g3[r * C1 + 6 * h:r * C1 + 6 * h + 6, :, :]
                                     ).then_inc(p_loaded[k % 2], 16)

            sp.wait_ge(cleared, 1)
            load_xin(0, 0)
            for k in range(1, 3):
                sp.wait_ge(xl_done, 3 * k)
                load_xin(0, k)
            for k in range(2):
                step(0, k)
            with sp.Fori(0, NSB - 1) as i:
                for k in range(2, SPS + 2):
                    step(i, k)
            for k in range(2, SPS):
                step(NSB - 1, k)
            shift_h1(NSB - 1, 1)

            sp.wait_ge(conv3_mm, 1)
            sp.dma_start(H[:, 0, :], A["cls_tok"].rearrange("a b d -> (a b) d").broadcast_to([128, E])
                         ).then_inc(cls_loaded, 16)

            sp.wait_ge(proj_out, 2 * len(pairs))
            with sp.Fori(0, NEXP // 2) as i:
                for u in range(2):
                    sp.wait_ge(exp_done, 2 * i + u + 1)
                    sp.dma_start(ew1[u][:].rearrange("p h n -> p (h n)"), A["W1"][bass.ds(2 * i + u, 1)].rearrange("e p n -> (e p) n")
                                 ).then_inc(ew_loaded[u], 16)
                    sp.dma_start(ew2[u][:].rearrange("p h n -> p (h n)"), A["W2"][bass.ds(2 * i + u, 1)].rearrange("e p n -> (e p) n")
                                 ).then_inc(ew_loaded[u], 16)
            sp.wait_ge(down_out, NEXP * len(pairs) + 2)
            sp.dma_start(out, H[:]).then_inc(stored, 16)
            sp.wait_ge(stored, 16)

        @block.gpsimd
        def _(pool):
            for t in (xin, g0[0], g0[1]):
                last = pool.memset(t[:], 0.0)
            last.then_inc(cleared, 1)
            pool.sem_inc(dl_done, 6)

            def low_of_input(i, k):
                n = SPS * i + k
                pool.wait_ge(xh_done, n + 1)
                for j in range(3):
                    y = slice(4 * j, 4 * j + 4)
                    pool.tensor_tensor(xl[:, y], xin[:, y], xh[:, y].bitcast(F32), ALU.subtract).then_inc(xl_done, 1)

            def low_of_depthwise(i, k):
                n = SPS * i + k
                for j in range(3):
                    pool.wait_ge(dh_done, 3 * n + j + 1)
                    y = slice(4 * j, 4 * j + 4)
                    pool.tensor_tensor(dl[:, y], acc[k % 2][:, y], dh[:, y].bitcast(F32), ALU.subtract
                                       ).then_inc(dl_done, 1)

            def step(i, k):
                low_of_depthwise(i, k)
                if not (isinstance(i, int) and SPS * i + k + 2 >= SPS * NSB):
                    low_of_input(i, k + 2)

            for k in range(2):
                low_of_input(0, k)
            for k in range(2):
                step(0, k)
            with pool.Fori(0, NSB - 1) as i:
                for k in range(2, SPS + 2):
                    step(i, k)
            for k in range(2, SPS):
                step(NSB - 1, k)

            pool.wait_ge(ln_done, 1)
            pool.memset(NT[96:97, :, :, :], 1.0)
            pool.memset(ot1[64:65, :, :], 1.0).then_inc(ones_set, 1)
            for a in range(2):
                def keys(t, u, sub):
                    n = 4 * (t + NITS * a) + sub
                    if sub == 0:
                        pool.wait_ge(qk_ready, 4 * (t + NITS * a + 1))
                    pool.wait_ge(s_mm, n + 1)
                    for h in range(2):
                        for j in range(4):
                            last = pool.tensor_tensor(
                                kbd[sub % 2][:, h, j, :].rearrange("p (g k) -> p g k", g=6),
                                bc(qkT[u][:, 2 + h, 4 * sub + j, :], 1, 6),
                                bc(headmask[:], 2, NTOK), ALU.mult)
                    last.then_inc(kbd_ready, 1)

                with pool.Fori(0, NITS // 2) as i:
                    for u in range(2):
                        for sub in range(4):
                            keys(2 * i + u, u, sub)

        @block.tensor
        def _(pe):
            pe.wait_ge(w_built, 1)
            pe.sem_inc(conv1_steps, 2)
            pe.sem_inc(conv2_blocks, 1)
            pe.sem_inc(down_mm, 1)
            pe.sem_inc(v_mm, 2)

            def conv0(i, k, first):
                n = SPS * i + k
                for j in range(3):
                    if first == 1:
                        pe.wait_ge(gelu0_done, j + 1)
                    elif first is None:
                        pe.wait_ge(gelu3_done, 3 * n + j + 1)
                    pe.wait_ge(xl_done, 3 * n + j + 1)
                    for c in range(2):
                        y = 4 * j + 2 * c
                        for t, (w, x, dx) in enumerate([(w, x, dx) for w, x in ((w0h, xh), (w0l, xh), (w0h, xl))
                                                        for dx in range(3)]):
                            last = pe.matmul(ps[0:LANES, 2 * j + c, 0:CH], w[:, dx, :],
                                             x[:, y:y + 2, :, dx:dx + RH], start=(t == 0), stop=(t == 8))
                    last.then_inc(conv0_done, 1)

            def pointwise(i, k, last_step):
                n = SPS * i + k
                u, g = k % 2, k % NGRP
                for j in range(3):
                    if last_step:
                        pe.wait_ge(gelu3_done, 3 * (n - 1) + j + 1 + 6)
                    else:
                        pe.wait_ge(gelu0_done, 3 * (n + 1) + j + 1)
                    pe.wait_ge(dl_done, 3 * n + j + 1 + 6)
                    for c in range(2):
                        y = 4 * j + 2 * c
                        for t, (w, x) in enumerate(((wpwh, dh), (wpwl, dh), (wpwh, dl))):
                            pe.matmul(ps[0:LANES, 2 * j + c, 0:CH], w[:, g, :], x[:, y:y + 2, :],
                                      start=(t == 0), stop=False)
                        last = pe.matmul(ps[0:LANES, 2 * j + c, 0:CH], ident[0:LANES, 0:LANES],
                                         g0[u][:, y + 1:y + 3, :, 1:RH + 1], start=False, stop=True)
                    last.then_inc(pw_done, 1)

            def conv1(i, k):
                g = k % NGRP
                pe.wait_ge(p_loaded[k % 2], all_patches(i, k + 1, k % 2))
                pe.wait_ge(c12_out, conv1_chunk(i, k, 0) + 1)
                for c in range(CPS[g]):
                    n = min(3, GRPR[g] - 3 * c)
                    lanes = slice(64 * (c // 2), 64 * (c // 2) + 64)
                    for h in range(2):
                        last = pe.matmul(ps[lanes, 6 + c % 2, 0:n * 9 * BI], w1[:, h, :],
                                         patches[k % 2][:, h, 3 * c:3 * c + n, :], start=(h == 0), stop=(h == 1))
                    last.then_inc(c12_done, 1)
                pe.wait_ge(c12_done, conv1_chunk(i, k, c) + 1)
                pe.sem_inc(conv1_steps, 1)

            def conv2(i, b):
                pe.wait_ge(h1_shifted, 16 * (2 * i + b + 1))
                pe.wait_ge(c12_out, conv2_chunk(i, b, 0) + 1)
                hv = h1[:].rearrange("p (y x i) -> p y x i", y=21, x=21)
                for part in range(2):
                    for odd in range(2):
                        for dy in range(2):
                            y0 = 10 * part + dy
                            last = pe.matmul(ps[64 * odd:64 * odd + 64, 6 + part, 0:25 * BI], w2[:, dy, :],
                                             hv[:, y0:y0 + 9:2, 2 * odd:2 * odd + 17:4, :],
                                             start=(dy == 0), stop=(dy == 1))
                    last.then_inc(c12_done, 1)
                pe.wait_ge(c12_done, conv2_chunk(i, b, 1) + 1)
                pe.sem_inc(conv2_blocks, 1)

            def step(i, k):
                static = isinstance(i, int)
                pointwise(i, k, static and SPS * i + k == SPS * NSB - 1)
                if not (static and SPS * i + k + 2 >= SPS * NSB):
                    conv0(i, k + 2, None)
                if k % NGRP == 1 and k > NGRP:
                    conv2(i, k // NGRP - 1)
                if not (static and SPS * i + k == 0):
                    conv1(i, k - 1)

            conv0(0, 0, 0)
            conv0(0, 1, 1)
            for k in range(2):
                step(0, k)
            with pe.Fori(0, NSB - 1) as i:
                for k in range(2, SPS + 2):
                    step(i, k)
            for k in range(2, SPS):
                step(NSB - 1, k)
            conv1(NSB - 1, SPS - 1)
            conv2(NSB - 1, 1)

            pe.wait_ge(c12_out, NBLK * CPB + 1)
            for n, (s, m) in enumerate(pairs):
                if n >= 4:
                    pe.wait_ge(h_ready, n - 3)
                for t in range(max(s, 1), s + m):
                    y, x = divmod(t - 1, 5)
                    for dy in range(2):
                        last = pe.matmul(ps[:, n % 4, (t - s) * E:(t - s + 1) * E], h2[:, (2 * y + dy) * 5 + x, :],
                                         w3[:, dy, :], start=(dy == 0), stop=(dy == 1))
                last.then_inc(conv3_mm, 1)

            def turn_tokens(a):
                pe.wait_ge(ln_done, [1, 3, 4][a])
                for n, (h, s, m) in enumerate(quads):
                    if a or n >= 4:
                        pe.wait_ge(tr_out, NQ * a + n - 3)
                    for t in range(m):
                        last = pe.transpose(ps[0:96, 4 + n % 4, t * 128:(t + 1) * 128],
                                            N[:, s + t, 96 * h:96 * h + 96], ident[:])
                    last.then_inc(tr_mm, 1)

            def attention(a):
                KR = (96, 97)

                def qk(t, m):
                    for rot in range(2 if a == 0 else 1):
                        q = 8 * t + 2 * m + rot if a == 0 else 8 * NITS + 4 * t + m
                        w = wrot if rot else wa[a]
                        pe.wait_ge(qk_out, q + 1)
                        for h in range(2):
                            last = pe.matmul(ps[0:96, (2 * m + rot if a == 0 else m) % 2, 0:NTOK * BI],
                                             w[0:KR[h], h, 96 * m:96 * m + 96],
                                             NT[0:KR[h], h, :, bass.ds(t * BI, BI)].rearrange("p s i -> p i s"),
                                             start=(h == 0), stop=(h == 1))
                        last.then_inc(qk_mm, 1)

                def scores(t, u, sub):
                    n = 4 * (t + NITS * a) + sub
                    pe.wait_ge(kbd_ready, n + 1)
                    pe.wait_ge(s_out, n + 1)
                    v = sub % 2
                    for j in range(4):
                        for h in range(2):
                            last = pe.matmul(ps[32 * j:32 * j + NTOK, 2 + v, h * 156:(h + 1) * 156],
                                             qkT[u][:, h, 4 * sub + j, :], kbd[v][:, h, j, :],
                                             start=True, stop=True)
                    last.then_inc(s_mm, 1)

                def values(t, u, sub):
                    n = 4 * (t + NITS * a) + sub
                    pe.wait_ge(xg_ready, n + 1)
                    for b in range(2):
                        pe.wait_ge(v_out, 2 * n + b + 1)
                        for j in range(2):
                            for h in range(2):
                                last = pe.matmul(ps[0:104, 5 + b, j * E:(j + 1) * E],
                                                 xg[sub % 2][0:KR[h], h, 2 * b + j, :],
                                                 wa[a][0:KR[h], h, 2 * E:3 * E], start=(h == 0), stop=(h == 1))
                        last.then_inc(v_mm, 1)

                def outputs(t, u, sub):
                    n = 4 * (t + NITS * a) + sub
                    v = sub % 2
                    pe.wait_ge(p_ready, n + 1)
                    pe.wait_ge(pt_out, n + 1)
                    for c in range(3):
                        last = pe.transpose(ps[0:104, 4, c * 128:(c + 1) * 128],
                                            P[v][:, 4 * c:4 * c + 4, :], ident[:])
                    last.then_inc(pt_mm, 1)
                    pe.wait_ge(v_out, 2 * n + 4)
                    pe.wait_ge(pt_out, n + 2)
                    pe.wait_ge(o_out, n + 1)
                    for c in range(3):
                        for j in range(4):
                            last = pe.matmul(ps[64 * (c % 2):64 * (c % 2) + 64, 7,
                                                (c // 2) * 104 + j * NTOK:(c // 2) * 104 + (j + 1) * NTOK],
                                             vbd[v][:, j, 64 * c:64 * c + 64], PT[v][:, c, 32 * j:32 * j + NTOK],
                                             start=True, stop=True)
                    last.then_inc(o_mm, 1)

                def turn(t, u, final):
                    for sub in range(4):
                        if sub < 3:
                            scores(t, u, sub + 1)
                        elif not final:
                            scores(t + 1, 1 - u, 0)
                        values(t, u, sub)
                        if sub < 2 and not final:
                            qk(t + 1, 2 * sub)
                            qk(t + 1, 2 * sub + 1)
                        outputs(t, u, sub)

                pe.wait_ge(tr_out, NQ * (a + 1))
                pe.wait_ge(ones_set, 1)
                for m in range(4):
                    qk(0, m)
                scores(0, 0, 0)
                with pe.Fori(0, NITS // 2 - 1) as i:
                    for u in range(2):
                        turn(2 * i + u, u, False)
                turn(NITS - 2, 0, False)
                turn(NITS - 1, 1, True)

                pe.wait_ge(o_out, 4 * NITS * (a + 1) + 1)
                for n, (s, m) in enumerate(pairs):
                    if a or n >= 2:
                        pe.wait_ge(proj_out, len(pairs) * a + n - 1)
                    for t in range(m):
                        o = ps[:, n % 2, t * E:(t + 1) * E]
                        pe.matmul(o, ot0[:, s + t, :], wp0[a][:], start=True, stop=False)
                        last = pe.matmul(o, ot1[:, s + t, :], wp1[a][:], start=False, stop=True)
                    last.then_inc(proj_mm, 1)

            pe.wait_ge(ps_cleared, 1)
            turn_tokens(0)
            attention(0)
            turn_tokens(1)
            attention(1)
            turn_tokens(2)

            pe.wait_ge(tr_out, 3 * NQ)
            for s in range(NTOK):
                for h in range(2):
                    last = pe.matmul(ps[:, 0, s * NEXP:(s + 1) * NEXP], NT[0:96, h, s, :], wg[:, h, :],
                                     start=(h == 0), stop=(h == 1))
            last.then_inc(lg_mm, 1)
            pe.wait_ge(gates_ready, 1)
            for n, (s, m) in enumerate(ebl):
                if n >= 2:
                    pe.wait_ge(gt_out, n - 1)
                for t in range(m):
                    last = pe.transpose(ps[0:NEXP, 1 + n % 2, t * 128:(t + 1) * 128], gates[:, s + t, :], ident[:])
                last.then_inc(gt_mm, 1)
            pe.wait_ge(gt_out, len(ebl))
            for n, (s, m) in enumerate(pairs):
                if n >= 2:
                    pe.wait_ge(b2_out, n - 1)
                for t in range(m):
                    last = pe.matmul(ps[:, 3 + n % 2, t * E:(t + 1) * E], gT[:, s + t, :], b2[:], start=True, stop=True)
                last.then_inc(b2_mm, 1)

            with pe.Fori(0, NEXP // 2) as i:
                for u in range(2):
                    pe.wait_ge(ew_loaded[u], 32 * (i + 1))
                    for n, (s, m) in enumerate(ebl):
                        w = (n + u) % 2
                        for c in range(HC):
                            q = (u * len(ebl) + n) * HC + c
                            pe.wait_ge(up_out, 2 * len(ebl) * HC * i + q + 1)
                            for h in range(2):
                                last = pe.matmul(ps[:, q % 3, 0:m * 128], ew1[u][:, h, c * 128:(c + 1) * 128],
                                                 NT[0:96, h, s:s + m, :], start=(h == 0), stop=(h == 1))
                            last.then_inc(up_mm, 1)
                        pe.wait_ge(up_out, 2 * len(ebl) * HC * i + q + 4)
                        for p in range(0, m, 2):
                            d = u * len(pairs) + (s + p) // 2
                            pe.wait_ge(down_out, 2 * len(pairs) * i + d + 1)
                            for t in range(2):
                                for c in range(HC):
                                    last = pe.matmul(ps[:, 3 + d % 2, t * E:(t + 1) * E],
                                                     hT[w][:, c, (p + t) * 128:(p + t + 1) * 128], ew2[u][:, c, :],
                                                     start=(c == 0), stop=(c == HC - 1))
                            last.then_inc(down_mm, 1)
                    pe.wait_ge(down_mm, len(pairs) * (2 * i + u + 1) + 1)
                    pe.sem_inc(exp_done, 1)

        @block.scalar
        def _(act):
            act.wait_ge(w_loaded, ALL_LOADED)
            act.wait_ge(cleared, 1)
            act.sem_inc(gelu3_done, 6)
            act.sem_inc(c12_out, 1)
            act.sem_inc(pt_out, 1)
            act.sem_inc(o_out, 1)
            act.sem_inc(up_out, 3)

            def gelu0(i, k, first):
                n = SPS * i + k
                u = k % 2
                if not first:
                    act.wait_ge(pw_done, 3 * (n - 1) + 6)
                for j in range(3):
                    act.wait_ge(conv0_done, 3 * n + j + 1)
                    act.activation(g0[u][:, 4 * j + 1:4 * j + 5, :, 1:RH + 1].rearrange("p y i x -> p (y i) x"),
                                   ps[0:LANES, 2 * j:2 * j + 2, 0:CH], ACT.Gelu,
                                   bias=sb0[:, 1:2], scale=sb0[:, 0:1]).then_inc(gelu0_done, 1)

            def high_of_input(i, k):
                n = SPS * i + k
                act.wait_ge(xin_loaded, 48 * (n + 1))
                if not (isinstance(n, int) and n == 0):
                    act.wait_ge(conv0_done, 3 * n)
                act.copy(xh[:], xin[:]).then_inc(xh_done, 1)

            def gelu_dw(i, k):
                n = SPS * i + k
                act.wait_ge(dw_done, n + 1)
                def gelu_rows(j):
                    y = slice(4 * j, 4 * j + 4)
                    act.activation(acc[k % 2][:, y], acc[k % 2][:, y], ACT.Gelu,
                                   bias=sbdw[:, 1, k % NGRP:k % NGRP + 1]).then_inc(gelud_done, 1)

                def high_rows(j):
                    y = slice(4 * j, 4 * j + 4)
                    act.wait_ge(gelud_done, 3 * n + j + 1)
                    act.wait_ge(pw_done, 3 * (n - 1) + j + 1 + 6)
                    act.copy(dh[:, y], acc[k % 2][:, y]).then_inc(dh_done, 1)

                gelu_rows(0)
                gelu_rows(1)
                high_rows(0)
                gelu_rows(2)
                high_rows(1)
                high_rows(2)

            def gelu3(i, k):
                n = SPS * i + k
                act.wait_ge(p_loaded[1 - k % 2], all_patches(i, k, 1 - k % 2))
                for j in range(3):
                    act.wait_ge(pw_done, 3 * n + j + 1 + 6)
                    src = ps[0:LANES, 2 * j:2 * j + 2, 0:CH].rearrange("p c (l x) -> p c l x", x=RH)
                    dst = g3[:].rearrange("p (y x) (a b i) -> p a b y i x", y=4, a=3, b=3)
                    for b in range(3):
                        last = act.activation(dst[:, j, b], src[:, :, :, 4 * b:4 * b + 4], ACT.Gelu,
                                              bias=bpw[:, k % NGRP:k % NGRP + 1])
                    last.then_inc(gelu3_done, 1)

            hv = h1[0:64, :].rearrange("p (y x i) -> p y x i", y=21, x=21)

            def gelu1(i, k):
                g, b = k % NGRP, k // NGRP
                if g == 0:
                    act.wait_ge(conv2_blocks, 2 * i + b + 1)
                for c in range(CPS[g]):
                    act.wait_ge(c12_done, conv1_chunk(i, k, c) + 1)
                    lanes = slice(64 * (c // 2), 64 * (c // 2) + 64)
                    for m in range(min(3, GRPR[g] - 3 * c)):
                        gy, gx = divmod(RG * g + 3 * c + m, G7)
                        last = act.activation(hv[:, 3 * gy:3 * gy + 3, 3 * gx:3 * gx + 3, :].rearrange("p y x i -> p y (x i)"),
                                              ps[lanes, 6 + c % 2, m * 9 * BI:(m + 1) * 9 * BI].rearrange("p (y w) -> p y w", y=3),
                                              ACT.Gelu, bias=sb1[lanes, 1:2], scale=sb1[lanes, 0:1])
                    last.then_inc(c12_out, 1)
                if g == NGRP - 1:
                    act.wait_ge(c12_out, conv1_chunk(i, k, c) + 1 + 1)
                    act.sem_inc(h1_done, 1)

            def gelu2(i, b):
                for part in range(2):
                    act.wait_ge(c12_done, conv2_chunk(i, b, part) + 1)
                    act.wait_ge(cleared, 1)
                    act.activation(h2[:, 25 * part:25 * part + 25, bass.ds(i * SBI + b * BI, BI)],
                                   ps[:, 6 + part, 0:25 * BI].rearrange("p (y i) -> p y i", i=BI), ACT.Gelu,
                                   bias=sb2[:, 1:2], scale=sb2[:, 0:1]).then_inc(c12_out, 1)

            def step(i, k):
                static = isinstance(i, int)
                gelu_dw(i, k)
                more = not (static and SPS * i + k + 2 >= SPS * NSB)
                if more:
                    high_of_input(i, k + 2)
                if not (static and SPS * i + k < 2):
                    gelu1(i, k - 2)
                gelu3(i, k)
                if more:
                    gelu0(i, k + 2, False)
                if k % NGRP == 1 and k > NGRP:
                    gelu2(i, k // NGRP - 1)

            for k in range(2):
                high_of_input(0, k)
                gelu0(0, k, True)
            for k in range(2):
                step(0, k)
            with act.Fori(0, NSB - 1) as i:
                for k in range(2, SPS + 2):
                    step(i, k)
            for k in range(2, SPS):
                step(NSB - 1, k)
            gelu1(NSB - 1, SPS - 2)
            gelu1(NSB - 1, SPS - 1)
            gelu2(NSB - 1, 1)

            def std(n):
                act.wait_ge(var_ready, n + 1)
                act.activation(rstd[:], mv[:, :, 1], ACT.Sqrt, bias=epsv).then_inc(std_ready, 1)

            epsv = stats[:, 0, 0:1]

            def turn_tokens(a):
                for n, (h, s, m) in enumerate(quads):
                    act.wait_ge(tr_mm, NQ * a + n + 1)
                    src = ps[0:96, 4 + n % 4, 0:m * 128]
                    dst = NT[0:96, h, s:s + m, :]
                    if a == 0:
                        act.activation(dst, src, ACT.Identity).then_inc(tr_out, 1)
                    else:
                        act.activation(dst, src, ACT.Identity, scale=lnwb[:, 2 * a - 2, h:h + 1],
                                       bias=lnwb[:, 2 * a - 1, h:h + 1]).then_inc(tr_out, 1)

            def attention(a):
                def qk_copy(t, u, m):
                    act.wait_ge(qk_mm, 8 * NITS + 4 * t + m + 1)
                    act.wait_ge(s_mm, 4 * (t + NITS * a) - 4 + 2)
                    act.activation(qkT[u][:, m], ps[0:96, m % 2, 0:NTOK * BI], ACT.Identity).then_inc(qk_out, 1)
                    act.wait_ge(qk_out, 8 * NITS + 4 * t + m + 1 + 2)
                    act.sem_inc(qk_ready, 1)

                def exps(t, sub):
                    n = 4 * (t + NITS * a) + sub
                    act.wait_ge(v_mm, 2 * n)
                    act.wait_ge(s_shift, n + 1)
                    act.activation(P[sub % 2][:], P[sub % 2][:], ACT.Exp, scale=HD ** -0.5).then_inc(s_exp, 1)

                def gather(t, sub):
                    for h in range(2):
                        src = NT[:, h, :, bass.ds(t * BI + 4 * sub, 4)].rearrange("p s i -> p i s")
                        last = act.copy(xg[sub % 2][:, h].rearrange("p i (c s) -> p i c s", c=4), bc(src, 2, 4))
                    last.then_inc(xg_ready, 1)

                def turn(t, u, final):
                    for sub in range(4):
                        n = 4 * (t + NITS * a) + sub
                        if not (final and sub == 3):
                            exps(t + (sub + 1) // 4, (sub + 1) % 4)
                            gather(t + (sub + 1) // 4, (sub + 1) % 4)
                        if a == 1 and sub < 2 and not final:
                            qk_copy(t + 1, 1 - u, 2 * sub)
                            qk_copy(t + 1, 1 - u, 2 * sub + 1)
                        act.wait_ge(pt_mm, n + 1)
                        act.activation(PT[sub % 2][:], ps[0:104, 4, 0:384], ACT.Identity).then_inc(pt_out, 1)
                        act.wait_ge(o_mm, n + 1)
                        at = t * BI + 4 * sub
                        act.wait_ge(cleared, 1)
                        act.activation(ot0[:, :, bass.ds(at, 4)], ps[:, 7, 0:104].rearrange("p (j q) -> p q j", j=4),
                                       ACT.Identity)
                        act.activation(ot1[0:64, :, bass.ds(at, 4)],
                                       ps[0:64, 7, 104:208].rearrange("p (j q) -> p q j", j=4),
                                       ACT.Identity).then_inc(o_out, 1)

                act.wait_ge(tr_out, NQ * (a + 1))
                act.wait_ge(ones_set, 1)
                if a == 1:
                    for m in range(4):
                        qk_copy(0, 0, m)
                gather(0, 0)
                act.wait_ge(s_shift, 4 * NITS * a + 1)
                act.activation(P[0][:], P[0][:], ACT.Exp, scale=HD ** -0.5).then_inc(s_exp, 1)
                with act.Fori(0, NITS // 2 - 1) as i:
                    for u in range(2):
                        turn(2 * i + u, u, False)
                turn(NITS - 2, 0, False)
                turn(NITS - 1, 1, True)

            std(0)
            turn_tokens(0)
            attention(0)
            std(1)
            std(2)
            turn_tokens(1)
            attention(1)
            std(3)
            turn_tokens(2)
            act.wait_ge(e_ready, 1)
            act.activation(gg[:, 1, :], gg[:, 0, :], ACT.Exp).then_inc(e_exp, 1)
            for n, (s, m) in enumerate(ebl):
                act.wait_ge(gt_mm, n + 1)
                act.activation(gT[:, s:s + m, :], ps[0:NEXP, 1 + n % 2, 0:m * 128], ACT.Identity).then_inc(gt_out, 1)
            with act.Fori(0, NEXP // 2) as i:
                for u in range(2):
                    act.copy(b1e[u][:], b1t[:, bass.ds((2 * i + u) * HC, HC)]).then_inc(b1_here, 1)
                    act.wait_ge(b1_here, 2 * i + u + 1)
                    for n, (s, m) in enumerate(ebl):
                        w = (n + u) % 2
                        before = max(s - 4, 0) // 2 if n else 0
                        act.wait_ge(down_mm, len(pairs) * (2 * i + u) + before + 1)
                        for c in range(HC):
                            q = (u * len(ebl) + n) * HC + c
                            act.wait_ge(up_mm, 2 * len(ebl) * HC * i + q + 1)
                            act.activation(hT[w][:, c, 0:m * 128], ps[:, q % 3, 0:m * 128], ACT.Gelu,
                                           bias=b1e[u][:, c:c + 1]).then_inc(up_out, 1)

        @block.vector
        def _(dve):
            links = [0]

            def link(ins):
                links[0] += 1
                ins.then_inc(chain, 1)
                dve.wait_ge(chain, links[0])

            dve.wait_ge(w_loaded, ALL_LOADED)
            for dx in range(3):
                dve.tensor_tensor(w0[:, dx, :].rearrange("p (r c) -> p r c", r=RG),
                                  bc(w0rep[:, dx, :], 1, RG), bc(regmask[0:90, 0:RG], 2, C1), ALU.mult)
            link(dve.tensor_tensor(pwrep[:], pwrep[:], spwrep[:], ALU.mult))
            for g in range(NGRP):
                last = dve.tensor_tensor(wpw[:, g, :].rearrange("p (r c) -> p r c", r=RG),
                                         bc(pwrep[:, g, :], 1, RG), bc(regmask[:, RG:2 * RG], 2, C1), ALU.mult)
            link(last)
            for w, hi, lo in ((w0, w0h, w0l), (wpw, wpwh, wpwl)):
                link(dve.tensor_copy(hi[:], w[:]))
                dve.tensor_tensor(lo[:], w[:], hi[:].bitcast(F32), ALU.subtract)
            dve.tensor_tensor(wdw[:], wdw[:], bc(sbdw[:, 0, :], 2, 9), ALU.mult)
            for dy in range(2):
                dve.tensor_tensor(w3[:, dy, :], w3[:, dy, :], s3row[:], ALU.mult)
            for h in range(2):
                src = wa[0][:, h, 0:2 * E].rearrange("p (n e) -> p n e", e=2)
                dst = wrot[:, h, :].rearrange("p (n e) -> p n e", e=2)
                dve.tensor_scalar(dst[:, :, 0], src[:, :, 1], -1.0, None, ALU.mult)
                last = dve.tensor_copy(dst[:, :, 1], src[:, :, 0])
            last.then_inc(w_built, 1)
            dve.wait_ge(w_built, 1)
            dve.sem_inc(pw_done, 6)
            dve.sem_inc(qk_out, 2)
            dve.sem_inc(s_out, 2)
            dve.sem_inc(s_mm, 2)
            dve.sem_inc(v_out, 2)
            dve.sem_inc(exp_done, 2)

            def depthwise(i, k):
                n = SPS * i + k
                u, g = k % 2, k % NGRP
                dve.wait_ge(gelu0_done, 3 * (n + 1))
                dve.wait_ge(dl_done, 3 * (n - 1) + 6)
                o = acc[u][:].rearrange("p y (i x) -> p (y i) x", x=RH)
                for t in range(9):
                    dy, dx = divmod(t, 3)
                    src = g0[u][:, dy:dy + RH, :, dx:dx + RH].rearrange("p y i x -> p (y i) x")
                    if t == 0:
                        ins = dve.tensor_scalar(o, src, wdw[:, g, 0:1], None, ALU.mult)
                    else:
                        dve.wait_ge(dwtap, 8 * n + t)
                        ins = dve.scalar_tensor_tensor(o, src, wdw[:, g, t:t + 1], o, ALU.mult, ALU.add)
                    ins.then_inc(dw_done if t == 8 else dwtap, 1)

            with dve.Fori(0, NSB) as i:
                for k in range(SPS):
                    depthwise(i, k)

            for n, (s, m) in enumerate(pairs):
                dve.wait_ge(conv3_mm, n + 1)
                a = max(s, 1)
                dve.tensor_tensor(H[:, a:s + m, :], ps[:, n % 4, (a - s) * E:m * E].rearrange("p (t e) -> p t e", e=E),
                                  bc(b3row[:], 1, s + m - a), ALU.add).then_inc(h_ready, 1)
            dve.wait_ge(h_ready, len(pairs))
            dve.wait_ge(cls_loaded, 16)
            link(dve.memset(ps[:, 2:4, :], 0.0))
            dve.sem_inc(ps_cleared, 1)

            def layernorm(n, src, dst):
                for s in range(NTOK):
                    last = dve.bn_stats(stats[:, s, :], src[:, s, :])
                link(last)
                for s in range(NTOK):
                    last = dve.bn_aggr(mv[:, s, :], stats[:, s, :])
                link(last)
                link(dve.memset(stats[:, 0, 0:1], EPS))
                dve.sem_inc(var_ready, 1)
                dve.wait_ge(std_ready, n + 1)
                link(dve.reciprocal(rstd[:], rstd[:]))
                for s in range(NTOK):
                    last = dve.tensor_scalar(dst[:, s, :], src[:, s, :], mv[:, s, 0:1], rstd[:, s:s + 1],
                                             ALU.subtract, ALU.mult)
                link(last)
                dve.sem_inc(ln_done, 1)

            def attention(a):
                def rotate(t, u, m):
                    for rot in range(2):
                        dve.wait_ge(qk_mm, 8 * t + 2 * m + rot + 1)
                        dve.tensor_tensor(rope[m % 2][:, rot], ps[0:96, rot, 0:NTOK * BI].rearrange("p (i s) -> p i s", i=BI),
                                          bc((sin if rot else cos)[:], 1, BI), ALU.mult).then_inc(qk_out, 1)
                    dve.wait_ge(qk_out, 8 * t + 2 * m + 2 + 2)
                    dve.tensor_tensor(qkT[u][:, m], rope[m % 2][:, 0], rope[m % 2][:, 1], ALU.add
                                      ).then_inc(qk_ready, 1)

                def softmax(t, sub):
                    n = 4 * (t + NITS * a) + sub
                    v = sub % 2
                    Pv = P[v]
                    S = ps[:, 2 + v, 0:HEADS * NTOK].rearrange("p (h k) -> p h k", k=NTOK)
                    base = 3 * n
                    dve.wait_ge(s_mm, n + 1 + 2)
                    if a == 0:
                        dve.tensor_tensor(Pv[:], S, bc(causal[:], 1, HEADS), ALU.add).then_inc(s_out, 1)
                    else:
                        dve.tensor_copy(Pv[:], S).then_inc(s_out, 1)
                    dve.wait_ge(s_out, n + 1 + 2)
                    dve.tensor_reduce(smax[:], Pv[:], AX_X, ALU.max).then_inc(sm, 1)
                    dve.wait_ge(sm, base + 1)
                    dve.tensor_tensor(Pv[:], Pv[:], bc(smax[:], 2, NTOK), ALU.subtract).then_inc(s_shift, 1)

                def normalise(t, sub):
                    n = 4 * (t + NITS * a) + sub
                    Pv = P[sub % 2]
                    dve.wait_ge(s_exp, n + 1)
                    dve.tensor_reduce(ssum[:], Pv[:], AX_X, ALU.add).then_inc(sm, 1)
                    dve.wait_ge(sm, 3 * n + 2)
                    dve.reciprocal(srec[:], ssum[:]).then_inc(sm, 1)
                    dve.wait_ge(sm, 3 * n + 3)
                    dve.tensor_tensor(Pv[:], Pv[:], bc(srec[:], 2, NTOK), ALU.mult).then_inc(p_ready, 1)

                def values(t, sub):
                    n = 4 * (t + NITS * a) + sub
                    for b in range(2):
                        dve.wait_ge(v_mm, 2 * n + b + 1 + 2)
                        dve.tensor_tensor(vbd[sub % 2][:, 2 * b:2 * b + 2, :],
                                          ps[0:104, 5 + b, 0:2 * E].rearrange("p (j e) -> p j e", j=2),
                                          bc(vmask[:], 1, 2), ALU.mult).then_inc(v_out, 1)

                def turn(t, u, final):
                    for sub in range(4):
                        if not (final and sub == 3):
                            softmax(t + (sub + 1) // 4, (sub + 1) % 4)
                        values(t, sub)
                        if not (final and sub == 3):
                            normalise(t + (sub + 1) // 4, (sub + 1) % 4)
                        if a == 0 and sub < 2 and not final:
                            rotate(t + 1, 1 - u, 2 * sub)
                            rotate(t + 1, 1 - u, 2 * sub + 1)

                if a == 0:
                    for m in range(4):
                        rotate(0, 0, m)
                softmax(0, 0)
                normalise(0, 0)
                with dve.Fori(0, NITS // 2 - 1) as i:
                    for u in range(2):
                        turn(2 * i + u, u, False)
                turn(NITS - 2, 0, False)
                turn(NITS - 1, 1, True)
                for n, (s, m) in enumerate(pairs):
                    dve.wait_ge(proj_mm, len(pairs) * a + n + 1)
                    R = (H, X)[a]
                    dve.tensor_tensor(R[:, s:s + m, :], R[:, s:s + m, :],
                                      ps[:, n % 2, 0:m * E].rearrange("p (t e) -> p t e", e=E), ALU.add
                                      ).then_inc(proj_out, 1)
                dve.wait_ge(proj_out, len(pairs) * (a + 1))

            layernorm(0, H, N)
            attention(0)
            layernorm(1, H, X)
            layernorm(2, X, N)
            attention(1)
            layernorm(3, X, N)

            dve.wait_ge(lg_mm, 1)
            link(dve.tensor_copy(logits[:], ps[:, 0, 0:NTOK * NEXP].rearrange("p (s e) -> p s e", e=NEXP)))
            for s in range(NTOK):
                last = dve.max(top[:, s, :], logits[:, s, :])
            link(last)
            for s in range(NTOK):
                last = dve.max_index(topi[:, s, :], top[:, s, :], logits[:, s, :])
            link(last)
            link(dve.tensor_copy(topf[:], topi[:, :, 0:2]))
            link(dve.tensor_tensor(gg[:, 0, :], top[:, :, 1], top[:, :, 0], ALU.subtract))
            dve.sem_inc(e_ready, 1)
            dve.wait_ge(e_exp, 1)
            link(dve.tensor_scalar(gg[:, 0, :], gg[:, 1, :], 1.0, None, ALU.add))
            link(dve.reciprocal(gg[:, 2, :], gg[:, 0, :]))
            link(dve.tensor_tensor(gg[:, 3, :], gg[:, 1, :], gg[:, 2, :], ALU.mult))
            link(dve.tensor_tensor(gates[:], bc(iota8[:], 1, NTOK), bc(topf[:, :, 0], 2, NEXP), ALU.is_equal))
            link(dve.tensor_tensor(gates[:], gates[:], bc(gg[:, 2, :], 2, NEXP), ALU.mult))
            link(dve.tensor_tensor(oneh[:], bc(iota8[:], 1, NTOK), bc(topf[:, :, 1], 2, NEXP), ALU.is_equal))
            link(dve.tensor_tensor(oneh[:], oneh[:], bc(gg[:, 3, :], 2, NEXP), ALU.mult))
            link(dve.tensor_tensor(gates[:], gates[:], oneh[:], ALU.add))
            dve.sem_inc(gates_ready, 1)
            link(dve.tensor_tensor(H[:], H[:], X[:], ALU.add))
            for n, (s, m) in enumerate(pairs):
                dve.wait_ge(b2_mm, n + 1)
                dve.tensor_tensor(H[:, s:s + m, :], H[:, s:s + m, :],
                                  ps[:, 3 + n % 2, 0:m * E].rearrange("p (t e) -> p t e", e=E), ALU.add
                                  ).then_inc(b2_out, 1)
            dve.wait_ge(b2_out, len(pairs))
            dve.sem_inc(down_out, 2)
            with dve.Fori(0, NEXP // 2) as i:
                for u in range(2):
                    for n, (s, m) in enumerate(pairs):
                        d = u * len(pairs) + n
                        dve.wait_ge(down_mm, 2 * len(pairs) * i + d + 2)
                        for t in range(m):
                            last = dve.scalar_tensor_tensor(H[:, s + t, :], ps[:, 3 + d % 2, t * E:(t + 1) * E],
                                                            gates[:, s + t, bass.ds(2 * i + u, 1)], H[:, s + t, :],
                                                            ALU.mult, ALU.add)
                        last.then_inc(down_out, 1)


def shape_constants(np):
    f = np.float32
    k = {"k_ident": np.eye(128, dtype=f)}
    reg = np.zeros((LANES, 2 * RG), f)
    for p in range(90):
        reg[p, (p % 30) // 3] = 1
    for p in range(LANES):
        reg[p, RG + p // C1] = 1
    k["k_regmask"] = reg
    k["k_headmask"] = (np.arange(96)[:, None] // HD == np.arange(6)[None, :]).astype(f)
    k["k_vmask"] = (np.arange(104)[:, None] // NTOK == (np.arange(E)[None, :] % 64) // HD).astype(f)
    q = np.minimum(np.arange(128) % 32, NTOK - 1)
    k["k_causal"] = np.where(np.arange(NTOK)[None, :] <= q[:, None], 0, -1e30).astype(f)
    inv = (f(1) / np.power(f(10000), np.arange(0, HD, 2, dtype=f) / f(HD))).astype(f)
    fr = (np.arange(NTOK, dtype=f)[:, None] * inv[None, :]).astype(f)
    for name, fn in (("k_cos", np.cos), ("k_sin", np.sin)):
        k[name] = np.ascontiguousarray(np.tile(np.repeat(fn(fr), 2, axis=-1).T, (6, 1)).astype(f))
    k["k_iota"] = np.tile(np.arange(NEXP, dtype=f), (128, 1))
    return k


def by_group(np, a, *tail):
    a = a.reshape((NREG * C1,) + tail)
    a = np.concatenate([a, np.zeros((NGRP * LANES - NREG * C1,) + tail, a.dtype)])
    return np.swapaxes(a.reshape((NGRP, LANES) + tail), 0, 1)


def lay_out(np, v):
    f = np.float32
    d = {}
    p = np.zeros((NIMG, CIN, HW + 2, HW + 2), f)
    p[:, :, 1:HW + 1, 1:HW + 1] = v["x"]
    w = np.empty((NBLK, NREG, CIN, WIN, BI, WIN), f)
    for r in range(NREG):
        y, x = RH * (r // G7), RH * (r % G7)
        w[:, r] = p[:, :, y:y + WIN, x:x + WIN].reshape(NBLK, BI, CIN, WIN, WIN).transpose(0, 2, 3, 1, 4)
    d["windows"] = w.reshape(NBLK, NREG * CIN, WIN * LINE)
    t = v["L0_tok_w0"].transpose(2, 1, 3, 0)
    d["w0"] = np.repeat(t[:, None], RG, axis=1).reshape(90, 3, C1)
    d["sb0"] = np.tile(np.stack([v["L0_tok_s0"], v["L0_tok_b0"]], 1), (RG, 1))
    d["wdw"] = by_group(np, v["L0_tok_wdw"], 9)
    d["sbdw"] = np.stack([by_group(np, v["L0_tok_sdw"]), by_group(np, v["L0_tok_bdw"])], 1)
    d["bpw"] = by_group(np, v["L0_tok_bpw"])
    t = v["L0_tok_wpw"].reshape(NREG, C1, C1).transpose(0, 2, 1)
    d["wpw"] = by_group(np, t, C1)
    d["spw"] = by_group(np, np.repeat(v["L0_tok_spw"].reshape(NREG, 1, C1), C1, axis=1), C1)
    t = np.zeros((C1 * 16, 64), f)
    t[:, :C2] = v["L0_tok_w1"].transpose(1, 2, 3, 0).reshape(C1 * 16, C2)
    d["w1"] = t.reshape(2, 96, 64).transpose(1, 0, 2)
    for c in "12":
        t = np.zeros((2, 64, 2), f)
        t[:, :C2, 0], t[:, :C2, 1] = v["L0_tok_s" + c], v["L0_tok_b" + c]
        d["sb" + c] = t.reshape(128, 2)
    for name, m, mp in (("w2", C2, 64), ("w3", E, E)):
        t = np.zeros((2, 64, 2, mp), f)
        t[:, :C2, :, :m] = v["L0_tok_" + name].transpose(3, 1, 2, 0)
        d[name] = t.reshape(128, 2, mp)
    for a, (w, b) in enumerate(((v["L0_attn_W_attn"], v["L0_attn_b_attn"]),
                                (v["L0_ffn_qkv_w"].T, v["L0_ffn_qkv_b"]))):
        t = np.zeros((97, 2, 3 * E), f)
        t[:96] = w.reshape(2, 96, 3 * E).transpose(1, 0, 2)
        t[96, 1] = b
        d[f"wa{a}"] = t
    d["wp0"] = np.concatenate([v["L0_attn_W_proj"], v["L0_attn_b_proj"][None]])
    d["wp1"] = np.concatenate([v["L0_ffn_proj_w"].T, v["L0_ffn_proj_b"][None]])
    d["lnwb"] = np.stack([v["L0_ffn_" + n].reshape(2, 96).T for n in ("norm1_w", "norm1_b", "norm2_w", "norm2_b")], 1)
    d["wg"] = v["L0_ffn_w_gate"].reshape(2, 96, NEXP).transpose(1, 0, 2)
    d["b1"] = v["L0_ffn_b1"].reshape(NEXP * HC, 128).T
    d["W1"] = v["L0_ffn_W1"].reshape(NEXP, 2, 96, HID).transpose(0, 2, 1, 3).reshape(NEXP * 96, 2 * HID)
    d["W1"] = d["W1"].reshape(NEXP, 96, 2 * HID)
    d["W2"] = v["L0_ffn_W2"].reshape(NEXP, HC, 128, E).transpose(0, 2, 1, 3).reshape(NEXP, 128, HC * E)
    for n in ("cls_tok", "L0_tok_s3", "L0_tok_b3", "L0_ffn_b2"):
        d[n] = v[n]
    return d


def kernel(**inputs):
    import numpy as _np
    import concourse.bacc as _bacc
    from concourse import mybir as _mybir
    from concourse.bass_utils import run_bass_kernel_spmd as _run

    nc = _bacc.Bacc("TRN2", target_bir_lowering=False, num_devices=1)
    arrays, A = {}, {}
    every = lay_out(_np, {name: _np.asarray(a) for name, a in inputs.items()})
    every.update(shape_constants(_np))
    for name, a in every.items():
        arrays[f"in_{name}_dram"] = _np.ascontiguousarray(a)
        A[name] = nc.dram_tensor(f"in_{name}_dram", a.shape, _mybir.dt.from_np(a.dtype), kind="ExternalInput").ap()
    out = nc.dram_tensor("out_0_dram", (NIMG, NTOK, E), _mybir.dt.float32, kind="ExternalOutput").ap()
    vit_tower(nc, A, out)
    r = _run(nc, [arrays], core_ids=[0])
    return r.results[0]["out_0_dram"]
```

```python
from contextlib import ExitStack

import concourse.bass as bass
from concourse import mybir

F32 = mybir.dt.float32
F32R = mybir.dt.float32r
U32 = mybir.dt.uint32
I32 = mybir.dt.int32
BF16 = mybir.dt.bfloat16
ACT = mybir.ActivationFunctionType
ALU = mybir.AluOpType
AX_X = mybir.AxisListType.X

NIMG, CIN, HW = 128, 3, 84
G7, RH = 7, 12
NREG = G7 * G7
C1, C2, E = 12, 48, 192
RG = 10
NGRP = 5
BI = 16
NBLK = NIMG // BI
SBI = 2 * BI
NSB = NIMG // SBI
SPS = 2 * NGRP
LANES = RG * C1
WIN = RH + 2
LINE = BI * WIN
GRPR = [RG] * (NGRP - 1) + [NREG - RG * (NGRP - 1)]
CH = 2 * BI * RH
NTOK = 26
HEADS, HD = 12, 16
NEXP, HID = 8, 768
HC = HID // 128
EPS = 1e-5
NITS = NIMG // BI
SBANK = (2, 3, 5, 6)
TOPK = 2
SLOTS = TOPK * NIMG * NTOK
ET = 256
ECAP = NIMG * NTOK + ET
TILES = (SLOTS + NEXP * (ET - 1)) // ET
MAXT = NIMG * NTOK // ET
R_BASE = 0
R_STEP = R_BASE + NEXP
R_TILE = R_STEP + MAXT
R_TRI = R_TILE + TILES
R_ID = R_TRI + NEXP * NEXP
R_FILL = R_ID + NTOK
R_ALL = R_FILL + 2
DBANK = (3, 6)
PARTS = ((0, 12), (12, 14))
CMB = [(0, 7), (7, 7), (14, 6), (20, 6)]


def bc(ap, dim, n):
    a = ap.unsqueeze(dim)
    shape = list(a.shape)
    shape[dim] = n
    return a.broadcast_to(shape)


CPS = [-(-r // 3) for r in GRPR]
CPB = sum(CPS) + 2


def at(table, t):
    return table[0:1, t:t + 1] if isinstance(t, int) else table[0:1, bass.ds(t, 1)]


def run_tiles(eng, step):
    for v in range(3):
        step(0, v)
    whole = (TILES - 3) // 4
    with eng.Fori(0, whole) as i:
        for v in range(3, 7):
            step(i, v)
    for v in range(4 * whole + 3, TILES + 2):
        step(0, v)


def static_last(t):
    return isinstance(t, int) and t == NITS - 2


def inside(i, v):
    return not isinstance(i, int) or v < TILES


def started(i, v):
    return not isinstance(i, int) or v >= 0


def conv1_chunk(i, k, c):
    return 2 * CPB * i + CPB * (k // NGRP) + sum(CPS[:k % NGRP]) + c


def conv2_chunk(i, b, part):
    return 2 * CPB * i + CPB * b + CPB - 2 + part


def vit_tower(nc, A, out):
    def all_patches(i, k, u):
        full, part = (sum(32 * GRPR[t % NGRP] for t in range(m) if t % 2 == u) for m in (SPS, k))
        return full * i + part + 1

    with ExitStack() as ctx:
        def sb(name, shape, dt=F32, to=ctx):
            return to.enter_context(nc.sbuf_tensor(name, shape, dt))

        def sem(name):
            return ctx.enter_context(nc.semaphore(name))

        ident = sb("ident", [128, 128])
        regmask = sb("regmask", [LANES, 2 * RG])
        headmask = sb("headmask", [96, 6])
        vmask = sb("vmask", [104, E])
        causal = sb("causal", [128, NTOK])
        cos = sb("cos", [96, NTOK])
        sin = sb("sin", [96, NTOK])
        iota8 = sb("iota8", [128, NEXP])
        sb0 = sb("sb0", [LANES, 2])
        sb1 = sb("sb1", [128, 2])
        sb2 = sb("sb2", [128, 2])
        lnwb = sb("lnwb", [96, 4, 2])
        wg = sb("wg", [96, 2, NEXP])
        b1t = sb("b1t", [128, NEXP * HC])
        route = sb("route", [128, R_ALL])
        upper = sb("upper", [128, 128], BF16)
        ones = sb("ones", [128, 128], BF16)
        g12 = sb("g12", [128, TOPK, NTOK])
        tok = ExitStack()
        w3 = sb("w3", [128, 2, E], to=tok)
        s3row = sb("s3row", [128, E], to=tok)
        b3row = sb("b3row", [128, E], to=tok)
        wa = [sb(f"wa{a}", [128, 2, 3 * E], to=tok) for a in range(2)]
        wrot = sb("wrot", [128, 2, 2 * E], to=tok)
        wp0 = [sb(f"wp0_{a}", [128, E], to=tok) for a in range(2)]
        wp1 = [sb(f"wp1_{a}", [65, E], to=tok) for a in range(2)]

        conv = ExitStack()
        h2 = sb("h2", [128, 50, NIMG], to=conv)
        w0rep = sb("w0rep", [LANES, 3, C1], to=conv)
        w0h = sb("w0h", [LANES, 3, LANES], F32R, to=conv)
        w0l = sb("w0l", [LANES, 3, LANES], F32R, to=conv)
        wpwh = sb("wpwh", [LANES, NGRP, LANES], F32R, to=conv)
        wpwl = sb("wpwl", [LANES, NGRP, LANES], F32R, to=conv)
        wdw = sb("wdw", [LANES, NGRP, 9], to=conv)
        sbdw = sb("sbdw", [LANES, 2, NGRP], to=conv)
        pwrep = sb("pwrep", [LANES, NGRP, C1], to=conv)
        spwrep = sb("spwrep", [LANES, NGRP, C1], to=conv)
        bpw = sb("bpw", [LANES, NGRP], to=conv)
        w1 = sb("w1", [96, 2, 64], to=conv)
        w2 = sb("w2", [128, 2, 64], to=conv)
        xin = sb("xin", [LANES, RH, BI, WIN], to=conv)
        xh = sb("xh", [LANES, RH, BI, WIN], F32R, to=conv)
        xl = sb("xl", [LANES, RH, BI, WIN], F32R, to=conv)
        dh = sb("dh", [LANES, RH, BI * RH], F32R, to=conv)
        dl = sb("dl", [LANES, RH, BI * RH], F32R, to=conv)
        g0 = [sb(f"g0_{u}", [LANES, WIN, BI, WIN], to=conv) for u in range(2)]
        acc = [sb(f"acc{u}", [LANES, RH, BI * RH], to=conv) for u in range(2)]
        g3 = sb("g3", [LANES, 16, 9 * BI], to=conv)
        patches = [sb(f"patches{u}", [96, 2, RG, 9 * BI], to=conv) for u in range(2)]
        whole = ExitStack()
        w0 = sb("w0", [LANES, 3, LANES], to=whole)
        wpw = sb("wpw", [LANES, NGRP, LANES], to=whole)
        whole.close()
        h1 = sb("h1", [128, 21 * 21 * BI], to=conv)
        upper_f = sb("upper_f", [128, 128], to=conv)
        conv.close()

        H = ctx.enter_context(nc.sbuf_tensor("H", [128, NTOK, E], F32, side="right"))
        att = tok
        ot0 = sb("ot0", [128, NTOK, NIMG], to=att)
        ot1 = sb("ot1", [65, NTOK, NIMG], to=att)
        vrep = [sb(f"vrep{u}", [104, BI, E], to=att) for u in range(2)]
        qkT = [sb(f"qkT{u}", [96, 4, BI, NTOK], to=att) for u in range(2)]
        rope = [sb(f"rope{u}", [96, 2, BI, NTOK], to=att) for u in range(2)]
        NT = sb("NT", [128, 2, NTOK, NIMG], to=att)
        X = sb("X", [128, NTOK, E], to=att)
        XS = sb("XS", [128, NTOK, E + 1], to=att)
        N = XS[:, :, 0:E]
        V = N
        stats = sb("stats", [128, NTOK, 6], to=att)
        mv = sb("mv", [128, NTOK, 2], to=att)
        rstd = sb("rstd", [128, NTOK], to=att)
        small = ExitStack()
        kbd = [sb(f"kbd{u}", [96, 2, 4, 6 * NTOK], to=small) for u in range(2)]
        P = [sb(f"P{v}", [128, HEADS, NTOK], to=small) for v in range(4)]
        PT = [sb(f"PT{u}", [104, 3, 128], to=small) for u in range(2)]
        vbd = [sb(f"vbd{u}", [104, 4, E], to=small) for u in range(2)]
        smax = sb("smax", [128, HEADS], to=small)
        ssum = sb("ssum", [128, HEADS], to=small)
        srec = sb("srec", [128, HEADS], to=small)
        small.close()
        logits = sb("logits", [128, NTOK, NEXP], to=att)
        top = sb("top", [128, NTOK, 8], to=att)
        topi = sb("topi", [128, NTOK, 8], U32, to=att)
        topf = sb("topf", [128, NTOK, 2], to=att)
        gg = sb("gg", [128, 2, NTOK], to=att)
        oneh = [sb(f"oneh{j}", [128, NTOK, NEXP], to=att) for j in range(TOPK)]
        chosen = sb("chosen", [128, NTOK + 1, NEXP], BF16, to=att)
        rank = sb("rank", [128, NTOK + 1, NEXP], to=att)
        posf = sb("posf", [128, TOPK, NTOK], to=att)
        pos = sb("pos", [128, TOPK, NTOK], I32, to=att)
        id2 = sb("id2", [128, NTOK], I32, to=att)
        filler = sb("filler", [128, 2, E + 1], to=att)
        full = sb("full", [128, NEXP, MAXT], to=att)
        ntile = sb("ntile", [128, NEXP], to=att)
        square = sb("square", [128, NEXP, NEXP], to=att)
        tend = sb("tend", [128, NEXP], to=att)
        lastt = sb("lastt", [128, 1], to=att)
        tilek = sb("tilek", [128, TILES], to=att)
        past = sb("past", [128, TILES, NEXP], to=att)
        tilef = sb("tilef", [128, 2, TILES], to=att)
        att.close()
        tile_e = sb("tile_e", [128, TILES], I32)
        tile_r = sb("tile_r", [128, TILES], I32)
        fill_r = sb("fill_r", [128, NEXP], I32)
        back = ExitStack()
        Y = sb("Y", [128, NTOK, TOPK, E], to=back)
        back.close()
        W1 = sb("W1", [96, NEXP, 2 * HID])
        W2 = sb("W2", [128, NEXP, HC * E])
        xt = [sb(f"xt{u}", [128, 2, E + 1]) for u in range(2)]
        dest = [sb(f"dest{v}", [128, 2], I32) for v in range(4)]
        xf = [sb(f"xf{u}", [96, 2, ET]) for u in range(2)]
        xfh = [sb(f"xfh{u}", [96, 2, ET], F32R) for u in range(2)]
        xfl = [sb(f"xfl{u}", [96, 2, ET], F32R) for u in range(2)]
        w1h = [sb(f"w1h{u}", [96, 2, HID], F32R) for u in range(2)]
        w1l = [sb(f"w1l{u}", [96, 2, HID], F32R) for u in range(2)]
        w2s = [sb(f"w2s{u}", [128, HC, 2, E], F32R) for u in range(2)]
        b1e = [sb(f"b1e{u}", [128, HC]) for u in range(2)]
        b2e = [sb(f"b2e{u}", [128, E]) for u in range(2)]
        hf = sb("hf", [128, 3, 2 * ET])
        hh = [sb(f"hh{u}", [128, 3, 2 * ET], F32R) for u in range(2)]
        hl = [sb(f"hl{u}", [128, 3, 2 * ET], F32R) for u in range(2)]
        yt = [sb(f"yt{u}", [128, 2, E]) for u in range(2)]

        all_values = nc.dram_tensor("all_values", (NIMG, NTOK, E), F32).ap()
        sorted_x = nc.dram_tensor("sorted_x", (NEXP * ECAP, E + 1), F32).ap()
        results = nc.dram_tensor("results", (SLOTS + 2 * 128, E), F32).ap()

        ps = ctx.enter_context(nc.psum_tensor("ps", [128, 8, 512], F32))

        first_loaded = sem("first_loaded")
        w_loaded = sem("w_loaded")
        cleared = sem("cleared")
        w_built = sem("w_built")
        xin_loaded = sem("xin_loaded")
        conv0_done = sem("conv0_done")
        gelu0_done = sem("gelu0_done")
        xh_done = sem("xh_done")
        xl_done = sem("xl_done")
        dh_done = sem("dh_done")
        dl_done = sem("dl_done")
        dw_done = sem("dw_done")
        dwtap = sem("dwtap")
        gelud_done = sem("gelud_done")
        pw_done = sem("pw_done")
        gelu3_done = sem("gelu3_done")
        p_loaded = [sem(f"p_loaded{u}") for u in range(2)]
        c12_done = sem("c12_done")
        c12_out = sem("c12_out")
        conv1_steps = sem("conv1_steps")
        h1_done = sem("h1_done")
        h1_shifted = sem("h1_shifted")
        conv2_blocks = sem("conv2_blocks")

        block = ctx.enter_context(nc.Block())

        loads = []

        def load(dst, src):
            loads.append((dst, src))

        for dst, name in ((regmask, "k_regmask"), (w0rep, "w0"), (sb0, "sb0"), (wdw, "wdw"), (sbdw, "sbdw"),
                          (pwrep, "wpw"), (spwrep, "spw"), (bpw, "bpw")):
            load(dst[:], A[name])
        NFIRST = len(loads)
        for dst, name in ((ident, "k_ident"), (headmask, "k_headmask"), (vmask, "k_vmask"),
                          (causal, "k_causal"), (cos, "k_cos"), (sin, "k_sin"), (iota8, "k_iota"),
                          (w1, "w1"), (sb1, "sb1"), (w2, "w2"), (sb2, "sb2"), (w3, "w3"),
                          (wa[0], "wa0"), (wa[1], "wa1"), (lnwb, "lnwb"), (wg, "wg"), (route, "k_route"),
                          (b1t, "b1")):
            load(dst[:], A[name])
        load(upper_f[:], A["k_upper"])
        for a in range(2):
            load(wp0[a][:], A[f"wp{a}"][0:128])
            load(wp1[a][:], A[f"wp{a}"][128:193])
        load(s3row[:], A["L0_tok_s3"].unsqueeze(0).broadcast_to([128, E]))
        load(b3row[:], A["L0_tok_b3"].unsqueeze(0).broadcast_to([128, E]))
        ALL_LOADED = 16 * (len(loads) - NFIRST)

        conv3_mm = sem("conv3_mm")
        h_ready = sem("h_ready")
        cls_loaded = sem("cls_loaded")
        chain = sem("chain")
        var_ready = sem("var_ready")
        std_ready = sem("std_ready")
        ln_done = sem("ln_done")
        tr_mm = sem("tr_mm")
        tr_out = sem("tr_out")
        rows_cleared = sem("rows_cleared")
        ones_set = sem("ones_set")
        val_mm = sem("val_mm")
        val_out = sem("val_out")
        val_stored = sem("val_stored")
        vrep_loaded = [sem(f"vrep_loaded{u}") for u in range(2)]
        qk_mm = sem("qk_mm")
        qk_out = sem("qk_out")
        qk_ready = sem("qk_ready")
        kbd_ready = sem("kbd_ready")
        s_mm = sem("s_mm")
        s_out = sem("s_out")
        s_shift = sem("s_shift")
        sm = sem("softmax_stat")
        s_exp = sem("s_exp")
        p_ready = sem("p_ready")
        pt_mm = sem("pt_mm")
        pt_out = sem("pt_out")
        v_out = sem("v_out")
        o_mm = sem("o_mm")
        o_out = sem("o_out")
        proj_mm = sem("proj_mm")
        proj_out = sem("proj_out")
        ps_cleared = sem("ps_cleared")
        lg_mm = sem("lg_mm")
        e_ready = sem("e_ready")
        e_exp = sem("e_exp")
        chosen_ready = sem("chosen_ready")
        rank_mm = sem("rank_mm")
        ids_ready = sem("ids_ready")
        pos_ready = sem("pos_ready")
        sorted_x_in = sem("sorted_x_in")
        tiles_ready = sem("tiles_ready")
        filled = sem("filled")
        x_added = sem("x_added")
        w_resident = sem("w_resident")
        xt_loaded = [sem(f"xt_loaded{u}") for u in range(2)]
        b2_loaded = [sem(f"b2_loaded{u}") for u in range(2)]
        xT_mm = sem("xT_mm")
        x_scaled = sem("x_scaled")
        xf_done = sem("xf_done")
        x_done = sem("x_done")
        w1h_done = sem("w1h_done")
        w1l_done = sem("w1l_done")
        w1_turn = sem("w1_turn")
        dest_kept = sem("dest_kept")
        w2_steps = sem("w2_steps")
        w2_done = sem("w2_done")
        b1_here = sem("b1_here")
        up_mm = sem("up_mm")
        gelu_done = sem("gelu_done")
        h_steps = sem("h_steps")
        h_done = sem("h_done")
        down_mm = sem("down_mm")
        y_steps = sem("y_steps")
        y_ready = sem("y_ready")
        y_turn = sem("y_turn")
        y_out = sem("y_out")
        y_landed = sem("y_landed")
        y_back = [sem(f"y_back{c}") for c in range(len(CMB))]
        combined = sem("combined")
        stored = sem("stored")

        pairs = [(s, min(2, NTOK - s)) for s in range(0, NTOK, 2)]
        quads = [(h, s, min(4, NTOK - s)) for s in range(0, NTOK, 4) for h in range(2)]
        NQ = len(quads)

        @block.sync
        def _(sp):
            for u in range(2):
                sp.sem_inc(p_loaded[u], 1)

            def load_xin(i, k):
                g, b = k % NGRP, k // NGRP
                for dy in range(3):
                    sp.dma_start(xin[30 * dy:30 * dy + 3 * GRPR[g]].rearrange("p y i x -> p (y i x)"),
                                 A["windows"][bass.ds(2 * i + b, 1), 3 * RG * g:3 * (RG * g + GRPR[g]),
                                              dy * LINE:(dy + RH) * LINE].rearrange("b r w -> (b r) w")
                                 ).then_inc(xin_loaded, 16)

            def shift_h1(i, b):
                sp.wait_ge(h1_done, 2 * i + b + 1)
                sp.dma_start(h1[64:128, 0:(21 * 21 - 1) * BI], h1[0:64, BI:21 * 21 * BI]
                             ).then_inc(h1_shifted, 16)

            def step(i, k):
                if k % NGRP == 1 and k > NGRP:
                    shift_h1(i, k // NGRP - 1)
                if not (isinstance(i, int) and SPS * i + k + 3 >= SPS * NSB):
                    sp.wait_ge(xl_done, 3 * (SPS * i + k + 3))
                    load_xin(i, k + 3)
                sp.wait_ge(gelu3_done, 3 * (SPS * i + k + 1) + 6)
                sp.wait_ge(conv1_steps, SPS * i + k + 1)
                for r in range(GRPR[k % NGRP]):
                    for h in range(2):
                        sp.dma_start(patches[k % 2][:, h, r, :], g3[r * C1 + 6 * h:r * C1 + 6 * h + 6, :, :]
                                     ).then_inc(p_loaded[k % 2], 16)

            for dst, src in loads[:NFIRST]:
                sp.dma_start(dst, src).then_inc(first_loaded, 16)
            sp.wait_ge(cleared, 1)
            load_xin(0, 0)
            for dst, src in loads[NFIRST:]:
                sp.dma_start(dst, src).then_inc(w_loaded, 16)
            for k in range(1, 3):
                sp.wait_ge(xl_done, 3 * k)
                load_xin(0, k)
            for k in range(2):
                step(0, k)
            with sp.Fori(0, NSB - 1) as i:
                for k in range(2, SPS + 2):
                    step(i, k)
            for k in range(2, SPS):
                step(NSB - 1, k)
            shift_h1(NSB - 1, 1)

            sp.wait_ge(conv3_mm, 1)
            sp.dma_start(H[:, 0, :], A["cls_tok"].rearrange("a b d -> (a b) d").broadcast_to([128, E])
                         ).then_inc(cls_loaded, 16)

            for a in range(2):
                def spread(i, u):
                    t = 2 * i + u
                    for c in range(4):
                        sp.dma_start(vrep[u][c * NTOK:(c + 1) * NTOK],
                                     all_values[bass.ds(t * BI, BI)].rearrange("i s e -> s i e")
                                     ).then_inc(vrep_loaded[u], 16)

                for n, (s, m) in enumerate(pairs):
                    sp.wait_ge(val_out, len(pairs) * a + n + 1)
                    sp.dma_start(all_values[:, s:s + m, :], V[:, s:s + m, :]).then_inc(val_stored, 16)
                sp.wait_ge(val_stored, 16 * len(pairs) * (a + 1))
                for u in range(2):
                    spread(0, u)
                with sp.Fori(1, NITS // 2) as i:
                    for u in range(2):
                        sp.wait_ge(v_out, 4 * (2 * i + u - 1 + NITS * a))
                        spread(i, u)

            sp.wait_ge(proj_out, 2 * len(pairs))
            for e in range(NEXP):
                sp.dma_start(W1[:, e, :], A["W1"][e]).then_inc(w_resident, 16)
                sp.dma_start(W2[:, e, :], A["W2"][e]).then_inc(w_resident, 16)

            sp.wait_ge(tiles_ready, 1)
            for e in range(NEXP):
                r = sp.value_load(fill_r[0:1, e:e + 1], min_val=0, max_val=NEXP * ECAP - ET)
                sp.dma_start(sorted_x[bass.ds(r, ET), :].rearrange("(a p) c -> p a c", p=128), filler[:]
                             ).then_inc(filled, 16)

            def load_rows(i, v):
                t = 4 * i + v
                r = sp.value_load(at(tile_r, t), min_val=0, max_val=NEXP * ECAP - ET)
                src = sorted_x[bass.ds(r, ET), :].rearrange("(a p) c -> p a c", p=128)
                if v >= 2:
                    sp.wait_ge(xT_mm, t - 1)
                    sp.wait_ge(dest_kept, t - 1)
                sp.dma_start(xt[v % 2][:], src).then_inc(xt_loaded[v % 2], 16)

            def load_b2(i, v):
                t = 4 * i + v
                e = sp.value_load(at(tile_e, t), min_val=0, max_val=NEXP - 1)
                src = A["L0_ffn_b2"][bass.ds(e, 1), :].broadcast_to([128, E])
                if v >= 2:
                    sp.wait_ge(y_ready, t - 1 + 2)
                sp.dma_start(b2e[v % 2][:], src).then_inc(b2_loaded[v % 2], 16)

            sp.wait_ge(sorted_x_in, 16 * TOPK * NTOK)
            sp.wait_ge(filled, 16 * NEXP)
            sp.wait_ge(x_added, 1)
            load_rows(0, 0)
            load_rows(0, 1)
            run_tiles(sp, lambda i, v: (load_rows(i, v + 2) if inside(i, v + 2) else None,
                                        load_b2(i, v) if inside(i, v) else None))

            sp.wait_ge(y_out, 32 * TILES)
            sp.wait_ge(up_mm, 3 * TILES)
            by_token = results[0:SLOTS].rearrange("(b t j) e -> b t j e", b=NIMG, j=TOPK)
            for c, (s, m) in enumerate(CMB):
                sp.dma_start(Y[:, s:s + m], by_token[:, s:s + m]).then_inc(y_back[c], 16)
            for c, (s, m) in enumerate(CMB):
                sp.wait_ge(combined, c + 1)
                sp.dma_start(out[:, s:s + m, :], H[:, s:s + m, :]).then_inc(stored, 16)
            sp.wait_ge(stored, 16 * len(CMB))

        @block.gpsimd
        def _(pool):
            pool.memset(xin[:], 0.0).then_inc(cleared, 1)
            pool.memset(g0[0][:], 0.0)
            pool.memset(g0[1][:], 0.0).then_inc(cleared, 1)
            pool.sem_inc(dl_done, 6)

            def low_of_input(i, k):
                n = SPS * i + k
                pool.wait_ge(xh_done, n + 1)
                for j in range(3):
                    y = slice(4 * j, 4 * j + 4)
                    pool.tensor_tensor(xl[:, y], xin[:, y], xh[:, y].bitcast(F32), ALU.subtract).then_inc(xl_done, 1)

            def low_of_depthwise(i, k):
                n = SPS * i + k
                for j in range(3):
                    pool.wait_ge(dh_done, 3 * n + j + 1)
                    y = slice(4 * j, 4 * j + 4)
                    pool.tensor_tensor(dl[:, y], acc[k % 2][:, y], dh[:, y].bitcast(F32), ALU.subtract
                                       ).then_inc(dl_done, 1)

            def step(i, k):
                low_of_depthwise(i, k)
                if not (isinstance(i, int) and SPS * i + k + 2 >= SPS * NSB):
                    low_of_input(i, k + 2)

            for k in range(2):
                low_of_input(0, k)
            for k in range(2):
                step(0, k)
            with pool.Fori(0, NSB - 1) as i:
                for k in range(2, SPS + 2):
                    step(i, k)
            for k in range(2, SPS):
                step(NSB - 1, k)

            pool.wait_ge(conv3_mm, len(pairs))
            pool.memset(NT[96:128, :, :, :], 0.0).then_inc(rows_cleared, 1)
            pool.wait_ge(rows_cleared, 1)
            pool.memset(NT[96:97, :, :, :], 1.0)
            pool.memset(ot1[64:65, :, :], 1.0).then_inc(ones_set, 1)
            for a in range(2):
                def keys(t, u, sub):
                    n = 4 * (t + NITS * a) + sub
                    if sub == 0:
                        pool.wait_ge(qk_ready, 4 * (t + NITS * a + 1))
                    pool.wait_ge(s_mm, n + 1)
                    for h in range(2):
                        for j in range(4):
                            last = pool.tensor_tensor(
                                kbd[sub % 2][:, h, j, :].rearrange("p (g k) -> p g k", g=6),
                                bc(qkT[u][:, 2 + h, 4 * sub + j, :], 1, 6),
                                bc(headmask[:], 2, NTOK), ALU.mult)
                    last.then_inc(kbd_ready, 1)

                with pool.Fori(0, NITS // 2) as i:
                    for u in range(2):
                        for sub in range(4):
                            keys(2 * i + u, u, sub)

            for k, (s0, m) in enumerate(PARTS):
                for j in range(TOPK):
                    pool.wait_ge(ids_ready, k + j + 1)
                    pool.wait_ge(pos_ready, TOPK * k + j + 1)
                    for s in range(s0, s0 + m):
                        pool.indirect_dma_start(sorted_x[:], bass.IndirectOffsetOnAxis(ap=pos[:, j, s:s + 1], axis=0),
                                                XS[:, s, :], None).then_inc(sorted_x_in, 16)
                    if j == 0:
                        pool.wait_ge(sorted_x_in, 16 * (TOPK * s0 + m))
                        pool.tensor_copy(XS.bitcast(I32)[:, s0:s0 + m, E:E + 1], id2[:, s0:s0 + m].unsqueeze(2)
                                         ).then_inc(ids_ready, 1)

            def w1_low(i, v):
                t = 4 * i + v
                e = pool.value_load(at(tile_e, t), min_val=0, max_val=NEXP - 1)
                for h in range(2):
                    pool.wait_ge(w1h_done, 2 * t + h + 1)
                    pool.sem_inc(w1_turn, 1)
                    pool.tensor_tensor(w1l[v % 2][:, h, :], W1[:, bass.ds(e, 1), h * HID:(h + 1) * HID].rearrange("p a n -> p (a n)"),
                                       w1h[v % 2][:, h, :].bitcast(F32), ALU.subtract).then_inc(w1l_done, 1)

            def scatter(i, v):
                t = 4 * i + v
                pool.wait_ge(y_ready, t + 1 + 2)
                pool.sem_inc(y_turn, 1)
                if v:
                    pool.wait_ge(y_out, 32 * t)
                pool.sem_inc(y_landed, 1)
                for a in range(2):
                    pool.indirect_dma_start(results[:], bass.IndirectOffsetOnAxis(ap=dest[v % 4][:, a:a + 1], axis=0),
                                            yt[v % 2][:, a, :], None).then_inc(y_out, 16)

            pool.wait_ge(w_resident, 32 * NEXP)
            pool.wait_ge(sorted_x_in, 16 * TOPK * NTOK)
            pool.wait_ge(filled, 16 * NEXP)
            pool.wait_ge(x_added, 1)
            pool.wait_ge(tiles_ready, 1)
            w1_low(0, 0)
            run_tiles(pool, lambda i, v: (w1_low(i, v + 1) if inside(i, v + 1) else None,
                                          scatter(i, v - 2) if started(i, v - 2) else None))

        @block.tensor
        def _(pe):
            pe.wait_ge(w_built, 1)
            pe.sem_inc(conv1_steps, 2)
            pe.sem_inc(conv2_blocks, 1)

            def conv0(i, k, first):
                n = SPS * i + k
                for j in range(3):
                    if first == 1:
                        pe.wait_ge(gelu0_done, j + 1)
                    elif first is None:
                        pe.wait_ge(gelu3_done, 3 * n + j + 1)
                    pe.wait_ge(xl_done, 3 * n + j + 1)
                    for c in range(2):
                        y = 4 * j + 2 * c
                        for t, (w, x, dx) in enumerate([(w, x, dx) for w, x in ((w0h, xh), (w0l, xh), (w0h, xl))
                                                        for dx in range(3)]):
                            last = pe.matmul(ps[0:LANES, 2 * j + c, 0:CH], w[:, dx, :],
                                             x[:, y:y + 2, :, dx:dx + RH], start=(t == 0), stop=(t == 8))
                    last.then_inc(conv0_done, 1)

            def pointwise(i, k, last_step):
                n = SPS * i + k
                u, g = k % 2, k % NGRP
                for j in range(3):
                    if last_step:
                        pe.wait_ge(gelu3_done, 3 * (n - 1) + j + 1 + 6)
                    else:
                        pe.wait_ge(gelu0_done, 3 * (n + 1) + j + 1)
                    pe.wait_ge(dl_done, 3 * n + j + 1 + 6)
                    for c in range(2):
                        y = 4 * j + 2 * c
                        for t, (w, x) in enumerate(((wpwh, dh), (wpwl, dh), (wpwh, dl))):
                            pe.matmul(ps[0:LANES, 2 * j + c, 0:CH], w[:, g, :], x[:, y:y + 2, :],
                                      start=(t == 0), stop=False)
                        last = pe.matmul(ps[0:LANES, 2 * j + c, 0:CH], ident[0:LANES, 0:LANES],
                                         g0[u][:, y + 1:y + 3, :, 1:RH + 1], start=False, stop=True)
                    last.then_inc(pw_done, 1)

            def conv1(i, k):
                g = k % NGRP
                pe.wait_ge(p_loaded[k % 2], all_patches(i, k + 1, k % 2))
                pe.wait_ge(c12_out, conv1_chunk(i, k, 0) + 1)
                for c in range(CPS[g]):
                    n = min(3, GRPR[g] - 3 * c)
                    lanes = slice(64 * (c // 2), 64 * (c // 2) + 64)
                    for h in range(2):
                        last = pe.matmul(ps[lanes, 6 + c % 2, 0:n * 9 * BI], w1[:, h, :],
                                         patches[k % 2][:, h, 3 * c:3 * c + n, :], start=(h == 0), stop=(h == 1))
                    last.then_inc(c12_done, 1)
                pe.wait_ge(c12_done, conv1_chunk(i, k, c) + 1)
                pe.sem_inc(conv1_steps, 1)

            def conv2(i, b):
                pe.wait_ge(h1_shifted, 16 * (2 * i + b + 1))
                pe.wait_ge(c12_out, conv2_chunk(i, b, 0) + 1)
                hv = h1[:].rearrange("p (y x i) -> p y x i", y=21, x=21)
                for part in range(2):
                    for odd in range(2):
                        for dy in range(2):
                            y0 = 10 * part + dy
                            last = pe.matmul(ps[64 * odd:64 * odd + 64, 6 + part, 0:25 * BI], w2[:, dy, :],
                                             hv[:, y0:y0 + 9:2, 2 * odd:2 * odd + 17:4, :],
                                             start=(dy == 0), stop=(dy == 1))
                    last.then_inc(c12_done, 1)
                pe.wait_ge(c12_done, conv2_chunk(i, b, 1) + 1)
                pe.sem_inc(conv2_blocks, 1)

            def step(i, k):
                static = isinstance(i, int)
                pointwise(i, k, static and SPS * i + k == SPS * NSB - 1)
                if not (static and SPS * i + k + 2 >= SPS * NSB):
                    conv0(i, k + 2, None)
                if k % NGRP == 1 and k > NGRP:
                    conv2(i, k // NGRP - 1)
                if not (static and SPS * i + k == 0):
                    conv1(i, k - 1)

            conv0(0, 0, 0)
            conv0(0, 1, 1)
            pe.wait_ge(w_built, 2)
            for k in range(2):
                step(0, k)
            with pe.Fori(0, NSB - 1) as i:
                for k in range(2, SPS + 2):
                    step(i, k)
            for k in range(2, SPS):
                step(NSB - 1, k)
            conv1(NSB - 1, SPS - 1)
            conv2(NSB - 1, 1)

            pe.wait_ge(c12_out, NBLK * CPB + 1)
            for n, (s, m) in enumerate(pairs):
                if n >= 4:
                    pe.wait_ge(h_ready, n - 3)
                for t in range(max(s, 1), s + m):
                    y, x = divmod(t - 1, 5)
                    for dy in range(2):
                        last = pe.matmul(ps[:, n % 4, (t - s) * E:(t - s + 1) * E], h2[:, (2 * y + dy) * 5 + x, :],
                                         w3[:, dy, :], start=(dy == 0), stop=(dy == 1))
                last.then_inc(conv3_mm, 1)

            def turn_tokens(a):
                for n, (h, s, m) in enumerate(quads):
                    pe.wait_ge(ln_done, NTOK * (0, 2, 3)[a] + s + m)
                    if a or n >= 4:
                        pe.wait_ge(tr_out, NQ * a + n - 3)
                    for t in range(m):
                        last = pe.transpose(ps[0:96, 4 + n % 4, t * 128:(t + 1) * 128],
                                            N[:, s + t, 96 * h:96 * h + 96], ident[:])
                    last.then_inc(tr_mm, 1)
                    if a == 2 and h == 1 and s:
                        logits_of(s - 4, 4)
                        if s == PARTS[0][1] + 4:
                            ranks(0)

            def logits_of(s0, m):
                pe.wait_ge(tr_out, 2 * NQ + 2 * (s0 // 4) + 2)
                for s in range(s0, s0 + m):
                    k = s >= PARTS[1][0]
                    for h in range(2):
                        last = pe.matmul(ps[:, k, s * NEXP:(s + 1) * NEXP], NT[0:96, h, s, :], wg[:, h, :],
                                         start=(h == 0), stop=(h == 1))
                if s0 + m in (PARTS[0][1], NTOK):
                    last.then_inc(lg_mm, 1)

            def ranks(k):
                s0, m = PARTS[k]
                n = m + k
                bank = ps[:, 2 + k, 0:n * NEXP].rearrange("p (t e) -> p t e", e=NEXP)
                pe.wait_ge(chosen_ready, k + 1)
                pe.matmul(bank, upper[:], chosen[:, s0:s0 + n, :], start=True, stop=False)
                for s in range(s0 + n - 1):
                    t = max(s + 1 - s0, 0)
                    last = pe.matmul(bank[:, t:n, :], ones[:], bc(chosen[:, s, :], 1, n - t), start=False,
                                     stop=(s == s0 + n - 2))
                last.then_inc(rank_mm, 1)

            def attention(a):

                def qk(t, m):
                    for rot in range(2 if a == 0 else 1):
                        q = 8 * t + 2 * m + rot if a == 0 else 8 * NITS + 4 * t + m
                        w = wrot if rot else wa[a]
                        pe.wait_ge(qk_out, q + 1)
                        for h in range(2):
                            last = pe.matmul(ps[0:96, (2 * m + rot if a == 0 else m) % 2, 0:NTOK * BI],
                                             w[:, h, 96 * m:96 * m + 96],
                                             NT[:, h, :, bass.ds(t * BI, BI)].rearrange("p s i -> p i s"),
                                             start=(h == 0), stop=(h == 1))
                        last.then_inc(qk_mm, 1)

                def scores(t, u, sub):
                    n = 4 * (t + NITS * a) + sub
                    pe.wait_ge(kbd_ready, n + 1)
                    pe.wait_ge(s_out, n + 1)
                    v = sub % 2
                    for j in range(4):
                        for h in range(2):
                            last = pe.matmul(ps[32 * j:32 * j + NTOK, SBANK[sub], h * 156:(h + 1) * 156],
                                             qkT[u][:, h, 4 * sub + j, :], kbd[v][:, h, j, :],
                                             start=True, stop=True)
                    last.then_inc(s_mm, 1)

                def values():
                    for n, (s, m) in enumerate(pairs):
                        if n >= 2:
                            pe.wait_ge(val_out, len(pairs) * a + n - 1)
                        for j in range(m):
                            for h in range(2):
                                last = pe.matmul(ps[:, 5 + n % 2, j * E:(j + 1) * E], NT[:, h, s + j, :],
                                                 wa[a][:, h, 2 * E:3 * E], start=(h == 0), stop=(h == 1))
                        last.then_inc(val_mm, 1)

                def turn_probs(t, sub):
                    n = 4 * (t + NITS * a) + sub
                    pe.wait_ge(p_ready, n + 1)
                    pe.wait_ge(pt_out, n + 1)
                    for c in range(3):
                        last = pe.transpose(ps[0:104, 4, c * 128:(c + 1) * 128],
                                            P[sub][:, 4 * c:4 * c + 4, :], ident[:])
                    last.then_inc(pt_mm, 1)

                def outputs(t, sub):
                    n = 4 * (t + NITS * a) + sub
                    v = sub % 2
                    pe.wait_ge(v_out, n + 1)
                    pe.wait_ge(pt_out, n + 2)
                    pe.wait_ge(o_out, n + 1)
                    for c in range(3):
                        for j in range(4):
                            last = pe.matmul(ps[64 * (c % 2):64 * (c % 2) + 64, 7,
                                                (c // 2) * 104 + j * NTOK:(c // 2) * 104 + (j + 1) * NTOK],
                                             vbd[v][:, j, 64 * c:64 * c + 64], PT[v][:, c, 32 * j:32 * j + NTOK],
                                             start=True, stop=True)
                    last.then_inc(o_mm, 1)

                def turn(t, u, final):
                    for sub in range(4):
                        turn_probs(t, sub)
                        if sub < 2:
                            scores(t, u, sub + 2)
                        elif not final:
                            scores(t + 1, 1 - u, sub - 2)
                        if sub == 0 and not final:
                            qk(t + 1, 3)
                        elif sub > 0 and not (final or static_last(t)):
                            qk(t + 2, sub - 1)
                        outputs(t, sub)

                pe.wait_ge(tr_out, NQ * (a + 1))
                pe.wait_ge(ones_set, 1)
                values()
                for m in range(7):
                    qk(m // 4, m % 4)
                scores(0, 0, 0)
                scores(0, 0, 1)
                pe.wait_ge(val_out, len(pairs) * (a + 1))
                with pe.Fori(0, NITS // 2 - 1) as i:
                    for u in range(2):
                        turn(2 * i + u, u, False)
                turn(NITS - 2, 0, False)
                turn(NITS - 1, 1, True)

                pe.wait_ge(o_out, 4 * NITS * (a + 1) + 1)
                for n, (s, m) in enumerate(pairs):
                    if a or n >= 2:
                        pe.wait_ge(proj_out, len(pairs) * a + n - 1)
                    for t in range(m):
                        o = ps[:, n % 2, t * E:(t + 1) * E]
                        pe.matmul(o, ot0[:, s + t, :], wp0[a][:], start=True, stop=False)
                        last = pe.matmul(o, ot1[:, s + t, :], wp1[a][:], start=False, stop=True)
                    last.then_inc(proj_mm, 1)

            pe.wait_ge(ps_cleared, 1)
            turn_tokens(0)
            attention(0)
            turn_tokens(1)
            attention(1)
            turn_tokens(2)

            logits_of(24, NTOK - 24)
            ranks(1)

            def turn_rows(i, v):
                t = 4 * i + v
                pe.wait_ge(xt_loaded[v % 2], 16 * (2 * i + v // 2 + 1))
                pe.wait_ge(xf_done, t + 1)
                for h in range(2):
                    for a in range(2):
                        last = pe.transpose(ps[0:96, 5, h * ET + a * 128:h * ET + (a + 1) * 128],
                                            xt[v % 2][:, a, 96 * h:96 * h + 96], ident[:])
                last.then_inc(xT_mm, 1)

            def up(i, v):
                t, u = 4 * i + v, v % 2
                pe.wait_ge(w1l_done, 2 * t + 2)
                pe.wait_ge(x_done, t + 1)
                for p in range(3):
                    pe.wait_ge(gelu_done, 3 * t + p + 1)
                    for c in range(2):
                        o = ps[:, p, c * ET:(c + 1) * ET]
                        at_c = slice((2 * p + c) * 128, (2 * p + c + 1) * 128)
                        for h in range(2):
                            pe.matmul(o, w1h[u][:, h, at_c], xfh[u][:, h, :], start=(h == 0), stop=False)
                            pe.matmul(o, w1h[u][:, h, at_c], xfl[u][:, h, :], start=False, stop=False)
                            last = pe.matmul(o, w1l[u][:, h, at_c], xfh[u][:, h, :], start=False, stop=(h == 1))
                    last.then_inc(up_mm, 1)

            def down(i, v):
                t, u = 4 * i + v, v % 2
                pe.wait_ge(w2_done, t + 1)
                pe.wait_ge(y_ready, t + 1)
                for p in range(3):
                    pe.wait_ge(h_done, 3 * t + p + 1 + 3)
                for a in range(2):
                    bank = ps[:, DBANK[u] + a, :]
                    for c in range(HC):
                        cols = slice((c % 2) * ET + a * 128, (c % 2) * ET + (a + 1) * 128)
                        hi, lo = hh[u][:, c // 2, cols], hl[u][:, c // 2, cols]
                        pe.matmul(bank[:, 0:2 * E], hi, w2s[u][:, c].rearrange("p a e -> p (a e)"), start=(c == 0), stop=False)
                        last = pe.matmul(bank[:, 0:E], lo, w2s[u][:, c, 0, :], start=False, stop=(c == HC - 1))
                last.then_inc(down_mm, 1)

            turn_rows(0, 0)
            run_tiles(pe, lambda i, v: (turn_rows(i, v + 1) if inside(i, v + 1) else None,
                                        up(i, v) if inside(i, v) else None,
                                        down(i, v - 1) if started(i, v - 1) and inside(i, v - 1) else None))

        @block.scalar
        def _(act):
            act.wait_ge(first_loaded, 16 * NFIRST)
            act.wait_ge(cleared, 2)
            act.sem_inc(gelu3_done, 6)
            act.sem_inc(c12_out, 1)
            act.sem_inc(pt_out, 1)
            act.sem_inc(o_out, 1)

            def gelu0(i, k, first):
                n = SPS * i + k
                u = k % 2
                if not first:
                    act.wait_ge(pw_done, 3 * (n - 1) + 6)
                for j in range(3):
                    act.wait_ge(conv0_done, 3 * n + j + 1)
                    act.activation(g0[u][:, 4 * j + 1:4 * j + 5, :, 1:RH + 1].rearrange("p y i x -> p (y i) x"),
                                   ps[0:LANES, 2 * j:2 * j + 2, 0:CH], ACT.Gelu,
                                   bias=sb0[:, 1:2], scale=sb0[:, 0:1]).then_inc(gelu0_done, 1)

            def high_of_input(i, k):
                n = SPS * i + k
                act.wait_ge(xin_loaded, 48 * (n + 1))
                if not (isinstance(n, int) and n == 0):
                    act.wait_ge(conv0_done, 3 * n)
                act.copy(xh[:], xin[:]).then_inc(xh_done, 1)

            def gelu_dw(i, k):
                n = SPS * i + k
                act.wait_ge(dw_done, n + 1)
                def gelu_rows(j):
                    y = slice(4 * j, 4 * j + 4)
                    act.activation(acc[k % 2][:, y], acc[k % 2][:, y], ACT.Gelu,
                                   bias=sbdw[:, 1, k % NGRP:k % NGRP + 1]).then_inc(gelud_done, 1)

                def high_rows(j):
                    y = slice(4 * j, 4 * j + 4)
                    act.wait_ge(gelud_done, 3 * n + j + 1)
                    act.wait_ge(pw_done, 3 * (n - 1) + j + 1 + 6)
                    act.copy(dh[:, y], acc[k % 2][:, y]).then_inc(dh_done, 1)

                gelu_rows(0)
                gelu_rows(1)
                high_rows(0)
                gelu_rows(2)
                high_rows(1)
                high_rows(2)

            def gelu3(i, k):
                n = SPS * i + k
                act.wait_ge(p_loaded[1 - k % 2], all_patches(i, k, 1 - k % 2))
                for j in range(3):
                    act.wait_ge(pw_done, 3 * n + j + 1 + 6)
                    src = ps[0:LANES, 2 * j:2 * j + 2, 0:CH].rearrange("p c (l x) -> p c l x", x=RH)
                    dst = g3[:].rearrange("p (y x) (a b i) -> p a b y i x", y=4, a=3, b=3)
                    for b in range(3):
                        last = act.activation(dst[:, j, b], src[:, :, :, 4 * b:4 * b + 4], ACT.Gelu,
                                              bias=bpw[:, k % NGRP:k % NGRP + 1])
                    last.then_inc(gelu3_done, 1)

            hv = h1[0:64, :].rearrange("p (y x i) -> p y x i", y=21, x=21)

            def gelu1(i, k):
                g, b = k % NGRP, k // NGRP
                if g == 0:
                    act.wait_ge(conv2_blocks, 2 * i + b + 1)
                for c in range(CPS[g]):
                    act.wait_ge(c12_done, conv1_chunk(i, k, c) + 1)
                    lanes = slice(64 * (c // 2), 64 * (c // 2) + 64)
                    for m in range(min(3, GRPR[g] - 3 * c)):
                        gy, gx = divmod(RG * g + 3 * c + m, G7)
                        last = act.activation(hv[:, 3 * gy:3 * gy + 3, 3 * gx:3 * gx + 3, :].rearrange("p y x i -> p y (x i)"),
                                              ps[lanes, 6 + c % 2, m * 9 * BI:(m + 1) * 9 * BI].rearrange("p (y w) -> p y w", y=3),
                                              ACT.Gelu, bias=sb1[lanes, 1:2], scale=sb1[lanes, 0:1])
                    last.then_inc(c12_out, 1)
                if g == NGRP - 1:
                    act.wait_ge(c12_out, conv1_chunk(i, k, c) + 1 + 1)
                    act.sem_inc(h1_done, 1)

            def gelu2(i, b):
                for part in range(2):
                    act.wait_ge(c12_done, conv2_chunk(i, b, part) + 1)
                    act.wait_ge(cleared, 1)
                    act.activation(h2[:, 25 * part:25 * part + 25, bass.ds(i * SBI + b * BI, BI)],
                                   ps[:, 6 + part, 0:25 * BI].rearrange("p (y i) -> p y i", i=BI), ACT.Gelu,
                                   bias=sb2[:, 1:2], scale=sb2[:, 0:1]).then_inc(c12_out, 1)

            def step(i, k):
                static = isinstance(i, int)
                gelu_dw(i, k)
                more = not (static and SPS * i + k + 2 >= SPS * NSB)
                if more:
                    high_of_input(i, k + 2)
                if not (static and SPS * i + k < 2):
                    gelu1(i, k - 2)
                gelu3(i, k)
                if more:
                    gelu0(i, k + 2, False)
                if k % NGRP == 1 and k > NGRP:
                    gelu2(i, k // NGRP - 1)

            for k in range(2):
                high_of_input(0, k)
                gelu0(0, k, True)
            act.wait_ge(w_loaded, ALL_LOADED)
            for k in range(2):
                step(0, k)
            with act.Fori(0, NSB - 1) as i:
                for k in range(2, SPS + 2):
                    step(i, k)
            for k in range(2, SPS):
                step(NSB - 1, k)
            gelu1(NSB - 1, SPS - 2)
            gelu1(NSB - 1, SPS - 1)
            gelu2(NSB - 1, 1)

            def std(n):
                act.wait_ge(var_ready, n + 1)
                act.activation(rstd[:], mv[:, :, 1], ACT.Sqrt, bias=epsv).then_inc(std_ready, 1)

            epsv = stats[:, 0, 0:1]

            def turn_tokens(a):
                for n, (h, s, m) in enumerate(quads):
                    act.wait_ge(tr_mm, NQ * a + n + 1)
                    src = ps[0:96, 4 + n % 4, 0:m * 128]
                    dst = NT[0:96, h, s:s + m, :]
                    if a == 0:
                        act.activation(dst, src, ACT.Identity).then_inc(tr_out, 1)
                    else:
                        act.activation(dst, src, ACT.Identity, scale=lnwb[:, 2 * a - 2, h:h + 1],
                                       bias=lnwb[:, 2 * a - 1, h:h + 1]).then_inc(tr_out, 1)

            def attention(a):
                def qk_copy(t, u, m):
                    act.wait_ge(qk_mm, 8 * NITS + 4 * t + m + 1)
                    act.wait_ge(s_mm, 4 * (t + NITS * a) - 4 + 2)
                    act.activation(qkT[u][:, m], ps[0:96, m % 2, 0:NTOK * BI], ACT.Identity).then_inc(qk_out, 1)
                    act.wait_ge(qk_out, 8 * NITS + 4 * t + m + 1 + 2)
                    act.sem_inc(qk_ready, 1)

                def exps(t, sub):
                    n = 4 * (t + NITS * a) + sub
                    act.wait_ge(s_shift, n + 1)
                    act.activation(P[sub][:], P[sub][:], ACT.Exp, scale=HD ** -0.5).then_inc(s_exp, 1)

                def values_out():
                    for n, (s, m) in enumerate(pairs):
                        act.wait_ge(val_mm, len(pairs) * a + n + 1)
                        act.activation(V[:, s:s + m, :], ps[:, 5 + n % 2, 0:m * E].rearrange("p (t e) -> p t e", e=E),
                                       ACT.Identity).then_inc(val_out, 1)

                def turn(t, u, final):
                    for sub in range(4):
                        n = 4 * (t + NITS * a) + sub
                        act.wait_ge(pt_mm, n + 1)
                        act.activation(PT[sub % 2][:], ps[0:104, 4, 0:384], ACT.Identity).then_inc(pt_out, 1)
                        if not (final and sub >= 2):
                            exps(t + (sub + 2) // 4, (sub + 2) % 4)
                        if a == 1 and sub == 0 and not final:
                            qk_copy(t + 1, 1 - u, 3)
                        elif a == 1 and sub > 0 and not (final or static_last(t)):
                            qk_copy(t + 2, u, sub - 1)
                        act.wait_ge(o_mm, n + 1)
                        at = t * BI + 4 * sub
                        act.wait_ge(cleared, 1)
                        act.activation(ot0[:, :, bass.ds(at, 4)], ps[:, 7, 0:104].rearrange("p (j q) -> p q j", j=4),
                                       ACT.Identity)
                        act.activation(ot1[0:64, :, bass.ds(at, 4)],
                                       ps[0:64, 7, 104:208].rearrange("p (j q) -> p q j", j=4),
                                       ACT.Identity).then_inc(o_out, 1)

                act.wait_ge(tr_out, NQ * (a + 1))
                act.wait_ge(ones_set, 1)
                values_out()
                if a == 1:
                    for m in range(7):
                        qk_copy(m // 4, m // 4, m % 4)
                exps(0, 0)
                exps(0, 1)
                with act.Fori(0, NITS // 2 - 1) as i:
                    for u in range(2):
                        turn(2 * i + u, u, False)
                turn(NITS - 2, 0, False)
                turn(NITS - 1, 1, True)

            std(0)
            turn_tokens(0)
            attention(0)
            std(1)
            std(2)
            turn_tokens(1)
            attention(1)
            std(3)
            turn_tokens(2)
            act.wait_ge(e_ready, 1)
            act.activation(gg[:, 1, :], gg[:, 0, :], ACT.Exp).then_inc(e_exp, 1)

            def w1_high(i, v):
                t, u = 4 * i + v, v % 2
                e = act.value_load(at(tile_e, t), min_val=0, max_val=NEXP - 1)
                if v >= 2:
                    act.wait_ge(up_mm, 3 * t - 3)
                    act.wait_ge(cleared, 1)
                for h in range(2):
                    act.copy(w1h[u][:, h, :], W1[:, bass.ds(e, 1), h * HID:(h + 1) * HID].rearrange("p a n -> p (a n)")
                             ).then_inc(w1h_done, 1)
                if v >= 2:
                    act.wait_ge(gelu_done, 3 * t)
                    act.wait_ge(cleared, 1)
                act.copy(b1e[u][:], b1t[:, bass.ds(e * HC, HC)]).then_inc(b1_here, 1)

            def out_of_turn(i, v):
                t, u = 4 * i + v, v % 2
                act.wait_ge(xT_mm, t + 1)
                if v >= 2:
                    act.wait_ge(x_done, t - 1)
                for h in range(2):
                    last = act.activation(xf[u][:, h, :], ps[0:96, 5, h * ET:(h + 1) * ET], ACT.Identity,
                                          scale=lnwb[:, 2, h:h + 1], bias=lnwb[:, 3, h:h + 1])
                last.then_inc(x_scaled, 1)
                act.wait_ge(x_scaled, t + 1)
                act.copy(xfh[u][:], xf[u][:]).then_inc(xf_done, 1)

            def gelu(i, v, p):
                t, u = 4 * i + v, v % 2
                if p == 0:
                    act.wait_ge(b1_here, t + 1)
                act.wait_ge(up_mm, 3 * t + p + 1)
                act.wait_ge(h_done, 3 * t + p + 1)
                for c in range(2):
                    last = act.activation(hf[:, p, c * ET:(c + 1) * ET], ps[:, p, c * ET:(c + 1) * ET], ACT.Gelu,
                                          bias=b1e[u][:, 2 * p + c:2 * p + c + 1])
                last.then_inc(gelu_done, 1)

            act.wait_ge(w_resident, 32 * NEXP)
            act.wait_ge(sorted_x_in, 16 * TOPK * NTOK)
            act.wait_ge(filled, 16 * NEXP)
            act.wait_ge(x_added, 1)
            act.wait_ge(tiles_ready, 1)
            w1_high(0, 0)
            out_of_turn(0, 0)

            def act_step(i, v):
                if inside(i, v + 1):
                    w1_high(i, v + 1)
                if inside(i, v):
                    gelu(i, v, 0)
                if inside(i, v + 1):
                    out_of_turn(i, v + 1)
                if inside(i, v):
                    gelu(i, v, 1)
                    gelu(i, v, 2)

            run_tiles(act, act_step)

        @block.vector
        def _(dve):
            links = [0]

            def link(ins):
                links[0] += 1
                ins.then_inc(chain, 1)
                dve.wait_ge(chain, links[0])

            dve.wait_ge(first_loaded, 16 * NFIRST)
            for dx in range(3):
                dve.tensor_tensor(w0[:, dx, :].rearrange("p (r c) -> p r c", r=RG),
                                  bc(w0rep[:, dx, :], 1, RG), bc(regmask[:, 0:RG], 2, C1), ALU.mult)
            link(dve.tensor_tensor(pwrep[:], pwrep[:], spwrep[:], ALU.mult))
            for g in range(NGRP):
                last = dve.tensor_tensor(wpw[:, g, :].rearrange("p (r c) -> p r c", r=RG),
                                         bc(pwrep[:, g, :], 1, RG), bc(regmask[:, RG:2 * RG], 2, C1), ALU.mult)
            link(last)
            for w, hi, lo in ((w0, w0h, w0l), (wpw, wpwh, wpwl)):
                link(dve.tensor_copy(hi[:], w[:]))
                dve.tensor_tensor(lo[:], w[:], hi[:].bitcast(F32), ALU.subtract)
            dve.tensor_tensor(wdw[:], wdw[:], bc(sbdw[:, 0, :], 2, 9), ALU.mult).then_inc(w_built, 1)
            dve.wait_ge(w_loaded, ALL_LOADED)
            dve.tensor_copy(upper[:], upper_f[:])
            dve.memset(ones[:], 1.0)
            for dy in range(2):
                dve.tensor_tensor(w3[:, dy, :], w3[:, dy, :], s3row[:], ALU.mult)
            for h in range(2):
                src = wa[0][:, h, 0:2 * E].rearrange("p (n e) -> p n e", e=2)
                dst = wrot[:, h, :].rearrange("p (n e) -> p n e", e=2)
                dve.tensor_scalar(dst[:, :, 0], src[:, :, 1], -1.0, None, ALU.mult)
                last = dve.tensor_copy(dst[:, :, 1], src[:, :, 0])
            last.then_inc(w_built, 1)
            dve.wait_ge(w_built, 2)
            dve.sem_inc(pw_done, 6)
            dve.sem_inc(qk_out, 2)
            dve.sem_inc(s_out, 4)
            dve.sem_inc(s_mm, 2)
            dve.sem_inc(xf_done, 1)
            dve.sem_inc(gelu_done, 3)
            dve.sem_inc(h_done, 3)
            dve.sem_inc(y_ready, 2)
            dve.sem_inc(y_landed, 2)

            def depthwise(i, k):
                n = SPS * i + k
                u, g = k % 2, k % NGRP
                dve.wait_ge(gelu0_done, 3 * (n + 1))
                dve.wait_ge(dl_done, 3 * (n - 1) + 6)
                o = acc[u][:].rearrange("p y (i x) -> p (y i) x", x=RH)
                for t in range(9):
                    dy, dx = divmod(t, 3)
                    src = g0[u][:, dy:dy + RH, :, dx:dx + RH].rearrange("p y i x -> p (y i) x")
                    if t == 0:
                        ins = dve.tensor_scalar(o, src, wdw[:, g, 0:1], None, ALU.mult)
                    else:
                        dve.wait_ge(dwtap, 8 * n + t)
                        ins = dve.scalar_tensor_tensor(o, src, wdw[:, g, t:t + 1], o, ALU.mult, ALU.add)
                    ins.then_inc(dw_done if t == 8 else dwtap, 1)

            with dve.Fori(0, NSB) as i:
                for k in range(SPS):
                    depthwise(i, k)

            def stats_of(src, tokens):
                for s in tokens:
                    last = dve.bn_stats(stats[:, s, :], src[:, s, :])
                return last

            for n, (s, m) in enumerate(pairs):
                dve.wait_ge(conv3_mm, n + 1)
                a = max(s, 1)
                dve.tensor_tensor(H[:, a:s + m, :], ps[:, n % 4, (a - s) * E:m * E].rearrange("p (t e) -> p t e", e=E),
                                  bc(b3row[:], 1, s + m - a), ALU.add).then_inc(h_ready, 1)
                if n:
                    dve.wait_ge(h_ready, n)
                    stats_of(H, range(max(s - 2, 1), s))
            dve.wait_ge(h_ready, len(pairs))
            stats_of(H, range(s, s + m))
            dve.wait_ge(cls_loaded, 16)
            link(stats_of(H, range(1)))
            link(dve.memset(ps[:, 2:4, :], 0.0))
            dve.sem_inc(ps_cleared, 1)

            def layernorm(n, src, dst):
                for s in range(NTOK):
                    last = dve.bn_aggr(mv[:, s, :], stats[:, s, :])
                link(last)
                link(dve.memset(stats[:, 0, 0:1], EPS))
                dve.sem_inc(var_ready, 1)
                dve.wait_ge(std_ready, n + 1)
                link(dve.reciprocal(rstd[:], rstd[:]))
                for s in range(NTOK):
                    dve.tensor_scalar(dst[:, s, :], src[:, s, :], mv[:, s, 0:1], rstd[:, s:s + 1],
                                      ALU.subtract, ALU.mult).then_inc(ln_done, 1)
                dve.wait_ge(ln_done, NTOK * (n + 1))

            def attention(a):
                def rotate(t, u, m):
                    for rot in range(2):
                        dve.wait_ge(qk_mm, 8 * t + 2 * m + rot + 1)
                        dve.tensor_tensor(rope[m % 2][:, rot], ps[0:96, rot, 0:NTOK * BI].rearrange("p (i s) -> p i s", i=BI),
                                          bc((sin if rot else cos)[:], 1, BI), ALU.mult).then_inc(qk_out, 1)
                    dve.wait_ge(qk_out, 8 * t + 2 * m + 2 + 2)
                    dve.tensor_tensor(qkT[u][:, m], rope[m % 2][:, 0], rope[m % 2][:, 1], ALU.add
                                      ).then_inc(qk_ready, 1)

                def softmax(t, sub):
                    n = 4 * (t + NITS * a) + sub
                    Pv = P[sub]
                    S = ps[:, SBANK[sub], 0:HEADS * NTOK].rearrange("p (h k) -> p h k", k=NTOK)
                    base = 3 * n
                    dve.wait_ge(s_mm, n + 1 + 2)
                    if a == 0:
                        dve.tensor_tensor(Pv[:], S, bc(causal[:], 1, HEADS), ALU.add).then_inc(s_out, 1)
                    else:
                        dve.tensor_copy(Pv[:], S).then_inc(s_out, 1)
                    dve.wait_ge(s_out, n + 1 + 4)
                    dve.tensor_reduce(smax[:], Pv[:], AX_X, ALU.max).then_inc(sm, 1)
                    dve.wait_ge(sm, base + 1)
                    dve.tensor_tensor(Pv[:], Pv[:], bc(smax[:], 2, NTOK), ALU.subtract).then_inc(s_shift, 1)

                def normalise(t, sub):
                    n = 4 * (t + NITS * a) + sub
                    Pv = P[sub]
                    dve.wait_ge(s_exp, n + 1)
                    dve.tensor_reduce(ssum[:], Pv[:], AX_X, ALU.add).then_inc(sm, 1)
                    dve.wait_ge(sm, 3 * n + 2)
                    dve.reciprocal(srec[:], ssum[:]).then_inc(sm, 1)
                    dve.wait_ge(sm, 3 * n + 3)
                    dve.tensor_tensor(Pv[:], Pv[:], bc(srec[:], 2, NTOK), ALU.mult).then_inc(p_ready, 1)

                def values(i, u, sub):
                    if sub == 0:
                        dve.wait_ge(vrep_loaded[u], 64 * (i + NITS // 2 * a) + 64)
                    dve.tensor_tensor(vbd[sub % 2][:], vrep[u][:, 4 * sub:4 * sub + 4, :], bc(vmask[:], 1, 4), ALU.mult
                                      ).then_inc(v_out, 1)

                def turn(i, u, final):
                    t = 2 * i + u
                    for sub in range(4):
                        if not (final and sub >= 2):
                            softmax(t + (sub + 2) // 4, (sub + 2) % 4)
                        elif sub == 2:
                            dve.wait_ge(o_mm, 4 * (t + NITS * a) + 2)
                        if sub < 3:
                            values(i, u, sub + 1)
                        elif not final:
                            values(i + u, 1 - u, 0)
                        if not (final and sub >= 2):
                            normalise(t + (sub + 2) // 4, (sub + 2) % 4)
                        if a == 0 and sub == 0 and not final:
                            rotate(t + 1, 1 - u, 3)
                        elif a == 0 and sub > 0 and not (final or static_last(t)):
                            rotate(t + 2, u, sub - 1)

                if a == 0:
                    for m in range(7):
                        rotate(m // 4, m // 4, m % 4)
                for sub in range(2):
                    softmax(0, sub)
                    normalise(0, sub)
                values(0, 0, 0)
                with dve.Fori(0, NITS // 2 - 1) as i:
                    for u in range(2):
                        turn(i, u, False)
                turn(NITS // 2 - 1, 0, False)
                turn(NITS // 2 - 1, 1, True)
                for n, (s, m) in enumerate(pairs):
                    dve.wait_ge(proj_mm, len(pairs) * a + n + 1)
                    R = (H, X)[a]
                    dve.tensor_tensor(R[:, s:s + m, :], R[:, s:s + m, :],
                                      ps[:, n % 2, 0:m * E].rearrange("p (t e) -> p t e", e=E), ALU.add
                                      ).then_inc(proj_out, 1)
                    if n:
                        dve.wait_ge(proj_out, len(pairs) * a + n)
                        stats_of(R, range(s - 2, s))
                dve.wait_ge(proj_out, len(pairs) * (a + 1))
                link(stats_of(R, range(s, s + m)))

            layernorm(0, H, N)
            attention(0)
            layernorm(1, H, X)
            link(stats_of(X, range(NTOK)))
            layernorm(2, X, N)
            attention(1)
            layernorm(3, X, N)

            dve.memset(filler[:], 0.0)
            link(dve.memset(chosen[:], 0.0))
            dve.tensor_copy(filler.bitcast(I32)[:, :, E:E + 1], route[:, R_FILL:R_FILL + 2].unsqueeze(2))
            dve.tensor_scalar(id2[:], route[:, R_ID:R_ID + NTOK], 1.0, None, ALU.add)
            link(dve.tensor_copy(XS.bitcast(I32)[:, :, E:E + 1], route[:, R_ID:R_ID + NTOK].unsqueeze(2)))
            dve.sem_inc(ids_ready, 1)

            def table(at, n):
                return route[:, at:at + n]

            for k, (s0, m) in enumerate(PARTS):
                dve.wait_ge(lg_mm, k + 1)
                part = slice(s0, s0 + m)
                link(dve.tensor_copy(logits[:, part], ps[:, k, s0 * NEXP:(s0 + m) * NEXP
                                                         ].rearrange("p (s e) -> p s e", e=NEXP)))
                for s in range(s0, s0 + m):
                    last = dve.max(top[:, s, :], logits[:, s, :])
                link(last)
                for s in range(s0, s0 + m):
                    last = dve.max_index(topi[:, s, :], top[:, s, :], logits[:, s, :])
                link(last)
                link(dve.tensor_copy(topf[:, part], topi[:, part, 0:2]))
                for j in range(TOPK):
                    last = dve.tensor_tensor(oneh[j][:, part], bc(iota8[:], 1, m), bc(topf[:, part, j], 2, NEXP),
                                             ALU.is_equal)
                link(last)
                link(dve.tensor_tensor(chosen[:, part, :], oneh[0][:, part], oneh[1][:, part], ALU.add))
                dve.sem_inc(chosen_ready, 1)
                dve.wait_ge(rank_mm, k + 1)
                link(dve.tensor_tensor(rank[:, s0:s0 + m + k, :],
                                       ps[:, 2 + k, 0:(m + k) * NEXP].rearrange("p (t e) -> p t e", e=NEXP),
                                       bc(table(R_BASE, NEXP), 1, m + k), ALU.add))
                for j in range(TOPK):
                    link(dve.tensor_tensor(oneh[j][:, part], oneh[j][:, part], rank[:, part, :], ALU.mult))
                    link(dve.tensor_reduce(posf[:, j, part], oneh[j][:, part], AX_X, ALU.add))
                    link(dve.tensor_copy(pos[:, j, part], posf[:, j, part]))
                    dve.sem_inc(pos_ready, 1)
            link(dve.tensor_tensor(gg[:, 0, :], top[:, :, 1], top[:, :, 0], ALU.subtract))
            dve.sem_inc(e_ready, 1)
            link(dve.tensor_copy(fill_r[:], rank[:, NTOK, :]))
            link(dve.tensor_tensor(ntile[:], rank[:, NTOK, :], table(R_BASE, NEXP), ALU.subtract))
            link(dve.tensor_tensor(full[:], bc(ntile[:], 2, MAXT), bc(table(R_STEP, MAXT), 1, NEXP), ALU.is_gt))
            link(dve.tensor_reduce(ntile[:], full[:], AX_X, ALU.add))
            link(dve.tensor_tensor(square[:], bc(ntile[:], 1, NEXP),
                                   table(R_TRI, NEXP * NEXP).rearrange("p (e f) -> p e f", e=NEXP), ALU.mult))
            link(dve.tensor_reduce(tend[:], square[:], AX_X, ALU.add))
            link(dve.tensor_scalar(lastt[:], tend[:, NEXP - 1:NEXP], -1.0, None, ALU.add))
            link(dve.tensor_scalar(tilek[:], table(R_TILE, TILES), lastt[:, 0:1], None, ALU.min))
            link(dve.tensor_tensor(past[:], bc(tilek[:], 2, NEXP), bc(tend[:], 1, TILES), ALU.is_ge))
            link(dve.tensor_reduce(tilef[:, 0, :], past[:], AX_X, ALU.add))
            link(dve.tensor_copy(tile_e[:], tilef[:, 0, :]))
            link(dve.tensor_tensor(past[:], past[:], bc(ntile[:], 1, TILES), ALU.mult))
            link(dve.tensor_reduce(tilef[:, 1, :], past[:], AX_X, ALU.add))
            link(dve.tensor_tensor(tilek[:], tilek[:], tilef[:, 1, :], ALU.subtract))
            link(dve.tensor_scalar(tilek[:], tilek[:], float(ET), None, ALU.mult))
            link(dve.scalar_tensor_tensor(tilek[:], tilef[:, 0, :], float(ECAP), tilek[:], ALU.mult, ALU.add))
            link(dve.tensor_copy(tile_r[:], tilek[:]))
            dve.sem_inc(tiles_ready, 1)
            dve.wait_ge(e_exp, 1)
            link(dve.tensor_scalar(gg[:, 0, :], gg[:, 1, :], 1.0, None, ALU.add))
            link(dve.reciprocal(g12[:, 0, :], gg[:, 0, :]))
            link(dve.tensor_tensor(g12[:, 1, :], gg[:, 1, :], g12[:, 0, :], ALU.mult))
            link(dve.tensor_tensor(H[:], H[:], X[:], ALU.add))
            dve.sem_inc(x_added, 1)

            def y_copy(i, v):
                t, u = 4 * i + v, v % 2
                dve.wait_ge(down_mm, t + 1)
                dve.wait_ge(b2_loaded[u], 16 * (2 * i + v // 2 + 1))
                dve.wait_ge(y_landed, t + 2)
                banks = ps[:, DBANK[u]:DBANK[u] + 2, :]
                dve.tensor_tensor(yt[u][:], banks[:, :, 0:E], bc(b2e[u][:], 1, 2), ALU.add).then_inc(y_steps, 1)
                dve.wait_ge(y_steps, t + 1)
                dve.tensor_tensor(yt[u][:], yt[u][:], banks[:, :, E:2 * E], ALU.add).then_inc(y_ready, 1)

            def split_w2(i, v):
                t, u = 4 * i + v, v % 2
                e = dve.value_load(at(tile_e, t), min_val=0, max_val=NEXP - 1)
                src = W2[:, bass.ds(e, 1), :].rearrange("p a (c n) -> p (a c) n", c=HC)
                if v >= 2 or not isinstance(i, int):
                    dve.wait_ge(down_mm, t - 1)
                dve.tensor_copy(w2s[u][:, :, 0, :], src).then_inc(w2_steps, 1)
                dve.wait_ge(w2_steps, t + 1)
                dve.tensor_tensor(w2s[u][:, :, 1, :], src, w2s[u][:, :, 0, :].bitcast(F32), ALU.subtract
                                  ).then_inc(w2_done, 1)

            def split_h(i, v, p):
                t, u = 4 * i + v, v % 2
                dve.wait_ge(gelu_done, 3 * t + p + 1 + 3)
                dve.tensor_copy(hh[u][:, p], hf[:, p]).then_inc(h_steps, 1)
                dve.wait_ge(h_steps, 3 * t + p + 1)
                dve.tensor_tensor(hl[u][:, p], hf[:, p], hh[u][:, p].bitcast(F32), ALU.subtract).then_inc(h_done, 1)

            def split_x(i, v):
                t, u = 4 * i + v, v % 2
                dve.wait_ge(xf_done, t + 1 + 1)
                if v >= 2 or not isinstance(i, int):
                    dve.wait_ge(up_mm, 3 * t - 3)
                dve.tensor_tensor(xfl[u][:], xf[u][:], xfh[u][:].bitcast(F32), ALU.subtract).then_inc(x_done, 1)

            def keep_dest(i, v):
                t, u = 4 * i + v, v % 2
                dve.wait_ge(xt_loaded[u], 16 * (2 * i + v // 2 + 1))
                if v >= 2:
                    dve.wait_ge(y_landed, t - 2 + 2)
                dve.tensor_copy(dest[v % 4][:].unsqueeze(2), xt[u].bitcast(I32)[:, :, E:E + 1]).then_inc(dest_kept, 1)

            dve.wait_ge(w_resident, 32 * NEXP)
            dve.wait_ge(sorted_x_in, 16 * TOPK * NTOK)
            dve.wait_ge(filled, 16 * NEXP)
            keep_dest(0, 0)
            split_x(0, 0)

            def dve_step(i, v):
                if started(i, v - 2):
                    y_copy(i, v - 2)
                if inside(i, v):
                    split_w2(i, v)
                    split_h(i, v, 0)
                if inside(i, v + 1):
                    keep_dest(i, v + 1)
                    split_x(i, v + 1)
                if inside(i, v):
                    split_h(i, v, 1)
                    split_h(i, v, 2)

            run_tiles(dve, dve_step)

            for c, (s, m) in enumerate(CMB):
                dve.wait_ge(y_back[c], 16)
                for j in range(TOPK):
                    for t in range(s, s + m):
                        last = dve.scalar_tensor_tensor(H[:, t, :], Y[:, t, j, :], g12[:, j, t:t + 1], H[:, t, :],
                                                        ALU.mult, ALU.add)
                    link(last)
                dve.sem_inc(combined, 1)


def shape_constants(np):
    f = np.float32
    k = {"k_ident": np.eye(128, dtype=f)}
    reg = np.zeros((LANES, 2 * RG), f)
    for p in range(90):
        reg[p, (p % 30) // 3] = 1
    for p in range(LANES):
        reg[p, RG + p // C1] = 1
    k["k_regmask"] = reg
    k["k_headmask"] = (np.arange(96)[:, None] // HD == np.arange(6)[None, :]).astype(f)
    k["k_vmask"] = (np.arange(104)[:, None] // NTOK == (np.arange(E)[None, :] % 64) // HD).astype(f)
    q = np.minimum(np.arange(128) % 32, NTOK - 1)
    k["k_causal"] = np.where(np.arange(NTOK)[None, :] <= q[:, None], 0, -1e30).astype(f)
    inv = (f(1) / np.power(f(10000), np.arange(0, HD, 2, dtype=f) / f(HD))).astype(f)
    fr = (np.arange(NTOK, dtype=f)[:, None] * inv[None, :]).astype(f)
    for name, fn in (("k_cos", np.cos), ("k_sin", np.sin)):
        k[name] = np.ascontiguousarray(np.tile(np.repeat(fn(fr), 2, axis=-1).T, (6, 1)).astype(f))
    r = np.zeros((128, R_ALL), f)
    r[:, R_BASE:R_STEP] = ECAP * np.arange(NEXP)
    r[:, R_STEP:R_TILE] = ET * np.arange(MAXT)
    r[:, R_TILE:R_TRI] = np.arange(TILES)
    r[:, R_TRI:R_ID] = np.tri(NEXP, dtype=f).ravel()
    r[:, R_ID:R_FILL] = TOPK * (NTOK * np.arange(128)[:, None] + np.arange(NTOK)[None, :])
    r[:, R_FILL:] = SLOTS + np.arange(128)[:, None] + 128 * np.arange(2)[None, :]
    k["k_route"] = r
    k["k_upper"] = np.triu(np.ones((128, 128), f), 1)
    k["k_iota"] = np.tile(np.arange(NEXP, dtype=f), (128, 1))
    return k


def by_group(np, a, *tail):
    a = a.reshape((NREG * C1,) + tail)
    a = np.concatenate([a, np.zeros((NGRP * LANES - NREG * C1,) + tail, a.dtype)])
    return np.swapaxes(a.reshape((NGRP, LANES) + tail), 0, 1)


def lay_out(np, v):
    f = np.float32
    d = {}
    p = np.zeros((NIMG, CIN, HW + 2, HW + 2), f)
    p[:, :, 1:HW + 1, 1:HW + 1] = v["x"]
    w = np.empty((NBLK, NREG, CIN, WIN, BI, WIN), f)
    for r in range(NREG):
        y, x = RH * (r // G7), RH * (r % G7)
        w[:, r] = p[:, :, y:y + WIN, x:x + WIN].reshape(NBLK, BI, CIN, WIN, WIN).transpose(0, 2, 3, 1, 4)
    d["windows"] = w.reshape(NBLK, NREG * CIN, WIN * LINE)
    t = v["L0_tok_w0"].transpose(2, 1, 3, 0)
    d["w0"] = np.repeat(t[:, None], RG, axis=1).reshape(90, 3, C1)
    d["w0"] = np.concatenate([d["w0"], np.zeros((LANES - 90, 3, C1), f)])
    d["sb0"] = np.tile(np.stack([v["L0_tok_s0"], v["L0_tok_b0"]], 1), (RG, 1))
    d["wdw"] = by_group(np, v["L0_tok_wdw"], 9)
    d["sbdw"] = np.stack([by_group(np, v["L0_tok_sdw"]), by_group(np, v["L0_tok_bdw"])], 1)
    d["bpw"] = by_group(np, v["L0_tok_bpw"])
    t = v["L0_tok_wpw"].reshape(NREG, C1, C1).transpose(0, 2, 1)
    d["wpw"] = by_group(np, t, C1)
    d["spw"] = by_group(np, np.repeat(v["L0_tok_spw"].reshape(NREG, 1, C1), C1, axis=1), C1)
    t = np.zeros((C1 * 16, 64), f)
    t[:, :C2] = v["L0_tok_w1"].transpose(1, 2, 3, 0).reshape(C1 * 16, C2)
    d["w1"] = t.reshape(2, 96, 64).transpose(1, 0, 2)
    for c in "12":
        t = np.zeros((2, 64, 2), f)
        t[:, :C2, 0], t[:, :C2, 1] = v["L0_tok_s" + c], v["L0_tok_b" + c]
        d["sb" + c] = t.reshape(128, 2)
    for name, m, mp in (("w2", C2, 64), ("w3", E, E)):
        t = np.zeros((2, 64, 2, mp), f)
        t[:, :C2, :, :m] = v["L0_tok_" + name].transpose(3, 1, 2, 0)
        d[name] = t.reshape(128, 2, mp)
    for a, (w, b) in enumerate(((v["L0_attn_W_attn"], v["L0_attn_b_attn"]),
                                (v["L0_ffn_qkv_w"].T, v["L0_ffn_qkv_b"]))):
        t = np.zeros((128, 2, 3 * E), f)
        t[:96] = w.reshape(2, 96, 3 * E).transpose(1, 0, 2)
        t[96, 1] = b
        d[f"wa{a}"] = t
    d["wp0"] = np.concatenate([v["L0_attn_W_proj"], v["L0_attn_b_proj"][None]])
    d["wp1"] = np.concatenate([v["L0_ffn_proj_w"].T, v["L0_ffn_proj_b"][None]])
    d["lnwb"] = np.stack([v["L0_ffn_" + n].reshape(2, 96).T for n in ("norm1_w", "norm1_b", "norm2_w", "norm2_b")], 1)
    d["wg"] = v["L0_ffn_w_gate"].reshape(2, 96, NEXP).transpose(1, 0, 2)
    d["b1"] = v["L0_ffn_b1"].reshape(NEXP * HC, 128).T
    d["W1"] = v["L0_ffn_W1"].reshape(NEXP, 2, 96, HID).transpose(0, 2, 1, 3).reshape(NEXP * 96, 2 * HID)
    d["W1"] = d["W1"].reshape(NEXP, 96, 2 * HID)
    d["W2"] = v["L0_ffn_W2"].reshape(NEXP, HC, 128, E).transpose(0, 2, 1, 3).reshape(NEXP, 128, HC * E)
    for n in ("cls_tok", "L0_tok_s3", "L0_tok_b3", "L0_ffn_b2"):
        d[n] = v[n]
    return d


def kernel(**inputs):
    import numpy as _np
    import concourse.bacc as _bacc
    from concourse import mybir as _mybir
    from concourse.bass_utils import run_bass_kernel_spmd as _run

    nc = _bacc.Bacc("TRN2", target_bir_lowering=False, num_devices=1)
    arrays, A = {}, {}
    every = lay_out(_np, {name: _np.asarray(a) for name, a in inputs.items()})
    every.update(shape_constants(_np))
    for name, a in every.items():
        arrays[f"in_{name}_dram"] = _np.ascontiguousarray(a)
        A[name] = nc.dram_tensor(f"in_{name}_dram", a.shape, _mybir.dt.from_np(a.dtype), kind="ExternalInput").ap()
    out = nc.dram_tensor("out_0_dram", (NIMG, NTOK, E), _mybir.dt.float32, kind="ExternalOutput").ap()
    vit_tower(nc, A, out)
    r = _run(nc, [arrays], core_ids=[0])
    return r.results[0]["out_0_dram"]
```
